# Optimizing a Trainium2 kernel written in Bass

```python
import numpy as np
import jax
import jax.numpy as jnp

def _softmax(x, axis=-1):
    return jax.nn.softmax(x, axis=axis)

def _gelu(x):
    return jax.nn.gelu(x, approximate=True)

def _silu(x):
    return jax.nn.silu(x)

def _sigmoid(x):
    return jax.nn.sigmoid(x)

def _layernorm(x, axis=-1, eps=1e-05):
    m = jnp.mean(x, axis=axis, keepdims=True)
    v = jnp.var(x, axis=axis, keepdims=True)
    return (x - m) / jnp.sqrt(v + eps)

def _scatter_add(tgt, idx, src, axis=0):
    return tgt.at[idx].add(src)

def _segment_sum(src, seg, n):
    return jax.ops.segment_sum(src, seg, n)
kernel_name = 'mk_early_fusion_embed_d4_tok_img256_r4_bb0d10'

def setup_inputs(seed: int=0):
    np.random.seed(seed)
    _w = jnp.asarray

    def _rec_inputs():
        import jax
        import jax.numpy as jnp
        _rk = jax.random.key(seed)
        x = -7.10856e-05 + 0.999911 * jax.random.normal(jax.random.fold_in(_rk, 1), (128, 1, 224, 224), jnp.float32)
        x_txt = jax.random.randint(jax.random.fold_in(_rk, 51), (128, 128), 0, 12500, jnp.int32)
        return (x, x_txt)
    x, x_txt = _rec_inputs()

    def _L0_tok_setup():
        import jax, jax.numpy as jnp
        import numpy as np
        INV_SQRT2 = 0.7071067811865476

        def haar_dwt2(x):
            lo = (x[..., ::2] + x[..., 1::2]) * INV_SQRT2
            hi = (x[..., ::2] - x[..., 1::2]) * INV_SQRT2
            cA = (lo[..., ::2, :] + lo[..., 1::2, :]) * INV_SQRT2
            cH = (lo[..., ::2, :] - lo[..., 1::2, :]) * INV_SQRT2
            cV = (hi[..., ::2, :] + hi[..., 1::2, :]) * INV_SQRT2
            cD = (hi[..., ::2, :] - hi[..., 1::2, :]) * INV_SQRT2
            return (cA, (cH, cV, cD))

        def wavedec2_maps(x, levels):
            a = x
            details = []
            for _ in range(levels):
                a, d = haar_dwt2(a)
                details.append(d)
            maps = [a]
            for d in reversed(details):
                maps.extend(d)
            return maps
        key = jax.random.key(seed)
        k1, k2 = jax.random.split(key)
        B, H, W_img = (64, 256, 256)
        x = jax.random.normal(k1, (B, 1, H, W_img), dtype=jnp.float32)
        n_maps = 1 + 3 * 2
        W = jax.random.normal(k2, (n_maps, 64), dtype=jnp.float32) * (1.0 / np.sqrt(n_maps))
        b = jnp.zeros((64,), dtype=jnp.float32)
        return {'x': x, 'W': W, 'b': b}
    _L0_tok_all = _L0_tok_setup()
    _L0_tok_in = {k: v for k, v in _L0_tok_all.items() if k in ('W', 'b')}
    del _L0_tok_all

    def _L0_txt_setup():
        import jax, jax.numpy as jnp
        import numpy as np
        INP_SIZE = 12500
        HIDDEN = 64
        KERNEL = 5
        WEIGHTS = jnp.array([0.1, 0.2, 0.4, 0.2, 0.1], dtype=jnp.float32)
        key = jax.random.key(seed)
        k1, k2 = jax.random.split(key)
        x = jax.random.randint(k1, (8, 1024), 0, INP_SIZE, dtype=jnp.int32)
        emb = jax.random.normal(k2, (INP_SIZE, HIDDEN), dtype=jnp.float32)
        return {'x': x, 'emb': emb}
    _L0_txt_all = _L0_txt_setup()
    _L0_txt_in = {k: v for k, v in _L0_txt_all.items() if k in ('emb',)}
    del _L0_txt_all

    def _L0_attn_setup():
        import jax, jax.numpy as jnp
        import numpy as np
        B, N, D = (8, 512, 64)
        key = jax.random.key(seed)
        k1, k2, k3, k4 = jax.random.split(key, 4)
        s = D ** (-0.5)
        return {'x': jax.random.normal(k1, (B, N, D), dtype=jnp.float32), 'Wq': jax.random.normal(k2, (D, D), dtype=jnp.float32) * s, 'Wk': jax.random.normal(k3, (D, D), dtype=jnp.float32) * s, 'Wv': jax.random.normal(k4, (D, D), dtype=jnp.float32) * s}
    _L0_attn_all = _L0_attn_setup()
    _L0_attn_in = {k: v for k, v in _L0_attn_all.items() if k in ('Wq', 'Wk', 'Wv')}
    del _L0_attn_all

    def _L0_ffn_setup():
        import jax, jax.numpy as jnp
        import numpy as np
        B, S, H, F, E, K = (8, 1024, 64, 128, 16, 2)
        EPS = 1e-05
        key = jax.random.key(seed)
        ks = jax.random.split(key, 9)
        sc = 0.02
        return {'x': jax.random.normal(ks[0], (B, S, H), dtype=jnp.float32), 'gate_w': jax.random.normal(ks[1], (H, E), dtype=jnp.float32) * sc, 'gate_b': jnp.zeros((E,), dtype=jnp.float32), 'w1': jax.random.normal(ks[2], (E, H, F), dtype=jnp.float32) * sc, 'b1': jnp.zeros((E, F), dtype=jnp.float32), 'w2': jax.random.normal(ks[3], (E, F, H), dtype=jnp.float32) * sc, 'b2': jnp.zeros((E, H), dtype=jnp.float32), 'gamma': jnp.ones((H,), dtype=jnp.float32), 'beta': jnp.zeros((H,), dtype=jnp.float32)}
    _L0_ffn_all = _L0_ffn_setup()
    _L0_ffn_in = {k: v for k, v in _L0_ffn_all.items() if k in ('gate_w', 'gate_b', 'w1', 'b1', 'w2', 'b2', 'gamma', 'beta')}
    del _L0_ffn_all

    def _L1_attn_setup():
        import jax, jax.numpy as jnp
        import numpy as np
        HEADS = 8
        DIM = 64
        DIM_HEAD = 64
        DH = DIM_HEAD // HEADS
        SCALE = DIM_HEAD ** (-0.5)
        LN_EPS = 1e-05
        key = jax.random.key(seed)
        k1, k2, k3 = jax.random.split(key, 3)
        b, n = (8, 2048)
        x = jax.random.normal(k1, (b, n, DIM), dtype=jnp.float32)
        Wqkv = jax.random.normal(k2, (DIM, 3 * DIM_HEAD), dtype=jnp.float32) * 0.02
        Wout = jax.random.normal(k3, (DIM_HEAD, DIM), dtype=jnp.float32) * 0.02
        bout = jnp.zeros((DIM,), dtype=jnp.float32)
        gamma = jnp.ones((DIM,), dtype=jnp.float32)
        beta = jnp.zeros((DIM,), dtype=jnp.float32)
        return {'x': x, 'Wqkv': Wqkv, 'Wout': Wout, 'bout': bout, 'gamma': gamma, 'beta': beta}
    _L1_attn_all = _L1_attn_setup()
    _L1_attn_in = {k: v for k, v in _L1_attn_all.items() if k in ('Wqkv', 'Wout', 'bout', 'gamma', 'beta')}
    del _L1_attn_all

    def _L1_ffn_setup():
        import jax, jax.numpy as jnp
        import numpy as np
        B, T, IN_DIM = (64, 64, 64)
        HID, OUT_DIM = (128, 64)
        N_LAYERS, N_EXPERTS, N_SHARED = (2, 16, 1)
        key = jax.random.key(seed)
        ks = jax.random.split(key, 10)
        s = 0.02
        x = jax.random.normal(ks[0], (B, T, IN_DIM), dtype=jnp.float32)
        route_id = jax.random.randint(ks[1], (B,), 0, N_EXPERTS)
        Wi = jax.random.normal(ks[2], (HID, IN_DIM), dtype=jnp.float32) * s
        bi = jnp.zeros((HID,), dtype=jnp.float32)
        Wr = jax.random.normal(ks[3], (N_LAYERS, N_EXPERTS, HID, HID), dtype=jnp.float32) * s
        br = jax.random.normal(ks[4], (N_LAYERS, N_EXPERTS, HID), dtype=jnp.float32) * s
        Ws = jax.random.normal(ks[5], (N_LAYERS, N_SHARED, HID, HID), dtype=jnp.float32) * s
        bs = jax.random.normal(ks[6], (N_LAYERS, N_SHARED, HID), dtype=jnp.float32) * s
        Wo = jax.random.normal(ks[7], (OUT_DIM, HID), dtype=jnp.float32) * s
        bo = jnp.zeros((OUT_DIM,), dtype=jnp.float32)
        return {'x': x, 'route_id': route_id, 'Wi': Wi, 'bi': bi, 'Wr': Wr, 'br': br, 'Ws': Ws, 'bs': bs, 'Wo': Wo, 'bo': bo}
    _L1_ffn_all = _L1_ffn_setup()
    _L1_ffn_in = {k: v for k, v in _L1_ffn_all.items() if k in ('route_id', 'Wi', 'bi', 'Wr', 'br', 'Ws', 'bs', 'Wo', 'bo')}
    del _L1_ffn_all

    def _L2_attn_setup():
        import jax, jax.numpy as jnp
        import numpy as np
        D_IN = 64
        D_OUT = 64
        key = jax.random.key(seed)
        kx, kq, kk, kv = jax.random.split(key, 4)
        scale = 1.0 / np.sqrt(D_IN)
        x = jax.random.normal(kx, (4, 1024, D_IN), dtype=jnp.float32)
        Wq = jax.random.uniform(kq, (D_OUT, D_IN), dtype=jnp.float32, minval=-scale, maxval=scale)
        Wk = jax.random.uniform(kk, (D_OUT, D_IN), dtype=jnp.float32, minval=-scale, maxval=scale)
        Wv = jax.random.uniform(kv, (D_OUT, D_IN), dtype=jnp.float32, minval=-scale, maxval=scale)
        return {'x': x, 'Wq': Wq, 'Wk': Wk, 'Wv': Wv}
    _L2_attn_all = _L2_attn_setup()
    _L2_attn_in = {k: v for k, v in _L2_attn_all.items() if k in ('Wq', 'Wk', 'Wv')}
    del _L2_attn_all

    def _L2_ffn_setup():
        import jax, jax.numpy as jnp
        import numpy as np
        E, D, H, TOP_K = (6, 64, 64, 2)
        ROUTER_H = D // 2
        key = jax.random.key(seed)
        ks = jax.random.split(key, 12)
        s = 1.0 / np.sqrt(D)
        sh = 1.0 / np.sqrt(H)
        sr = 1.0 / np.sqrt(ROUTER_H)
        return {'features': jax.random.normal(ks[0], (8, 1024, D), dtype=jnp.float32), 'router_w1': jax.random.uniform(ks[1], (D, ROUTER_H), jnp.float32, -s, s), 'router_b1': jnp.zeros((ROUTER_H,), jnp.float32), 'router_w2': jax.random.uniform(ks[2], (ROUTER_H, E), jnp.float32, -sr, sr), 'router_b2': jnp.zeros((E,), jnp.float32), 'expert_w1': jax.random.uniform(ks[3], (E, D, H), jnp.float32, -s, s), 'expert_b1': jnp.zeros((E, H), jnp.float32), 'expert_w2': jax.random.uniform(ks[4], (E, H, H), jnp.float32, -sh, sh), 'expert_b2': jnp.zeros((E, H), jnp.float32), 'expert_w3': jax.random.uniform(ks[5], (E, H, D), jnp.float32, -sh, sh), 'expert_b3': jnp.zeros((E, D), jnp.float32)}
    _L2_ffn_all = _L2_ffn_setup()
    _L2_ffn_in = {k: v for k, v in _L2_ffn_all.items() if k in ('router_w1', 'router_b1', 'router_w2', 'router_b2', 'expert_w1', 'expert_b1', 'expert_w2', 'expert_b2', 'expert_w3', 'expert_b3')}
    del _L2_ffn_all

    def _L3_attn_setup():
        import jax, jax.numpy as jnp
        import numpy as np
        DIM = 64
        HEADS = 4
        HEAD_DIM = DIM // HEADS
        SCALE = HEAD_DIM ** (-0.5)
        key = jax.random.key(seed)
        ks = jax.random.split(key, 9)
        B, N, C = (2, 1024, DIM)
        x = jax.random.normal(ks[0], (B, N, C), dtype=jnp.float32)
        lim = np.sqrt(6.0 / (C + C)).astype(np.float32)

        def w(k):
            return jax.random.uniform(k, (C, C), dtype=jnp.float32, minval=-lim, maxval=lim)
        return {'x': x, 'Wq': w(ks[1]), 'bq': jnp.zeros((C,), jnp.float32), 'Wk': w(ks[2]), 'bk': jnp.zeros((C,), jnp.float32), 'Wv': w(ks[3]), 'bv': jnp.zeros((C,), jnp.float32), 'Wo': w(ks[4]), 'bo': jnp.zeros((C,), jnp.float32)}
    _L3_attn_all = _L3_attn_setup()
    _L3_attn_in = {k: v for k, v in _L3_attn_all.items() if k in ('Wq', 'bq', 'Wk', 'bk', 'Wv', 'bv', 'Wo', 'bo')}
    del _L3_attn_all

    def _L3_ffn_setup():
        import jax, jax.numpy as jnp
        import numpy as np
        B, K, D = (128, 16, 64)
        E = 32
        H = int(D * 0.25)
        key = jax.random.key(seed)
        ks = jax.random.split(key, 7)
        d_rs = D ** (-0.5)
        h_rs = H ** (-0.5)
        x = jax.random.normal(ks[0], (B, K, D), dtype=jnp.float32)
        router_w = jax.random.uniform(ks[1], (E, D), jnp.float32, -d_rs, d_rs)
        router_b = jax.random.uniform(ks[2], (E,), jnp.float32, -d_rs, d_rs)
        W1 = jax.random.uniform(ks[3], (E, D, H), jnp.float32, -h_rs, h_rs)
        b1 = jax.random.uniform(ks[4], (E, H), jnp.float32, -h_rs, h_rs)
        W2 = jax.random.uniform(ks[5], (E, H, D), jnp.float32, -d_rs, d_rs)
        b2 = jax.random.uniform(ks[6], (E, D), jnp.float32, -d_rs, d_rs)
        return {'x': x, 'router_w': router_w, 'router_b': router_b, 'W1': W1, 'b1': b1, 'W2': W2, 'b2': b2}
    _L3_ffn_all = _L3_ffn_setup()
    _L3_ffn_in = {k: v for k, v in _L3_ffn_all.items() if k in ('router_w', 'router_b', 'W1', 'b1', 'W2', 'b2')}
    del _L3_ffn_all
    return {'x': x, 'x_txt': x_txt, 'L0_tok_W': _L0_tok_in['W'], 'L0_tok_b': _L0_tok_in['b'], 'L0_txt_emb': _L0_txt_in['emb'], 'L0_attn_Wq': _L0_attn_in['Wq'], 'L0_attn_Wk': _L0_attn_in['Wk'], 'L0_attn_Wv': _L0_attn_in['Wv'], 'L0_ffn_gate_w': _L0_ffn_in['gate_w'], 'L0_ffn_gate_b': _L0_ffn_in['gate_b'], 'L0_ffn_w1': _L0_ffn_in['w1'], 'L0_ffn_b1': _L0_ffn_in['b1'], 'L0_ffn_w2': _L0_ffn_in['w2'], 'L0_ffn_b2': _L0_ffn_in['b2'], 'L0_ffn_gamma': _L0_ffn_in['gamma'], 'L0_ffn_beta': _L0_ffn_in['beta'], 'L1_attn_Wqkv': _L1_attn_in['Wqkv'], 'L1_attn_Wout': _L1_attn_in['Wout'], 'L1_attn_bout': _L1_attn_in['bout'], 'L1_attn_gamma': _L1_attn_in['gamma'], 'L1_attn_beta': _L1_attn_in['beta'], 'L1_ffn_route_id': _L1_ffn_in['route_id'], 'L1_ffn_Wi': _L1_ffn_in['Wi'], 'L1_ffn_bi': _L1_ffn_in['bi'], 'L1_ffn_Wr': _L1_ffn_in['Wr'], 'L1_ffn_br': _L1_ffn_in['br'], 'L1_ffn_Ws': _L1_ffn_in['Ws'], 'L1_ffn_bs': _L1_ffn_in['bs'], 'L1_ffn_Wo': _L1_ffn_in['Wo'], 'L1_ffn_bo': _L1_ffn_in['bo'], 'L2_attn_Wq': _L2_attn_in['Wq'], 'L2_attn_Wk': _L2_attn_in['Wk'], 'L2_attn_Wv': _L2_attn_in['Wv'], 'L2_ffn_router_w1': _L2_ffn_in['router_w1'], 'L2_ffn_router_b1': _L2_ffn_in['router_b1'], 'L2_ffn_router_w2': _L2_ffn_in['router_w2'], 'L2_ffn_router_b2': _L2_ffn_in['router_b2'], 'L2_ffn_expert_w1': _L2_ffn_in['expert_w1'], 'L2_ffn_expert_b1': _L2_ffn_in['expert_b1'], 'L2_ffn_expert_w2': _L2_ffn_in['expert_w2'], 'L2_ffn_expert_b2': _L2_ffn_in['expert_b2'], 'L2_ffn_expert_w3': _L2_ffn_in['expert_w3'], 'L2_ffn_expert_b3': _L2_ffn_in['expert_b3'], 'L3_attn_Wq': _L3_attn_in['Wq'], 'L3_attn_bq': _L3_attn_in['bq'], 'L3_attn_Wk': _L3_attn_in['Wk'], 'L3_attn_bk': _L3_attn_in['bk'], 'L3_attn_Wv': _L3_attn_in['Wv'], 'L3_attn_bv': _L3_attn_in['bv'], 'L3_attn_Wo': _L3_attn_in['Wo'], 'L3_attn_bo': _L3_attn_in['bo'], 'L3_ffn_router_w': _L3_ffn_in['router_w'], 'L3_ffn_router_b': _L3_ffn_in['router_b'], 'L3_ffn_W1': _L3_ffn_in['W1'], 'L3_ffn_b1': _L3_ffn_in['b1'], 'L3_ffn_W2': _L3_ffn_in['W2'], 'L3_ffn_b2': _L3_ffn_in['b2']}

def reference(x, x_txt, L0_tok_W, L0_tok_b, L0_txt_emb, L0_attn_Wq, L0_attn_Wk, L0_attn_Wv, L0_ffn_gate_w, L0_ffn_gate_b, L0_ffn_w1, L0_ffn_b1, L0_ffn_w2, L0_ffn_b2, L0_ffn_gamma, L0_ffn_beta, L1_attn_Wqkv, L1_attn_Wout, L1_attn_bout, L1_attn_gamma, L1_attn_beta, L1_ffn_route_id, L1_ffn_Wi, L1_ffn_bi, L1_ffn_Wr, L1_ffn_br, L1_ffn_Ws, L1_ffn_bs, L1_ffn_Wo, L1_ffn_bo, L2_attn_Wq, L2_attn_Wk, L2_attn_Wv, L2_ffn_router_w1, L2_ffn_router_b1, L2_ffn_router_w2, L2_ffn_router_b2, L2_ffn_expert_w1, L2_ffn_expert_b1, L2_ffn_expert_w2, L2_ffn_expert_b2, L2_ffn_expert_w3, L2_ffn_expert_b3, L3_attn_Wq, L3_attn_bq, L3_attn_Wk, L3_attn_bk, L3_attn_Wv, L3_attn_bv, L3_attn_Wo, L3_attn_bo, L3_ffn_router_w, L3_ffn_router_b, L3_ffn_W1, L3_ffn_b1, L3_ffn_W2, L3_ffn_b2):
    import jax
    import jax.numpy as jnp

    def _L0_tok_ref(x, W, b):
        import jax, jax.numpy as jnp
        import numpy as np
        INV_SQRT2 = 0.7071067811865476

        def haar_dwt2(x):
            lo = (x[..., ::2] + x[..., 1::2]) * INV_SQRT2
            hi = (x[..., ::2] - x[..., 1::2]) * INV_SQRT2
            cA = (lo[..., ::2, :] + lo[..., 1::2, :]) * INV_SQRT2
            cH = (lo[..., ::2, :] - lo[..., 1::2, :]) * INV_SQRT2
            cV = (hi[..., ::2, :] + hi[..., 1::2, :]) * INV_SQRT2
            cD = (hi[..., ::2, :] - hi[..., 1::2, :]) * INV_SQRT2
            return (cA, (cH, cV, cD))

        def wavedec2_maps(x, levels):
            a = x
            details = []
            for _ in range(levels):
                a, d = haar_dwt2(a)
                details.append(d)
            maps = [a]
            for d in reversed(details):
                maps.extend(d)
            return maps
        imgs = x[:, 0]
        B = imgs.shape[0]
        maps = wavedec2_maps(imgs, 2)
        proc = [jax.image.resize(m, (B, 8, 8), method='bilinear') for m in maps]
        feat = jnp.stack(proc, axis=1)
        feat = feat.reshape(B, feat.shape[1], 64).transpose(0, 2, 1)
        return feat @ W + b

    def _L0_txt_ref(x, emb):
        import jax, jax.numpy as jnp
        import numpy as np
        INP_SIZE = 12500
        HIDDEN = 64
        KERNEL = 5
        WEIGHTS = jnp.array([0.1, 0.2, 0.4, 0.2, 0.1], dtype=jnp.float32)
        offsets = jnp.arange(-(KERNEL // 2), KERNEL // 2 + 1)
        idx = jnp.clip(x[..., None] + offsets, 0, INP_SIZE - 1)
        gathered = emb[idx]
        return jnp.einsum('btkh,k->bth', gathered, WEIGHTS)

    def _L0_attn_ref(x, Wq, Wk, Wv):
        import jax, jax.numpy as jnp
        import numpy as np
        B, N, D = (8, 512, 64)
        q = jnp.einsum('bnd,ed->bne', x, Wq)
        k = jnp.einsum('bnd,ed->bne', x, Wk)
        v = jnp.einsum('bnd,ed->bne', x, Wv)
        energy = jnp.einsum('bqd,bkd->bqk', q, k)
        scaling = jnp.asarray(x.shape[-1] ** (-0.5), x.dtype)
        att = jax.nn.softmax(energy, axis=-1) * scaling
        out = jnp.einsum('bqk,bkv->bqv', att, v)
        return out

    def _L0_ffn_ref(x, gate_w, gate_b, w1, b1, w2, b2, gamma, beta):
        import jax, jax.numpy as jnp
        import numpy as np
        B, S, H, F, E, K = (8, 1024, 64, 128, 16, 2)
        EPS = 1e-05
        gate_logits = x @ gate_w + gate_b
        topk_vals, topk_idx = jax.lax.top_k(gate_logits, K)
        topk_w = jax.nn.softmax(topk_vals, axis=-1)
        h = jax.nn.relu(jnp.einsum('bsh,ehf->bsef', x, w1) + b1)
        expert_out = jnp.einsum('bsef,efh->bseh', h, w2) + b2
        sel = jnp.take_along_axis(expert_out, topk_idx[:, :, :, None], axis=2)
        moe = jnp.sum(topk_w[..., None] * sel, axis=2)
        y = x + moe
        mu = jnp.mean(y, axis=-1, keepdims=True)
        var = jnp.var(y, axis=-1, keepdims=True)
        return (y - mu) / jnp.sqrt(var + EPS) * gamma + beta

    def _L1_attn_ref(x, Wqkv, Wout, bout, gamma, beta):
        import jax, jax.numpy as jnp
        import numpy as np
        HEADS = 8
        DIM = 64
        DIM_HEAD = 64
        DH = DIM_HEAD // HEADS
        SCALE = DIM_HEAD ** (-0.5)
        LN_EPS = 1e-05
        b, n, c = x.shape
        qkv = x @ Wqkv
        qkv = qkv.reshape(b, n, 3, HEADS, DH).transpose(2, 0, 3, 1, 4)
        q, k, v = (qkv[0], qkv[1], qkv[2])
        k = jax.nn.softmax(k, axis=-2)
        q = q * SCALE
        A = jnp.einsum('bhid,bhie->bhde', k, q)
        out = jnp.einsum('bhjd,bhde->bhje', v, A)
        out = out.reshape(b, n, c)
        out = out @ Wout + bout
        mu = jnp.mean(out, axis=-1, keepdims=True)
        var = jnp.var(out, axis=-1, keepdims=True)
        out = (out - mu) * jax.lax.rsqrt(var + LN_EPS) * gamma + beta
        return out

    def _L1_ffn_ref(x, route_id, Wi, bi, Wr, br, Ws, bs, Wo, bo):
        import jax, jax.numpy as jnp
        import numpy as np
        B, T, IN_DIM = (64, 64, 64)
        HID, OUT_DIM = (128, 64)
        N_LAYERS, N_EXPERTS, N_SHARED = (2, 16, 1)
        flat = x.reshape(-1, x.shape[-1])
        n_tok = flat.shape[0]
        route = jnp.repeat(route_id, n_tok // route_id.shape[0])
        h = jax.nn.relu(flat @ Wi.T + bi)
        n_layers, n_experts = (Wr.shape[0], Wr.shape[1])
        for l in range(n_layers):
            shared = (jnp.einsum('nd,shd->snh', h, Ws[l]) + bs[l][:, None, :]).mean(axis=0)
            routed = jnp.zeros_like(h)
            for e in range(n_experts):
                ye = h @ Wr[l, e].T + br[l, e]
                routed = routed + jnp.where((route == e)[:, None], ye, 0.0)
            h = jax.nn.relu(shared + routed + h)
        out = h @ Wo.T + bo
        return out.reshape(*x.shape[:-1], out.shape[-1])

    def _L2_attn_ref(x, Wq, Wk, Wv):
        import jax, jax.numpy as jnp
        import numpy as np
        D_IN = 64
        D_OUT = 64
        q = jnp.einsum('bsi,oi->bso', x, Wq)
        k = jnp.einsum('bsi,oi->bso', x, Wk)
        v = jnp.einsum('bsi,oi->bso', x, Wv)
        d_k = k.shape[-1]
        scores = jnp.einsum('bqd,bkd->bqk', q, k) / jnp.sqrt(jnp.asarray(d_k, q.dtype))
        weights = jax.nn.softmax(scores, axis=-1)
        return jnp.einsum('bqk,bkd->bqd', weights, v)

    def _L2_ffn_ref(features, router_w1, router_b1, router_w2, router_b2, expert_w1, expert_b1, expert_w2, expert_b2, expert_w3, expert_b3):
        import jax, jax.numpy as jnp
        import numpy as np
        E, D, H, TOP_K = (6, 64, 64, 2)
        ROUTER_H = D // 2
        rh = jax.nn.relu(features @ router_w1 + router_b1)
        expert_logits = jax.nn.softmax(rh @ router_w2 + router_b2, axis=-1)
        top_w, top_i = jax.lax.top_k(expert_logits, TOP_K)
        routing_weights = jax.nn.softmax(top_w, axis=-1)
        h1 = jax.nn.relu(jnp.einsum('bsd,edh->bseh', features, expert_w1) + expert_b1)
        h2 = jax.nn.relu(jnp.einsum('bseh,ehf->bsef', h1, expert_w2) + expert_b2)
        expert_out = jnp.einsum('bsef,efo->bseo', h2, expert_w3) + expert_b3
        sel = jnp.take_along_axis(expert_out, top_i[:, :, :, None], axis=2)
        combined = jnp.sum(sel * routing_weights[..., None], axis=2)
        return combined

    def _L3_attn_ref(x, Wq, bq, Wk, bk, Wv, bv, Wo, bo):
        import jax, jax.numpy as jnp
        import numpy as np
        DIM = 64
        HEADS = 4
        HEAD_DIM = DIM // HEADS
        SCALE = HEAD_DIM ** (-0.5)
        B, N, C = x.shape
        x = jnp.clip(x, -10000.0, 10000.0)

        def heads(t):
            return t.reshape(B, N, HEADS, HEAD_DIM).transpose(0, 2, 1, 3)
        q = heads((x @ Wq.T + bq).astype(jnp.float32))
        k = heads((x @ Wk.T + bk).astype(jnp.float32))
        v = heads((x @ Wv.T + bv).astype(jnp.float32))
        attn = jnp.einsum('bhnd,bhmd->bhnm', q, k) * SCALE
        attn = jax.nn.softmax(attn, axis=-1)
        out = jnp.einsum('bhnm,bhmd->bhnd', attn, v)
        out = out.transpose(0, 2, 1, 3).reshape(B, N, C)
        out = out.astype(jnp.bfloat16).astype(jnp.float32)
        return out @ Wo.T + bo

    def _L3_ffn_ref(x, router_w, router_b, W1, b1, W2, b2):
        import jax, jax.numpy as jnp
        import numpy as np
        B, K, D = (128, 16, 64)
        E = 32
        H = int(D * 0.25)
        xf = x.reshape(-1, D)
        logits = xf @ router_w.T + router_b
        idx = jnp.argmax(logits, axis=-1)
        w1t = jnp.take(W1, idx, axis=0)
        h = jnp.einsum('nd,ndh->nh', xf, w1t) + jnp.take(b1, idx, axis=0)
        h = jax.nn.relu(h)
        w2t = jnp.take(W2, idx, axis=0)
        out = jnp.einsum('nh,nhd->nd', h, w2t) + jnp.take(b2, idx, axis=0)
        out = jax.nn.relu(out)
        return out.reshape(x.shape)
    h = _L0_tok_ref(x, L0_tok_W, L0_tok_b)
    h = jnp.concatenate([h, _L0_txt_ref(x_txt, L0_txt_emb)], axis=1)
    h = h + _L0_attn_ref(_layernorm(h, axis=-1), L0_attn_Wq, L0_attn_Wk, L0_attn_Wv)
    h = h + _L0_ffn_ref(_layernorm(h, axis=-1), L0_ffn_gate_w, L0_ffn_gate_b, L0_ffn_w1, L0_ffn_b1, L0_ffn_w2, L0_ffn_b2, L0_ffn_gamma, L0_ffn_beta)
    h = h + _L1_attn_ref(_layernorm(h, axis=-1), L1_attn_Wqkv, L1_attn_Wout, L1_attn_bout, L1_attn_gamma, L1_attn_beta)
    h = h + _L1_ffn_ref(_layernorm(h, axis=-1), L1_ffn_route_id, L1_ffn_Wi, L1_ffn_bi, L1_ffn_Wr, L1_ffn_br, L1_ffn_Ws, L1_ffn_bs, L1_ffn_Wo, L1_ffn_bo)
    h = h + _L2_attn_ref(_layernorm(h, axis=-1), L2_attn_Wq, L2_attn_Wk, L2_attn_Wv)
    h = h + _L2_ffn_ref(_layernorm(h, axis=-1), L2_ffn_router_w1, L2_ffn_router_b1, L2_ffn_router_w2, L2_ffn_router_b2, L2_ffn_expert_w1, L2_ffn_expert_b1, L2_ffn_expert_w2, L2_ffn_expert_b2, L2_ffn_expert_w3, L2_ffn_expert_b3)
    h = h + _L3_attn_ref(_layernorm(h, axis=-1), L3_attn_Wq, L3_attn_bq, L3_attn_Wk, L3_attn_bk, L3_attn_Wv, L3_attn_bv, L3_attn_Wo, L3_attn_bo)
    h = h + _L3_ffn_ref(_layernorm(h, axis=-1), L3_ffn_router_w, L3_ffn_router_b, L3_ffn_W1, L3_ffn_b1, L3_ffn_W2, L3_ffn_b2)
    return h

_drawn_inputs = setup_inputs


def setup_inputs(seed=0):
    import zlib

    import numpy as np

    out = dict(_drawn_inputs(seed))
    spreads = {'L0_tok_b': (0.0, 0.1),
     'L0_ffn_gate_b': (0.0, 0.1),
     'L0_ffn_b1': (0.0, 0.73),
     'L0_ffn_b2': (0.0, 0.1),
     'L0_ffn_gamma': (1.0, 0.2),
     'L0_ffn_beta': (0.0, 0.1),
     'L1_attn_bout': (0.0, 0.1),
     'L1_attn_gamma': (1.0, 0.2),
     'L1_attn_beta': (0.0, 0.1),
     'L1_ffn_bi': (0.0, 0.638),
     'L1_ffn_bo': (0.0, 0.1),
     'L2_ffn_router_b1': (0.0, 0.33),
     'L2_ffn_router_b2': (0.0, 0.1),
     'L2_ffn_expert_b1': (0.0, 0.753),
     'L2_ffn_expert_b2': (0.0, 0.445),
     'L2_ffn_expert_b3': (0.0, 0.1),
     'L3_attn_bq': (0.0, 0.8),
     'L3_attn_bk': (0.0, 0.8),
     'L3_attn_bv': (0.0, 0.1),
     'L3_attn_bo': (0.0, 0.1)}
    factors = {'L0_ffn_w1': 4.53,
     'L0_ffn_w2': 3.65,
     'L1_attn_Wqkv': 8.0,
     'L1_attn_Wout': 8.0,
     'L1_ffn_Wi': 4.047,
     'L1_ffn_Wr': 6.808,
     'L1_ffn_br': 8.0,
     'L1_ffn_Ws': 6.932,
     'L1_ffn_bs': 8.0,
     'L2_attn_Wq': 3.897,
     'L2_attn_Wk': 3.63,
     'L3_ffn_b1': 5.915}
    for name, (base, spread) in spreads.items():
        noise = np.random.default_rng([zlib.crc32(name.encode()), seed]).standard_normal(out[name].shape)
        drawn = base * np.exp(spread * noise) if base else spread * noise
        out[name] = jnp.asarray(drawn.astype(out[name].dtype))
    for name, factor in factors.items():
        out[name] = (out[name] * factor).astype(out[name].dtype)
    return out
```

```python
from contextlib import ExitStack

import numpy as np

import concourse.bass as bass
from concourse import mybir

F32 = mybir.dt.float32
BF16 = mybir.dt.bfloat16
I32 = mybir.dt.int32
ALU = mybir.AluOpType
ACT = mybir.ActivationFunctionType
X = mybir.AxisListType.X

P = 128
BATCH, T, D = 128, 192, 64
IMG, TI, TT = 224, 64, 128
HALF = IMG // 2
VOCAB, TAPS = 12500, 5
QN = 2 * T
E0, F0 = 16, 128
E1, F1 = 16, 128
E2, R2 = 6, 32
E3, F3 = 32, 16
HEADS3 = 4
BIG = 1e30
EPS = 1e-5

PACK_A = [("rows", 64), ("cols", 64), ("tok_b", 1), ("taps", TAPS * P)]
PACK_B = [("ident", P), ("centre", P), ("mean", P),
          ("a0_wk", P), ("a0_wq", P), ("a0_wv", 4 * P),
          ("f0_gate_w", 2 * E0), ("f0_gate_b", 6 * E0), ("f0_rank", 6 * E0),
          ("f0_w1", E0 * F0), ("f0_b1", E0), ("f0_w2", E0 * D), ("f0_b2", P), ("f0_pick", 2 * E0),
          ("f0_gamma", 1), ("f0_beta", 1),
          ("a1_wq", P), ("a1_wk", P), ("a1_wv", P), ("a1_wo", 8 * P), ("a1_heads", P), ("a1_head", 8),
          ("a1_bo", 1), ("a1_gamma", 1), ("a1_beta", 1)]
PACK_C = [("f1_wi", F1), ("f1_bi", 1), ("f1_wr", 2 * E1 * F1), ("f1_br", 2 * E1),
          ("f1_ws", 2 * F1), ("f1_bs", 2), ("f1_wo", D), ("f1_bo", 1),
          ("a2_wk", P), ("a2_wq", P), ("a2_wv", 4 * P),
          ("f2_rw1", 2 * R2), ("f2_rb1", 1), ("f2_rw2", 2 * E2), ("f2_rb2", 6 * E2), ("f2_rank", 6 * E2),
          ("f2_w1", 3 * P), ("f2_b1", 3), ("f2_w2", 3 * P), ("f2_b2", 3), ("f2_w3", E2 * D), ("f2_b3", P),
          ("a3_wq", P), ("a3_bq", 1), ("a3_wk", P), ("a3_bk", 1), ("a3_wv", P), ("a3_bv", P),
          ("a3_wo", P), ("a3_bo", 1), ("a3_heads", 2 * HEADS3),
          ("f3_rw", 2 * D), ("f3_rb", 6 * E3), ("f3_rank", 6 * E3),
          ("f3_w1", 4 * P), ("f3_b1", 4), ("f3_shut", 4 * P), ("f3_w2", 4 * D), ("f3_b2", P)]


def columns(pack):
    at, where = 0, {}
    for name, n in pack:
        where[name] = (at, n)
        at += n
    return where, at


class Chip:

    def __init__(self, nc, quads, hidden, psum, eps):
        self.nc, self.quads, self.hidden, self.psum, self.eps = nc, quads, hidden, psum, eps
        self.operand = {}
        self.semaphores = []

    def semaphore(self, name):
        self.semaphores.append(self.nc.alloc_semaphore(name))
        return self.semaphores[-1]

    def end_phase(self):
        self.nc.clear_and_free_semaphores(self.semaphores)
        self.nc.all_engine_barrier()
        self.semaphores = []

    def place(self, pack, tile):
        for name, (at, n) in columns(pack)[0].items():
            self.operand[name] = tile[:, at:at + n]

    def bank(self, u, i):
        return self.psum[:, 4 * u + i, :]

    def h_quad(self, q):
        return self.hidden[:, bass.ds(q * QN, QN)]

    def loop(self, eng, body):
        body(0)
        if self.quads > 2:
            with eng.Fori(1, self.quads // 2) as it:
                body(it)


def embedding(chip, images, neighbours):
    nc, op = chip.nc, chip.operand
    group, side = 16, 8

    with ExitStack() as ctx:
        def sb(n, shape, dt=F32):
            return ctx.enter_context(nc.sbuf_tensor(f"emb_{n}", shape, dt))

        def sem(n):
            return chip.semaphore(f"emb_{n}")

        image = sb("image", [HALF, 4, 8, 2 * IMG])
        gathered = sb("gathered", [P, 2, group, TAPS * D])
        by_row = sb("by_row", [HALF, 2, 2, 512])
        maps = sb("maps", [32, 2, group, 4, side])
        index = sb("index", [TT, 2, group], I32)
        indexed, pool_passed = sem("indexed"), sem("pool_passed")
        loaded = [sem(f"loaded_{s}") for s in range(4)]
        fetched = [sem(f"fetched_{u}") for u in range(2)]
        rows_done, by_row_ready, cols_done, maps_ready = sem("rows_done"), sem("by_row_ready"), sem("cols_done"), sem("maps_ready")
        embedded, image_placed = sem("embedded"), sem("image_placed")
        weighed, text_act, text_dve = sem("weighed"), sem("text_act"), sem("text_dve")

        block = ctx.enter_context(nc.Block())

        def first(it):
            return isinstance(it, int) and it == 0

        def loop(eng, body):
            body(0)
            if chip.quads > 8:
                with eng.Fori(1, chip.quads // 8) as it:
                    body(it)

        def pairs_of(k):
            return chip.hidden[:, bass.ds(k * 8 * T, 8 * T)].rearrange("p (g t) -> p g t", t=T)

        def load(eng, it, half):
            for u in range(2):
                k = 2 * it + u
                if not first(it):
                    eng.wait_ge(rows_done, k - 1)
                some = images[bass.ds(k * group + 8 * half, 8), :, :, :]
                eng.dma_start(image[:, 2 * u + half, :, :],
                              some.rearrange("i o (p a) c -> p (i o) (a c)", a=2)).then_inc(loaded[2 * u + half], 16)

        @block.sync
        def _(sp):
            loop(sp, lambda it: load(sp, it, 0))

        @block.gpsimd
        def _(pool):
            def body(it):
                for u in range(2):
                    k = 2 * it + u
                    if not first(it):
                        pool.wait_ge(weighed, 2 * k - 2)
                    pool.sem_inc(pool_passed, 1)
                    nc.gpsimd.tensor_copy(index[:, u, :], chip.tokens[:, bass.ds(k * group, group)]).then_inc(indexed, 1)
                    pool.wait_ge(indexed, k + 1)
                    pool.sem_inc(pool_passed, 1)
                    for j in range(group):
                        nc.gpsimd.indirect_dma_start(
                            gathered[:, u, j, :], None, neighbours,
                            bass.IndirectOffsetOnAxis(ap=index[:, u, j:j + 1], axis=0),
                        ).then_inc(fetched[u], 16)

            loop(pool, body)

        @block.tensor
        def _(pe):
            def body(it):
                lanes = [(u, 2 * it + u) for u in range(2)]
                for u, k in lanes:
                    if not first(it):
                        pe.wait_ge(image_placed, k - 1)
                        pe.wait_ge(text_dve, k - 1)
                    for half in range(2):
                        pe.wait_ge(loaded[2 * u + half], 16 * (it + 1))
                        for ch in range(2):
                            for i in range(8):
                                for a in range(2):
                                    at = (8 * half + i) * 32
                                    last = nc.tensor.matmul(
                                        chip.bank(u, ch)[0:HALF, at:at + 32],
                                        image[:, 2 * u + half, i, a * IMG + ch * HALF:a * IMG + (ch + 1) * HALF],
                                        op["rows"][0:HALF, a * 32:(a + 1) * 32], start=(a == 0), stop=(a == 1))
                    last.then_inc(rows_done, 1)
                for u, k in lanes:
                    pe.wait_ge(by_row_ready, k + 1)
                    for ch in range(2):
                        last = nc.tensor.matmul(chip.bank(u, 2)[0:32, :], op["cols"][0:HALF, ch * 32:(ch + 1) * 32],
                                                by_row[:, u, ch, :], start=(ch == 0), stop=(ch == 1))
                    last.then_inc(cols_done, 1)
                for u, k in lanes:
                    pe.wait_ge(maps_ready, k + 1)
                    for cj in range(side):
                        for rt in range(4):
                            for b in range(2):
                                last = nc.tensor.matmul(
                                    chip.bank(u, 0)[64 * b:64 * b + 64, cj * 64:(cj + 1) * 64],
                                    chip.embed[0:32, (4 * cj + rt) * D:(4 * cj + rt + 1) * D],
                                    maps[:, u, b::2, rt, :], start=(rt == 0), stop=(rt == 3))
                    last.then_inc(embedded, 1)
                for u, k in lanes:
                    pe.wait_ge(fetched[u], 16 * group * (it + 1))
                    for half, bank in ((0, 3), (1, 1)):
                        if half == 0 and not first(it):
                            pe.wait_ge(text_act, k - 1)
                        for g in range(4):
                            for tap in range(TAPS):
                                for b in range(2):
                                    last = nc.tensor.matmul(
                                        chip.bank(u, bank)[64 * b:64 * b + 64, g * TT:(g + 1) * TT],
                                        gathered[:, u, 8 * half + 2 * g + b, tap * D:(tap + 1) * D],
                                        op["taps"][:, tap * P:(tap + 1) * P], start=(tap == 0), stop=(tap == TAPS - 1))
                        last.then_inc(weighed, 1)

            loop(pe, body)

        @block.scalar
        def _(act):
            def body(it):
                lanes = [(u, 2 * it + u) for u in range(2)]
                load(act, it, 1)
                for u, k in lanes:
                    act.wait_ge(rows_done, k + 1)
                    nc.scalar.activation(by_row[:, u, :, :], chip.psum[0:HALF, 4 * u:4 * u + 2, :],
                                         ACT.Copy).then_inc(by_row_ready, 1)
                for u, k in lanes:
                    act.wait_ge(cols_done, k + 1)
                    nc.scalar.activation(maps[:, u, :, :, :].rearrange("p i r c -> p (i r c)"), chip.bank(u, 2)[0:32, :],
                                         ACT.Copy).then_inc(maps_ready, 1)
                for u, k in lanes:
                    act.wait_ge(weighed, 2 * k + 1)
                    nc.scalar.activation(pairs_of(k)[:, 0:4, TI:T],
                                         chip.bank(u, 3).rearrange("p (g t) -> p g t", t=TT),
                                         ACT.Copy).then_inc(text_act, 1)

            loop(act, body)

        @block.vector
        def _(dve):
            def body(it):
                lanes = [(u, 2 * it + u) for u in range(2)]
                for u, k in lanes:
                    dve.wait_ge(embedded, k + 1)
                    nc.vector.tensor_scalar(pairs_of(k)[:, :, 0:TI].rearrange("p g (r c) -> p g c r", c=side),
                                            chip.bank(u, 0).rearrange("p (c g r) -> p g c r", c=side, g=8),
                                            op["tok_b"], None, ALU.add).then_inc(image_placed, 1)
                for u, k in lanes:
                    dve.wait_ge(weighed, 2 * k + 2)
                    nc.vector.tensor_copy(pairs_of(k)[:, 4:8, TI:T],
                                          chip.bank(u, 1).rearrange("p (g t) -> p g t", t=TT)).then_inc(text_dve, 1)

            loop(dve, body)


class Norm:

    def __init__(self, chip, ctx, tag, bank=None):
        nc = chip.nc
        self.chip, self.bank = chip, bank or chip.bank
        self.square = ctx.enter_context(nc.sbuf_tensor(f"{tag}_square", [P, 2, QN], F32))
        self.log = ctx.enter_context(nc.sbuf_tensor(f"{tag}_log", [P, 2, QN], F32))
        self.rstd = ctx.enter_context(nc.sbuf_tensor(f"{tag}_rstd", [P, 2, QN], F32))
        self.centred = chip.semaphore(f"{tag}_centred")
        self.squared = chip.semaphore(f"{tag}_squared")
        self.averaged = chip.semaphore(f"{tag}_averaged")
        self.logged = chip.semaphore(f"{tag}_logged")
        self.rstd_ready = chip.semaphore(f"{tag}_rstd_ready")
        self.ready = chip.semaphore(f"{tag}_ready")

    def centre(self, u, source):
        c = self.chip
        c.nc.tensor.matmul(self.bank(u, 0)[:, 0:QN], c.operand["centre"], source,
                           start=True, stop=True).then_inc(self.centred, 1)

    def squares(self, act, u, q):
        act.wait_ge(self.centred, q + 1)
        self.chip.nc.scalar.activation(self.square[:, u, :], self.bank(u, 0)[:, 0:QN],
                                       ACT.Square).then_inc(self.squared, 1)

    def average(self, pe, u, q):
        c = self.chip
        pe.wait_ge(self.squared, q + 1)
        c.nc.tensor.matmul(self.bank(u, 1)[:, 0:QN], c.operand["mean"], self.square[:, u, :],
                           start=True, stop=True).then_inc(self.averaged, 1)

    def logs(self, act, u, q):
        act.wait_ge(self.averaged, q + 1)
        self.chip.nc.scalar.activation(self.log[:, u, :], self.bank(u, 1)[:, 0:QN], ACT.Ln,
                                       bias=self.chip.eps[:, 0:1]).then_inc(self.logged, 1)

    def powers(self, act, u, q):
        act.wait_ge(self.logged, q + 1)
        self.chip.nc.scalar.activation(self.rstd[:, u, :], self.log[:, u, :], ACT.Exp,
                                       scale=-0.5).then_inc(self.rstd_ready, 1)

    def scale(self, dve, u, q, out):
        dve.wait_ge(self.rstd_ready, q + 1)
        self.chip.nc.vector.tensor_tensor(out, self.bank(u, 0)[:, 0:QN], self.rstd[:, u, :],
                                          ALU.mult).then_inc(self.ready, 1)


def attention(chip, name, score_scale, value_scale):
    nc, op, ident = chip.nc, chip.operand, chip.operand["ident"]
    with ExitStack() as ctx:
        def sb(n, shape, dt=F32):
            return ctx.enter_context(nc.sbuf_tensor(f"{name}_{n}", shape, dt))

        def sem(n):
            return chip.semaphore(f"{name}_{n}")

        norm = Norm(chip, ctx, f"{name}_norm")
        m_t = sb("m_t", [P, P])
        xn = sb("xn", [P, 2, QN])
        xb = sb("xb", [P, 2, 6, 2, 64])
        ym = sb("ym", [P, 2, QN])
        xt = sb("xt", [P, 2, 2, P])
        xz = sb("xz", [P, 2, 2, P])
        peak = sb("peak", [P, 2, 6])
        total = sb("total", [P, 2, 6])
        inverse = sb("inverse", [P, 2, 6])
        prob = sb("prob", [P, 2, 3, 2, T])
        prob_t = sb("prob_t", [P, 2, 3, QN])
        mix = sb("mix", [P, 2, 3, 2, 64])
        mix_t = sb("mix_t", [P, 2, 2, 3, 64])

        m_done, m_ready = sem("m_done"), sem("m_ready")
        cleared, pool_passed = sem("cleared"), sem("pool_passed")
        xb_ready, ym_done, ym_ready = sem("xb_ready"), sem("ym_done"), sem("ym_ready")
        xt_done, xt_ready, xz_ready = sem("xt_done"), sem("xt_ready"), sem("xz_ready")
        scored, peak_ready, exp_ready = sem("scored"), sem("peak_ready"), sem("exp_ready")
        inverse_ready = sem("inverse_ready")
        prob_done, prob_act, prob_dve = sem("prob_done"), sem("prob_act"), sem("prob_dve")
        mixed, mix_ready, mix_done, mix_t_ready = sem("mixed"), sem("mix_ready"), sem("mix_done"), sem("mix_t_ready")
        valued, h_ready = sem("valued"), sem("h_ready")

        def scores_of(u, pair):
            two = chip.psum[:, 4 * u + 2 * pair:4 * u + 2 * pair + 2, :]
            return two.rearrange("p b (c n) -> p (b c) n", n=256)[:, 0:3, 0:T]

        block = ctx.enter_context(nc.Block())

        @block.tensor
        def _(pe):
            nc.tensor.matmul(chip.bank(0, 3)[:, 0:P], op[f"{name}_wk"], op[f"{name}_wq"],
                             start=True, stop=True).then_inc(m_done, 1)
            pe.wait_ge(m_ready, 1)
            pe.wait_ge(cleared, 2)

            def body(it):
                lanes = [(u, 2 * it + u) for u in range(2)]
                for u, q in lanes:
                    if not (isinstance(it, int) and it == 0):
                        pe.wait_ge(h_ready, q - 1)
                    norm.centre(u, chip.h_quad(q))
                for u, q in lanes:
                    norm.average(pe, u, q)
                for u, q in lanes:
                    pe.wait_ge(norm.ready, q + 1)
                    nc.tensor.matmul(chip.bank(u, 1)[:, 0:QN], m_t[:, :], xn[:, u, :],
                                     start=True, stop=True).then_inc(ym_done, 1)
                    for s, out in ((0, chip.bank(u, 2)[:, 0:P]), (2, chip.bank(u, 2)[:, P:2 * P]),
                                   (1, chip.bank(u, 3)[:, 0:P])):
                        last = nc.tensor.transpose(out, xn[:, u, s * P:(s + 1) * P], ident)
                    last.then_inc(xt_done, 1)
                for u, q in lanes:
                    pe.wait_ge(xb_ready, q + 1)
                    pe.wait_ge(ym_ready, q + 1)
                    pe.wait_ge(xt_ready, q + 1)
                    pe.wait_ge(xz_ready, q + 1)
                    for pair in range(2):
                        for c in range(3):
                            last = nc.tensor.matmul(scores_of(u, pair)[:, c, :],
                                                    xb[:, u, 3 * pair + c, :, :].rearrange("p b t -> p (b t)"),
                                                    ym[:, u, pair * T:(pair + 1) * T], start=True, stop=True)
                        last.then_inc(scored, 1)
                for u, q in lanes:
                    pe.wait_ge(exp_ready, 2 * q + 2)
                    for s in range(3):
                        for c in range(3):
                            keys = prob[:, u, c, :, :].rearrange("p g t -> p (g t)")[:, s * P:(s + 1) * P]
                            last = nc.tensor.transpose(chip.bank(u, s)[:, c * P:(c + 1) * P], keys, ident)
                        last.then_inc(prob_done, 1)
                for u, q in lanes:
                    pe.wait_ge(prob_act, 2 * q + 2)
                    pe.wait_ge(prob_dve, q + 1)
                    for pair in range(2):
                        for c in range(3):
                            out = chip.bank(u, 3 if pair else 0)[:, c * P:(c + 1) * P]
                            nc.tensor.matmul(out, prob_t[:, u, 2 * pair, c * P:(c + 1) * P], xt[:, u, pair, :],
                                             start=True, stop=False)
                            last = nc.tensor.matmul(out, prob_t[:, u, 1, c * P:(c + 1) * P], xz[:, u, pair, :],
                                                    start=False, stop=True)
                    last.then_inc(mixed, 1)
                for u, q in lanes:
                    pe.wait_ge(mix_ready, q + 1)
                    for c in range(3):
                        last = nc.tensor.transpose(chip.bank(u, 1)[:, c * P:(c + 1) * P],
                                                   mix[:, u, c, :, :].rearrange("p g d -> p (g d)"), ident)
                    last.then_inc(mix_done, 1)
                for u, q in lanes:
                    pe.wait_ge(mix_t_ready, q + 1)
                    for pair in range(2):
                        for b in range(2):
                            wv = op[f"{name}_wv"][:, (2 * pair + b) * P:(2 * pair + b + 1) * P]
                            last = nc.tensor.matmul(chip.bank(u, 2)[:, pair * T:(pair + 1) * T], wv,
                                                    mix_t[:, u, b, :, :].rearrange("p c t -> p (c t)"),
                                                    start=(b == 0), stop=(b == 1))
                    last.then_inc(valued, 1)

            chip.loop(pe, body)

        @block.scalar
        def _(act):
            nc.scalar.preload_act_table_set("natural_log_exp_and_others")
            act.wait_ge(m_done, 1)
            nc.scalar.activation(m_t[:, :], chip.bank(0, 3)[:, 0:P], ACT.Copy,
                                 scale=score_scale).then_inc(m_ready, 1)

            def body(it):
                lanes = [(u, 2 * it + u) for u in range(2)]
                for u, q in lanes:
                    norm.squares(act, u, q)
                for u, q in lanes:
                    norm.logs(act, u, q)
                for u, q in lanes:
                    norm.powers(act, u, q)
                for u, q in lanes:
                    act.wait_ge(ym_done, q + 1)
                    nc.scalar.activation(ym[:, u, :], chip.bank(u, 1)[:, 0:QN], ACT.Copy).then_inc(ym_ready, 1)
                    act.wait_ge(xt_done, q + 1)
                    nc.scalar.activation(xt[:, u, :, :], chip.bank(u, 2)[:, 0:2 * P].rearrange("p (g d) -> p g d", g=2),
                                         ACT.Copy).then_inc(xt_ready, 1)
                for u, q in lanes:
                    for pair in range(2):
                        act.wait_ge(peak_ready, 2 * q + pair + 1)
                        for c in range(3):
                            last = nc.scalar.activation(prob[:, u, c, pair, :], scores_of(u, pair)[:, c, :], ACT.Exp,
                                                        bias=peak[:, u, 3 * pair + c:3 * pair + c + 1],
                                                        accum_out=total[:, u, 3 * pair + c:3 * pair + c + 1])
                        last.then_inc(exp_ready, 1)
                for u, q in lanes:
                    for s in (0, 2):
                        act.wait_ge(prob_done, 3 * q + s + 1)
                        nc.scalar.activation(prob_t[:, u, s, :], chip.bank(u, s)[:, 0:QN],
                                             ACT.Copy).then_inc(prob_act, 1)
                for u, q in lanes:
                    act.wait_ge(mix_done, q + 1)
                    nc.scalar.activation(mix_t[:, u, :, :, :].rearrange("p b c t -> p c b t"),
                                         chip.bank(u, 1)[:, 0:QN].rearrange("p (c b t) -> p c b t", c=3, b=2),
                                         ACT.Copy).then_inc(mix_t_ready, 1)

            chip.loop(act, body)

        @block.vector
        def _(dve):
            def body(it):
                lanes = [(u, 2 * it + u) for u in range(2)]
                for u, q in lanes:
                    norm.scale(dve, u, q, xn[:, u, :])
                for u, q in lanes:
                    dve.wait_ge(xt_done, q + 1)
                    for pair in range(2):
                        half = slice(64 * pair, 64 * pair + 64)
                        last = nc.vector.tensor_copy(xz[half, u, pair, :], chip.bank(u, 3)[half, 0:P])
                    last.then_inc(xz_ready, 1)
                for u, q in lanes:
                    for pair in range(2):
                        dve.wait_ge(scored, 2 * q + pair + 1)
                        nc.vector.tensor_reduce(peak[:, u, 3 * pair:3 * pair + 3], scores_of(u, pair), X, ALU.max,
                                                negate=True).then_inc(peak_ready, 1)
                for u, q in lanes:
                    dve.wait_ge(exp_ready, 2 * q + 2)
                    nc.vector.reciprocal(inverse[:, u, :], total[:, u, :]).then_inc(inverse_ready, 1)
                for u, q in lanes:
                    dve.wait_ge(prob_done, 3 * q + 2)
                    nc.vector.tensor_copy(prob_t[:, u, 1, :], chip.bank(u, 1)[:, 0:QN]).then_inc(prob_dve, 1)
                for u, q in lanes:
                    dve.wait_ge(mixed, q + 1)
                    dve.wait_ge(inverse_ready, q + 1)
                    for b in range(2):
                        half = slice(64 * b, 64 * b + 64)
                        for pair in range(2):
                            out = chip.bank(u, 3 if pair else 0)[half, 0:QN].rearrange("p (c b d) -> p c b d", c=3, b=2)
                            last = nc.vector.tensor_tensor(
                                mix[half, u, :, pair, :], out[:, :, b, :],
                                inverse[half, u, 3 * pair:3 * pair + 3].unsqueeze(2).to_broadcast([64, 3, 64]), ALU.mult)
                    last.then_inc(mix_ready, 1)
                for u, q in lanes:
                    dve.wait_ge(valued, q + 1)
                    nc.vector.scalar_tensor_tensor(chip.h_quad(q), chip.bank(u, 2)[:, 0:QN], value_scale,
                                                   chip.h_quad(q), ALU.mult, ALU.add).then_inc(h_ready, 1)

            chip.loop(dve, body)

        @block.gpsimd
        def _(pool):
            nc.gpsimd.memset(xb[:, :, :, :, :], 0.0).then_inc(cleared, 1)
            nc.gpsimd.memset(xz[:, :, :, :], 0.0).then_inc(cleared, 1)

            def body(it):
                lanes = [(u, 2 * it + u) for u in range(2)]
                for u, q in lanes:
                    pool.wait_ge(norm.ready, q + 1)
                    if not (isinstance(it, int) and it == 0):
                        pool.wait_ge(scored, 2 * q - 2)
                    pool.wait_ge(cleared, 2)
                    pool.sem_inc(pool_passed, 1)
                    for b in range(2):
                        half = slice(64 * b, 64 * b + 64)
                        last = nc.gpsimd.tensor_copy(xb[half, u, :, b, :],
                                                     xn[half, u, :].rearrange("p (c t) -> p c t", t=64))
                    last.then_inc(xb_ready, 1)

            chip.loop(pool, body)



def top_two(chip, dve, step, wait, scores, rank, experts, w, groups=12):
    nc = chip.nc

    def wide(a):
        return a.unsqueeze(2).to_broadcast([P, groups, experts])

    source = scores
    for n, (best, hot) in enumerate(((w["best1"], w["hot1"]), (w["best2"], w["hot2"]))):
        step(nc.vector.tensor_reduce(best[:, :], source, X, ALU.max))
        wait()
        step(nc.vector.tensor_tensor(w["equal"][:, :, :], source, wide(best[:, :]), ALU.is_equal))
        wait()
        step(nc.vector.tensor_tensor(w["ranked"][:, :, :], w["equal"][:, :, :], rank, ALU.mult))
        wait()
        step(nc.vector.tensor_reduce(w["first"][:, :], w["ranked"][:, :, :], X, ALU.max))
        wait()
        step(nc.vector.tensor_tensor(hot[:, :, :], rank, wide(w["first"][:, :]), ALU.is_equal))
        wait()
        if n == 0:
            step(nc.vector.scalar_tensor_tensor(w["rest"][:, :, :], hot[:, :, :], -3e38, source, ALU.mult, ALU.add))
            wait()
            source = w["rest"][:, :, :]


def gates_of_two(chip, dve, step, wait, experts, w, gap_ready, ratio_ready, gates_ready, it, groups=12):
    nc = chip.nc

    def wide(a):
        return a[:, :].unsqueeze(2).to_broadcast([P, groups, experts])

    nc.vector.tensor_tensor(w["gap"][:, :], w["best2"][:, :], w["best1"][:, :], ALU.subtract).then_inc(gap_ready, 1)
    dve.wait_ge(ratio_ready, it + 1)
    step(nc.vector.tensor_scalar(w["whole"][:, :], w["ratio"][:, :], 1.0, None, ALU.add))
    wait()
    step(nc.vector.reciprocal(w["w1"][:, :], w["whole"][:, :]))
    wait()
    step(nc.vector.tensor_tensor(w["w2"][:, :], w["ratio"][:, :], w["w1"][:, :], ALU.mult))
    wait()
    step(nc.vector.tensor_tensor(w["gate1"][:, :, :], w["hot1"][:, :, :], wide(w["w1"]), ALU.mult))
    wait()
    step(nc.vector.tensor_tensor(w["ranked"][:, :, :], w["hot2"][:, :, :], wide(w["w2"]), ALU.mult))
    wait()
    nc.vector.tensor_tensor(w["gate"][:, :, :], w["gate1"][:, :, :], w["ranked"][:, :, :],
                            ALU.add).then_inc(gates_ready, 1)
    dve.wait_ge(gates_ready, it + 1)


def experts0(chip):
    nc, op = chip.nc, chip.operand
    with ExitStack() as ctx:
        def sb(n, shape, dt=F32):
            return ctx.enter_context(nc.sbuf_tensor(f"f0_{n}", shape, dt))

        def sem(n):
            return chip.semaphore(f"f0_{n}")

        rows = 3 * 2 * E0
        norm = Norm(chip, ctx, "f0_norm", lambda u, i: chip.psum[:, 6 + i, :])
        post = Norm(chip, ctx, "f0_post", lambda u, i: chip.psum[:, 6 + i, :])
        xn = sb("xn", [P, 2, QN])
        y = sb("y", [P, 2, QN])
        yn = sb("yn", [P, 2, QN])
        yg = sb("yg", [P, 2, QN])
        scores = sb("scores", [P, 6, E0])
        work = {n: sb(n, [P, 6, E0]) for n in ("equal", "ranked", "rest", "hot1", "hot2", "gate1", "gate")}
        work |= {n: sb(n, [P, 6]) for n in ("best1", "best2", "first", "gap", "ratio", "whole", "w1", "w2")}
        remains = sb("remains", [P, 2, 3, 2 * E0])
        parts = sb("parts", [P, 3, 3, 2 * E0], BF16)
        parts_t = sb("parts_t", [rows, 2, QN], BF16)
        parts_t32 = sb("parts_t32", [rows, 2, QN])
        ident_b = sb("ident_b", [P, P], BF16)
        pick = sb("pick", [rows, E0, 2, D], BF16)
        hid = sb("hid", [P, 2, 2, QN])
        spread = sb("spread", [P, 2, QN])
        share = sb("share", [P, 2, QN])

        set_up, scored = sem("set_up"), sem("scored")
        steps = [sem(f"step{n}") for n in range(23)]
        gap_ready, ratio_ready = sem("gap_ready"), sem("ratio_ready")
        gates_ready, parts_ready, parts_done, parts_t_ready = (
            sem("gates_ready"), sem("parts_ready"), sem("parts_done"), sem("parts_t_ready"))
        base_done, base_ready = sem("base_done"), sem("base_ready")
        hid_done = [sem(f"hid_done{e}") for e in range(E0)]
        hid_ready = [sem(f"hid_ready{e}") for e in range(E0)]
        expert_done = [sem(f"expert_done{e}") for e in range(E0)]
        share_ready = [sem(f"share_ready{e}") for e in range(E0)]
        spread_done = [sem(f"spread_done{e}") for e in range(E0)]
        spread_ready = [sem(f"spread_ready{e}") for e in range(E0)]
        added = sem("added")
        yg_ready, h_ready = sem("yg_ready"), sem("h_ready")

        def at_start(q):
            return isinstance(q, int) and q == 0

        def loop(eng, quad):
            def both(it, last):
                for u in range(2):
                    quad(u, 2 * it + u, not (last and u == 1))

            pairs = chip.quads // 2
            both(0, pairs == 1)
            if pairs > 2:
                with eng.Fori(1, pairs - 1) as it:
                    both(it, False)
            if pairs > 1:
                both(pairs - 1, True)

        block = ctx.enter_context(nc.Block())

        @block.tensor
        def _(pe):
            def score(u, q):
                pe.wait_ge(norm.ready, q + 1)
                for j in range(3):
                    last = nc.tensor.matmul(chip.psum[:, 7, 2 * E0 * j:2 * E0 * (j + 1)],
                                            xn[:, u, j * P:(j + 1) * P], op["f0_gate_w"], start=True, stop=True)
                last.then_inc(scored, 1)

            def turn_gates(q):
                pe.wait_ge(parts_ready, q + 1)
                for j in range(3):
                    last = nc.tensor.matmul(chip.psum[0:rows, 6, j * P:(j + 1) * P],
                                            parts[:, j, :, :].rearrange("p a e -> p (a e)"), ident_b[:, :],
                                            start=True, stop=True)
                last.then_inc(parts_done, 1)

            def hidden(u, q, e):
                if e >= 2:
                    pe.wait_ge(hid_ready[e - 2], q + 1)
                elif not at_start(q):
                    pe.wait_ge(hid_ready[E0 - 2 + e], q)
                for b in range(2):
                    half = slice(64 * b, 64 * b + 64)
                    last = nc.tensor.matmul(chip.psum[:, 2 * (e % 2) + b, 0:QN], op["f0_w1"][half, e * F0:(e + 1) * F0],
                                            xn[half, u, :], start=True, stop=True)
                last.then_inc(hid_done[e], 1)

            def base(u, q):
                pe.wait_ge(parts_t_ready, 2 * q + 2)
                if not at_start(q):
                    pe.wait_ge(share_ready[E0 - 1], q)
                nc.tensor.matmul(chip.psum[:, 4, 0:QN], op["f0_b2"][0:rows, :], parts_t32[:, u, :],
                                 start=True, stop=True).then_inc(base_done, 1)

            def output(u, q, e):
                if e:
                    pe.wait_ge(share_ready[e - 1], q + 1)
                else:
                    pe.wait_ge(base_ready, q + 1)
                pe.wait_ge(hid_ready[e], q + 1)
                for b in range(2):
                    last = nc.tensor.matmul(chip.psum[64 * b:64 * b + 64, 4, 0:QN], op["f0_w2"][:, e * D:(e + 1) * D],
                                            hid[:, e % 2, b, :], start=True, stop=True)
                last.then_inc(expert_done[e], 1)

            def spread_gates(u, q, e):
                if e:
                    pe.wait_ge(spread_ready[e - 1], q + 1)
                elif not at_start(q):
                    pe.wait_ge(spread_ready[E0 - 1], q)
                nc.tensor.matmul(chip.psum[:, 5, 0:QN], pick[:, e, :, :].rearrange("p b d -> p (b d)"),
                                 parts_t[:, u, :], start=True, stop=True).then_inc(spread_done[e], 1)

            def quad(u, q, more):
                for e in range(E0):
                    hidden(u, q, e)
                    if e == 0:
                        base(u, q)
                    spread_gates(u, q, e)
                    if e == 1 and not at_start(q):
                        pe.wait_ge(added, E0 * q)
                        post.centre(1 - u, y[:, 1 - u, :])
                    if e == 2 and not at_start(q):
                        post.average(pe, 1 - u, q - 1)
                    if e == 5 and more:
                        if not at_start(q):
                            pe.wait_ge(post.ready, q)
                        norm.centre(1 - u, chip.h_quad(q + 1))
                    if e == 6 and more:
                        norm.average(pe, 1 - u, q + 1)
                    if e == 8 and more:
                        score(1 - u, q + 1)
                    if e:
                        output(u, q, e - 1)
                if more:
                    turn_gates(q + 1)
                output(u, q, E0 - 1)

            pe.wait_ge(set_up, 2)
            norm.centre(0, chip.h_quad(0))
            norm.average(pe, 0, 0)
            score(0, 0)
            turn_gates(0)
            loop(pe, quad)
            pe.wait_ge(added, E0 * chip.quads)
            post.centre(1, y[:, 1, :])
            post.average(pe, 1, chip.quads - 1)

        @block.scalar
        def _(act):
            nc.scalar.preload_act_table_set("natural_log_exp_and_others")
            def exponentiate(q):
                act.wait_ge(gap_ready, q + 1)
                nc.scalar.activation(work["ratio"][:, :], work["gap"][:, :], ACT.Exp).then_inc(ratio_ready, 1)

            def keep_gates(u, q):
                act.wait_ge(parts_done, q + 1)
                for copy in (parts_t, parts_t32):
                    nc.scalar.activation(copy[:, u, :], chip.psum[0:rows, 6, 0:QN], ACT.Copy).then_inc(parts_t_ready, 1)

            def quad(u, q, more):
                for e in range(E0):
                    act.wait_ge(hid_done[e], q + 1)
                    if e >= 2:
                        act.wait_ge(expert_done[e - 2], q + 1)
                    elif not at_start(q):
                        act.wait_ge(expert_done[E0 - 2 + e], q)
                    for b in range(2):
                        last = nc.scalar.activation(hid[:, e % 2, b, :], chip.psum[:, 2 * (e % 2) + b, 0:QN], ACT.Relu,
                                                    bias=op["f0_b1"][:, e:e + 1])
                    last.then_inc(hid_ready[e], 1)
                    if e == 1 and not at_start(q):
                        post.squares(act, 1 - u, q - 1)
                    if e == 3 and not at_start(q):
                        post.logs(act, 1 - u, q - 1)
                        post.powers(act, 1 - u, q - 1)
                    if e == 5 and more:
                        norm.squares(act, 1 - u, q + 1)
                    if e == 6 and more:
                        norm.logs(act, 1 - u, q + 1)
                        norm.powers(act, 1 - u, q + 1)
                    if e == 11 and more:
                        exponentiate(q + 1)
                if more:
                    keep_gates(1 - u, q + 1)

            norm.squares(act, 0, 0)
            norm.logs(act, 0, 0)
            norm.powers(act, 0, 0)
            exponentiate(0)
            keep_gates(0, 0)
            loop(act, quad)
            post.squares(act, 1, chip.quads - 1)
            post.logs(act, 1, chip.quads - 1)
            post.powers(act, 1, chip.quads - 1)

        @block.vector
        def _(dve):
            nc.vector.tensor_copy(ident_b[:, :], op["ident"]).then_inc(set_up, 1)
            nc.vector.tensor_copy(pick[:, :, :, :].rearrange("p e b d -> p (e b) d"),
                                  op["f0_pick"][0:rows, :].unsqueeze(2).to_broadcast([rows, 2 * E0, D])
                                  ).then_inc(set_up, 1)

            def gates(q, between):
                link = [0]

                def step(instruction):
                    instruction.then_inc(steps[link[0]], 1)

                def wait():
                    dve.wait_ge(steps[link[0]], q + 1)
                    link[0] += 1
                    if link[0] % 5 == 0:
                        between()

                dve.wait_ge(scored, q + 1)
                flat = scores[:, :, :]
                step(nc.vector.tensor_tensor(flat.rearrange("p g e -> p (g e)"), chip.psum[:, 7, 0:6 * E0],
                                             op["f0_gate_b"], ALU.add))
                wait()
                top_two(chip, dve, step, wait, flat, op["f0_rank"].rearrange("p (g e) -> p g e", e=E0), E0, work, 6)
                gates_of_two(chip, dve, step, wait, E0, work, gap_ready, ratio_ready, gates_ready, q, 6)
                gate = work["gate"][:, :, :].rearrange("p (j b) e -> p j (b e)", b=2)
                if not at_start(q):
                    dve.wait_ge(parts_done, q)
                step(nc.vector.tensor_copy(parts[:, :, 0, :], gate))
                wait()
                step(nc.vector.tensor_tensor(remains[:, 0, :, :], gate, parts[:, :, 0, :], ALU.subtract))
                wait()
                step(nc.vector.tensor_copy(parts[:, :, 1, :], remains[:, 0, :, :]))
                wait()
                nc.vector.tensor_tensor(parts[:, :, 2, :], remains[:, 0, :, :], parts[:, :, 1, :],
                                        ALU.subtract).then_inc(parts_ready, 1)

            def finish(u, q):
                yield post.scale(dve, u, q, yn[:, u, :])
                dve.wait_ge(post.ready, q + 1)
                yield nc.vector.tensor_scalar(yg[:, u, :], yn[:, u, :], op["f0_gamma"], op["f0_beta"],
                                              ALU.mult, ALU.add).then_inc(yg_ready, 1)
                dve.wait_ge(yg_ready, q + 1)
                yield nc.vector.tensor_tensor(chip.h_quad(q), chip.h_quad(q), yg[:, u, :], ALU.add)

            def quad(u, q, more):
                at = [0]

                def copy_gates(e):
                    dve.wait_ge(spread_done[e], q + 1)
                    nc.vector.tensor_copy(spread[:, e % 2, :], chip.psum[:, 5, 0:QN]).then_inc(spread_ready[e], 1)

                def share_of_next_expert():
                    e = at[0]
                    at[0] += 1
                    dve.wait_ge(expert_done[e], q + 1)
                    dve.wait_ge(spread_ready[e], q + 1)
                    if e >= 2 or not at_start(q):
                        dve.wait_ge(added, E0 * q + e - 1)
                    nc.vector.tensor_tensor(share[:, e % 2, :], chip.psum[:, 4, 0:QN], spread[:, e % 2, :],
                                            ALU.mult).then_inc(share_ready[e], 1)
                    if e + 1 < E0:
                        copy_gates(e + 1)

                dve.wait_ge(base_done, q + 1)
                nc.vector.tensor_tensor(y[:, u, :], chip.psum[:, 4, 0:QN], xn[:, u, :], ALU.add).then_inc(base_ready, 1)
                copy_gates(0)
                closing = iter(()) if at_start(q) else finish(1 - u, q - 1)
                while at[0] < 8:
                    share_of_next_expert()
                    if at[0] >= 4:
                        next(closing, None)
                    if at[0] == 7 and more:
                        norm.scale(dve, 1 - u, q + 1, xn[:, 1 - u, :])
                if more:
                    gates(q + 1, share_of_next_expert)
                while at[0] < E0:
                    share_of_next_expert()

            norm.scale(dve, 0, 0, xn[:, 0, :])
            gates(0, lambda: None)
            loop(dve, quad)
            for _ in finish(1, chip.quads - 1):
                pass

        @block.gpsimd
        def _(pool):
            def quad(u, q, more):
                pool.wait_ge(base_ready, q + 1)
                for e in range(E0):
                    if e:
                        pool.wait_ge(added, E0 * q + e)
                    pool.wait_ge(share_ready[e], q + 1)
                    nc.gpsimd.tensor_tensor(y[:, u, :], y[:, u, :], share[:, e % 2, :], ALU.add).then_inc(added, 1)

            loop(pool, quad)


def linear_attention(chip):
    nc, op, ident = chip.nc, chip.operand, chip.operand["ident"]
    with ExitStack() as ctx:
        def sb(n, shape, dt=F32):
            return ctx.enter_context(nc.sbuf_tensor(f"a1_{n}", shape, dt))

        def sem(n):
            return chip.semaphore(f"a1_{n}")

        norm = Norm(chip, ctx, "a1_norm")
        post = Norm(chip, ctx, "a1_post")
        xn = sb("xn", [P, 2, QN])
        value = sb("value", [P, 2, QN])
        query = sb("query", [P, 2, 3, P])
        peak = sb("peak", [P, 2, 2])
        total = sb("total", [P, 2, 2])
        inverse = sb("inverse", [P, 2, 2])
        key = sb("key", [P, 2, QN])
        key_t = sb("key_t", [P, 2, 2, P])
        key_z = sb("key_z", [P, 2, 2, P])
        outer = sb("outer", [P, 2, 2, P])
        o = sb("o", [P, 2, QN])
        spread_o = sb("spread", [P, 2, 2, 8, T])
        y = sb("y", [P, 2, QN])
        yn = sb("yn", [P, 2, QN])
        yg = sb("yg", [P, 2, QN])

        cleared = sem("cleared")
        projected, value_ready, query_ready = sem("projected"), sem("value_ready"), sem("query_ready")
        peak_ready, key_ready, inverse_ready = sem("peak_ready"), sem("key_ready"), sem("inverse_ready")
        key_done, key_t_ready, key_z_ready = sem("key_done"), sem("key_t_ready"), sem("key_z_ready")
        outer_done, outer_ready = sem("outer_done"), sem("outer_ready")
        o_done, o_ready, spread_ready = sem("o_done"), sem("o_ready"), sem("spread_ready")
        mixed, y_ready, yg_ready = sem("mixed"), sem("y_ready"), sem("yg_ready")

        block = ctx.enter_context(nc.Block())

        @block.tensor
        def _(pe):
            pe.wait_ge(cleared, 1)

            def body(it):
                lanes = [(u, 2 * it + u) for u in range(2)]
                for u, q in lanes:
                    if not (isinstance(it, int) and it == 0):
                        pe.wait_ge(post.ready, q - 1)
                    norm.centre(u, chip.h_quad(q))
                for u, q in lanes:
                    norm.average(pe, u, q)
                for u, q in lanes:
                    pe.wait_ge(norm.ready, q + 1)
                    nc.tensor.matmul(chip.bank(u, 1)[:, 0:QN], op["a1_wk"], xn[:, u, :], start=True, stop=True)
                    nc.tensor.matmul(chip.bank(u, 2)[:, 0:QN], op["a1_wv"], xn[:, u, :], start=True, stop=True)
                    for j in range(3):
                        last = nc.tensor.matmul(chip.bank(u, 3)[:, j * P:(j + 1) * P], xn[:, u, j * P:(j + 1) * P],
                                                op["a1_wq"], start=True, stop=True)
                    last.then_inc(projected, 1)
                for u, q in lanes:
                    pe.wait_ge(key_ready, q + 1)
                    pe.wait_ge(value_ready, q + 1)
                    for s, out in ((0, chip.bank(u, 0)[:, 0:P]), (2, chip.bank(u, 0)[:, P:2 * P]),
                                   (1, chip.bank(u, 2)[:, 0:P])):
                        last = nc.tensor.transpose(out, key[:, u, s * P:(s + 1) * P], ident)
                    last.then_inc(key_done, 1)
                for u, q in lanes:
                    pe.wait_ge(key_t_ready, q + 1)
                    pe.wait_ge(key_z_ready, q + 1)
                    pe.wait_ge(query_ready, q + 1)
                    for pair in range(2):
                        out = chip.bank(u, 1)[:, pair * P:(pair + 1) * P]
                        nc.tensor.matmul(out, key_t[:, u, pair, :], query[:, u, 2 * pair, :], start=True, stop=False)
                        last = nc.tensor.matmul(out, key_z[:, u, pair, :], query[:, u, 1, :], start=False, stop=True)
                    last.then_inc(outer_done, 1)
                for u, q in lanes:
                    pe.wait_ge(outer_ready, q + 1)
                    for pair in range(2):
                        last = nc.tensor.matmul(chip.bank(u, 3)[:, pair * T:(pair + 1) * T], outer[:, u, pair, :],
                                                value[:, u, pair * T:(pair + 1) * T], start=True, stop=True)
                    last.then_inc(o_done, 1)
                for u, q in lanes:
                    pe.wait_ge(spread_ready, q + 1)
                    tokens = spread_o[:, u, :, :, :].rearrange("p g h (j r) -> p r (g h j)", r=8)
                    for jr in range(8):
                        last = nc.tensor.matmul(chip.bank(u, 2)[:, 0:QN], op["a1_wo"][:, jr * P:(jr + 1) * P],
                                                tokens[:, jr, :], start=(jr == 0), stop=(jr == 7))
                    last.then_inc(mixed, 1)
                for u, q in lanes:
                    pe.wait_ge(y_ready, q + 1)
                    post.centre(u, y[:, u, :])
                for u, q in lanes:
                    post.average(pe, u, q)

            chip.loop(pe, body)

        @block.scalar
        def _(act):
            nc.scalar.preload_act_table_set("natural_log_exp_and_others")
            def body(it):
                lanes = [(u, 2 * it + u) for u in range(2)]
                for u, q in lanes:
                    norm.squares(act, u, q)
                for u, q in lanes:
                    norm.logs(act, u, q)
                for u, q in lanes:
                    norm.powers(act, u, q)
                for u, q in lanes:
                    act.wait_ge(projected, q + 1)
                    nc.scalar.activation(query[:, u, :, :], chip.bank(u, 3)[:, 0:QN].rearrange("p (s e) -> p s e", s=3),
                                         ACT.Copy, scale=D ** -0.5).then_inc(query_ready, 1)
                for u, q in lanes:
                    act.wait_ge(peak_ready, q + 1)
                    for pair in range(2):
                        cols = slice(pair * T, (pair + 1) * T)
                        last = nc.scalar.activation(key[:, u, cols], chip.bank(u, 1)[:, cols], ACT.Exp,
                                                    bias=peak[:, u, pair:pair + 1], accum_out=total[:, u, pair:pair + 1])
                    last.then_inc(key_ready, 1)
                for u, q in lanes:
                    act.wait_ge(key_done, q + 1)
                    nc.scalar.activation(key_t[:, u, :, :], chip.bank(u, 0)[:, 0:2 * P].rearrange("p (g d) -> p g d", g=2),
                                         ACT.Copy).then_inc(key_t_ready, 1)
                for u, q in lanes:
                    act.wait_ge(o_done, q + 1)
                    nc.scalar.activation(o[:, u, :], chip.bank(u, 3)[:, 0:QN], ACT.Copy).then_inc(o_ready, 1)
                for u, q in lanes:
                    act.wait_ge(mixed, q + 1)
                    nc.scalar.activation(y[:, u, :], chip.bank(u, 2)[:, 0:QN], ACT.Identity,
                                         bias=op["a1_bo"]).then_inc(y_ready, 1)
                for u, q in lanes:
                    post.squares(act, u, q)
                for u, q in lanes:
                    post.logs(act, u, q)
                for u, q in lanes:
                    post.powers(act, u, q)

            chip.loop(act, body)

        @block.vector
        def _(dve):
            nc.vector.memset(key_z[:, :, :, :], 0.0).then_inc(cleared, 1)
            dve.wait_ge(cleared, 1)

            def body(it):
                lanes = [(u, 2 * it + u) for u in range(2)]
                for u, q in lanes:
                    norm.scale(dve, u, q, xn[:, u, :])
                for u, q in lanes:
                    dve.wait_ge(projected, q + 1)
                    nc.vector.tensor_reduce(peak[:, u, :], chip.bank(u, 1)[:, 0:QN].rearrange("p (g t) -> p g t", t=T),
                                            X, ALU.max, negate=True).then_inc(peak_ready, 1)
                    nc.vector.tensor_copy(value[:, u, :], chip.bank(u, 2)[:, 0:QN]).then_inc(value_ready, 1)
                for u, q in lanes:
                    dve.wait_ge(key_ready, q + 1)
                    nc.vector.reciprocal(inverse[:, u, :], total[:, u, :]).then_inc(inverse_ready, 1)
                for u, q in lanes:
                    dve.wait_ge(key_done, q + 1)
                    for pair in range(2):
                        half = slice(64 * pair, 64 * pair + 64)
                        last = nc.vector.tensor_copy(key_z[half, u, pair, :], chip.bank(u, 2)[half, 0:P])
                    last.then_inc(key_z_ready, 1)
                for u, q in lanes:
                    dve.wait_ge(outer_done, q + 1)
                    dve.wait_ge(inverse_ready, q + 1)
                    for pair in range(2):
                        last = nc.vector.scalar_tensor_tensor(
                            outer[:, u, pair, :], chip.bank(u, 1)[:, pair * P:(pair + 1) * P],
                            inverse[:, u, pair:pair + 1], op["a1_heads"], ALU.mult, ALU.mult)
                    last.then_inc(outer_ready, 1)
                for u, q in lanes:
                    dve.wait_ge(o_ready, q + 1)
                    for h in range(8):
                        last = nc.vector.tensor_scalar(spread_o[:, u, :, h, :],
                                                       o[:, u, :].rearrange("p (g t) -> p g t", t=T),
                                                       op["a1_head"][:, h:h + 1], None, ALU.mult)
                    last.then_inc(spread_ready, 1)
                for u, q in lanes:
                    post.scale(dve, u, q, yn[:, u, :])
                for u, q in lanes:
                    dve.wait_ge(post.ready, q + 1)
                    nc.vector.tensor_scalar(yg[:, u, :], yn[:, u, :], op["a1_gamma"], op["a1_beta"],
                                            ALU.mult, ALU.add).then_inc(yg_ready, 1)
                for u, q in lanes:
                    dve.wait_ge(yg_ready, q + 1)
                    nc.vector.tensor_tensor(chip.h_quad(q), chip.h_quad(q), yg[:, u, :], ALU.add)

            chip.loop(dve, body)


def routed(chip):
    nc, op = chip.nc, chip.operand
    with ExitStack() as ctx:
        def sb(n, shape, dt=F32):
            return ctx.enter_context(nc.sbuf_tensor(f"f1_{n}", shape, dt))

        def sem(n):
            return chip.semaphore(f"f1_{n}")

        norm = Norm(chip, ctx, "f1_norm")
        xn = sb("xn", [P, 2, QN])
        shared = sb("shared", [P, 2, F1])
        weight = sb("weight", [P, 2, 2, 2, F1])
        bias = sb("bias", [P, 2, 2, 2])
        hid = [sb(f"hid{n}", [P, 2, 2, 2, T]) for n in range(3)]
        shared_ready = sem("shared_ready")
        weight_ready = sem("weight_ready")
        entered = sem("entered")
        hid_act = [sem(f"hid_act{n}") for n in range(3)]
        hid_dve = [sem(f"hid_dve{n}") for n in range(3)]
        layered = [sem(f"layered{n}") for n in range(2)]
        left, h_ready = sem("left"), sem("h_ready")

        block = ctx.enter_context(nc.Block())

        @block.tensor
        def _(pe):
            def body(it):
                lanes = [(u, 2 * it + u) for u in range(2)]
                for u, q in lanes:
                    if not (isinstance(it, int) and it == 0):
                        pe.wait_ge(h_ready, q - 1)
                    norm.centre(u, chip.h_quad(q))
                for u, q in lanes:
                    norm.average(pe, u, q)
                for u, q in lanes:
                    pe.wait_ge(norm.ready, q + 1)
                    for b in range(2):
                        half = slice(64 * b, 64 * b + 64)
                        last = nc.tensor.matmul(chip.bank(u, 2 + b)[:, 0:QN], op["f1_wi"][half, :], xn[half, u, :],
                                                start=True, stop=True)
                    last.then_inc(entered, 1)
                for layer in range(2):
                    for u, q in lanes:
                        pe.wait_ge(hid_act[layer], q + 1)
                        pe.wait_ge(hid_dve[layer], q + 1)
                        if layer == 0:
                            pe.wait_ge(weight_ready, q + 1)
                        for pair in range(2):
                            out = chip.bank(u, (2 * layer + pair) % 4)[:, 0:QN]
                            last = nc.tensor.matmul(out, weight[:, u, layer, pair, :],
                                                    hid[layer][:, u, pair, :, :].rearrange("p b t -> p (b t)"),
                                                    start=True, stop=True)
                        last.then_inc(layered[layer], 1)
                for u, q in lanes:
                    pe.wait_ge(hid_act[2], q + 1)
                    pe.wait_ge(hid_dve[2], q + 1)
                    for b in range(2):
                        for pair in range(2):
                            last = nc.tensor.matmul(
                                chip.bank(u, 0)[64 * b:64 * b + 64, pair * T:(pair + 1) * T], op["f1_wo"],
                                hid[2][:, u, pair, b, :], start=True, stop=True)
                    last.then_inc(left, 1)

            chip.loop(pe, body)

        @block.scalar
        def _(act):
            nc.scalar.preload_act_table_set("natural_log_exp_and_others")
            def body(it):
                lanes = [(u, 2 * it + u) for u in range(2)]
                for u, q in lanes:
                    norm.squares(act, u, q)
                for u, q in lanes:
                    norm.logs(act, u, q)
                for u, q in lanes:
                    norm.powers(act, u, q)
                for u, q in lanes:
                    act.wait_ge(entered, q + 1)
                    nc.scalar.activation(hid[0][:, u, :, 0, :], chip.bank(u, 2)[:, 0:QN].rearrange("p (g t) -> p g t", g=2),
                                         ACT.Relu, bias=op["f1_bi"]).then_inc(hid_act[0], 1)
                for layer in range(2):
                    for u, q in lanes:
                        act.wait_ge(layered[layer], q + 1)
                        nc.scalar.activation(hid[layer + 1][:, u, 0, :, :].rearrange("p b t -> p (b t)"),
                                             chip.bank(u, 2 * layer)[:, 0:QN], ACT.Relu,
                                             bias=bias[:, u, layer, 0:1]).then_inc(hid_act[layer + 1], 1)

            chip.loop(act, body)

        @block.vector
        def _(dve):
            def body(it):
                lanes = [(u, 2 * it + u) for u in range(2)]
                for u, q in lanes:
                    norm.scale(dve, u, q, xn[:, u, :])
                for u, q in lanes:
                    dve.wait_ge(entered, q + 1)
                    nc.vector.tensor_scalar(hid[0][:, u, :, 1, :], chip.bank(u, 3)[:, 0:QN].rearrange("p (g t) -> p g t", g=2),
                                            op["f1_bi"], 0.0, ALU.add, ALU.max).then_inc(hid_dve[0], 1)
                for layer in range(2):
                    for u, q in lanes:
                        dve.wait_ge(layered[layer], q + 1)
                        nc.vector.tensor_scalar(hid[layer + 1][:, u, 1, :, :].rearrange("p b t -> p (b t)"),
                                                chip.bank(u, 2 * layer + 1)[:, 0:QN], bias[:, u, layer, 1:2], 0.0,
                                                ALU.add, ALU.max).then_inc(hid_dve[layer + 1], 1)
                for u, q in lanes:
                    dve.wait_ge(left, q + 1)
                    nc.vector.scalar_tensor_tensor(chip.h_quad(q), chip.bank(u, 0)[:, 0:QN], op["f1_bo"],
                                                   chip.h_quad(q), ALU.add, ALU.add).then_inc(h_ready, 1)

            chip.loop(dve, body)

        @block.gpsimd
        def _(pool):
            for layer in range(2):
                last = nc.gpsimd.tensor_tensor(shared[:, layer, :], op["f1_ws"][:, layer * F1:(layer + 1) * F1],
                                               op["ident"], ALU.add)
                last.then_inc(shared_ready, 1)
            pool.wait_ge(shared_ready, 2)

            def body(it):
                lanes = [(u, 2 * it + u) for u in range(2)]
                for u, q in lanes:
                    if not (isinstance(it, int) and it == 0):
                        pool.wait_ge(h_ready, q - 1)
                    for pair in range(2):
                        route = pool.value_load(chip.routes[0:1, bass.ds(2 * q + pair, 1)], min_val=0, max_val=E1 - 1)
                        for layer in range(2):
                            nc.gpsimd.tensor_tensor(weight[:, u, layer, pair, :],
                                                    op["f1_wr"][:, bass.ds(route * F1 + layer * E1 * F1, F1)],
                                                    shared[:, layer, :], ALU.add)
                            last = nc.gpsimd.tensor_tensor(bias[:, u, layer, pair:pair + 1],
                                                           op["f1_br"][:, bass.ds(route + layer * E1, 1)],
                                                           op["f1_bs"][:, layer:layer + 1], ALU.add)
                    last.then_inc(weight_ready, 1)

            chip.loop(pool, body)


def experts2(chip):
    nc, op, ident = chip.nc, chip.operand, chip.operand["ident"]
    with ExitStack() as ctx:
        def sb(n, shape, dt=F32):
            return ctx.enter_context(nc.sbuf_tensor(f"f2_{n}", shape, dt))

        def sem(n):
            return chip.semaphore(f"f2_{n}")

        norm = Norm(chip, ctx, "f2_norm")
        xn = sb("xn", [P, 2, QN])
        router = sb("router", [2 * R2, 2, QN])
        scores = sb("scores", [P, 2, 6 * E2])
        rank = sb("rank", [P, 2, 6 * E2])
        shift, power, share = (sb(n, [P, 12, E2]) for n in ("shift", "power", "share"))
        top, total, inverse = (sb(n, [P, 12]) for n in ("top", "total", "inverse"))
        work = {n: sb(n, [P, 12, E2]) for n in ("equal", "ranked", "rest", "hot1", "hot2", "gate1", "gate")}
        work |= {n: sb(n, [P, 12]) for n in ("best1", "best2", "first", "gap", "ratio", "whole", "w1", "w2")}
        gate_t = sb("gate_t", [2 * E2, 2, QN])
        hid1 = sb("hid1", [P, 2, 2, QN])
        hid2 = sb("hid2", [P, 2, 2, 2, QN])
        gated = sb("gated", [P, 2, 2, 3, 2, D])

        rank_ready = sem("rank_ready")
        routed_done, router_ready, scored = sem("routed_done"), sem("router_ready"), sem("scored")
        shift_ready, power_ready = sem("shift_ready"), sem("power_ready")
        steps = [sem(f"step{n}") for n in range(21)]
        gap_ready, ratio_ready = sem("gap_ready"), sem("ratio_ready")
        gates_ready, gates_done, gate_t_ready = sem("gates_ready"), sem("gates_done"), sem("gate_t_ready")
        hid1_done, hid1_act, hid1_dve, hid2_done, hid2_ready = (
            [sem(f"{n}{k}") for k in range(3)] for n in ("hid1_done", "hid1_act", "hid1_dve", "hid2_done", "hid2_ready"))
        expert_done = [sem(f"expert_done{e}") for e in range(E2)]
        gated_ready = [sem(f"gated_ready{e}") for e in range(E2)]
        summed, h_ready = sem("summed"), sem("h_ready")

        block = ctx.enter_context(nc.Block())

        @block.tensor
        def _(pe):
            def body(it):
                lanes = [(u, 2 * it + u) for u in range(2)]
                for u, q in lanes:
                    if not (isinstance(it, int) and it == 0):
                        pe.wait_ge(h_ready, q - 1)
                    norm.centre(u, chip.h_quad(q))
                for u, q in lanes:
                    norm.average(pe, u, q)
                for u, q in lanes:
                    pe.wait_ge(norm.ready, q + 1)
                    nc.tensor.matmul(chip.bank(u, 2)[0:2 * R2, 0:QN], op["f2_rw1"], xn[:, u, :],
                                     start=True, stop=True).then_inc(routed_done, 1)

                def first(k):
                    for u, q in lanes:
                        if k:
                            pe.wait_ge(hid2_ready[k - 1], q + 1)
                        for b in range(2):
                            half = slice(64 * b, 64 * b + 64)
                            last = nc.tensor.matmul(chip.bank(u, b)[:, 0:QN], op["f2_w1"][half, k * P:(k + 1) * P],
                                                    xn[half, u, :], start=True, stop=True)
                        last.then_inc(hid1_done[k], 1)

                def second(k):
                    for u, q in lanes:
                        pe.wait_ge(hid1_act[k], q + 1)
                        pe.wait_ge(hid1_dve[k], q + 1)
                        for b in range(2):
                            last = nc.tensor.matmul(chip.bank(u, b)[:, 0:QN], op["f2_w2"][:, k * P:(k + 1) * P],
                                                    hid1[:, u, b, :], start=True, stop=True)
                        last.then_inc(hid2_done[k], 1)

                def outputs(e):
                    for u, q in lanes:
                        pe.wait_ge(hid2_ready[e // 2], q + 1)
                        if e:
                            pe.wait_ge(gated_ready[e - 1], q + 1)
                        for j in range(3):
                            for b in range(2):
                                last = nc.tensor.matmul(
                                    chip.bank(u, 2)[:, (2 * j + b) * D:(2 * j + b + 1) * D],
                                    hid2[:, u, (e // 2) % 2, b, j * P:(j + 1) * P], op["f2_w3"][:, e * D:(e + 1) * D],
                                    start=True, stop=True)
                        last.then_inc(expert_done[e], 1)

                def collect(e):
                    for u, q in lanes:
                        pe.wait_ge(gated_ready[e], q + 1)
                        for j in range(3):
                            last = nc.tensor.matmul(chip.bank(u, 3)[:, j * P:(j + 1) * P],
                                                    gated[:, u, e % 2, j, :, :].rearrange("p b d -> p (b d)"), ident,
                                                    is_transpose=True, start=False, stop=(e == E2 - 1),
                                                    skip_group_check=True)
                        if e == E2 - 1:
                            last.then_inc(summed, 1)

                first(0)
                for u, q in lanes:
                    pe.wait_ge(router_ready, q + 1)
                    for j in range(3):
                        last = nc.tensor.matmul(chip.bank(u, 2)[:, 2 * E2 * j:2 * E2 * (j + 1)],
                                                router[:, u, j * P:(j + 1) * P], op["f2_rw2"][0:2 * R2, :],
                                                start=True, stop=True)
                    last.then_inc(scored, 1)
                second(0)
                for u, q in lanes:
                    pe.wait_ge(gates_ready, it + 1)
                    for j in range(3):
                        last = nc.tensor.transpose(chip.bank(u, 3)[0:2 * E2, j * P:(j + 1) * P],
                                                   work["gate"][:, 6 * u + 2 * j:6 * u + 2 * j + 2, :]
                                                   .rearrange("p g e -> p (g e)"), ident)
                    last.then_inc(gates_done, 1)
                first(1)
                for u, q in lanes:
                    pe.wait_ge(gate_t_ready, q + 1)
                    nc.tensor.matmul(chip.bank(u, 3)[:, 0:QN], op["f2_b3"][0:2 * E2, :], gate_t[:, u, :],
                                     start=True, stop=False, skip_group_check=True)
                for k in range(3):
                    outputs(2 * k)
                    if k < 2:
                        second(k + 1)
                    collect(2 * k)
                    outputs(2 * k + 1)
                    if k == 0:
                        first(2)
                    collect(2 * k + 1)

            chip.loop(pe, body)

        @block.scalar
        def _(act):
            nc.scalar.preload_act_table_set("natural_log_exp_and_others")
            def body(it):
                lanes = [(u, 2 * it + u) for u in range(2)]
                for u, q in lanes:
                    norm.squares(act, u, q)
                for u, q in lanes:
                    norm.logs(act, u, q)
                for u, q in lanes:
                    norm.powers(act, u, q)
                for u, q in lanes:
                    act.wait_ge(routed_done, q + 1)
                    nc.scalar.activation(router[:, u, :], chip.bank(u, 2)[0:2 * R2, 0:QN], ACT.Relu,
                                         bias=op["f2_rb1"][0:2 * R2, :]).then_inc(router_ready, 1)

                def hidden1(k):
                    for u, q in lanes:
                        act.wait_ge(hid1_done[k], q + 1)
                        nc.scalar.activation(hid1[:, u, 0, :], chip.bank(u, 0)[:, 0:QN], ACT.Relu,
                                             bias=op["f2_b1"][:, k:k + 1]).then_inc(hid1_act[k], 1)

                def hidden2(k):
                    for u, q in lanes:
                        act.wait_ge(hid2_done[k], q + 1)
                        if k == 2:
                            act.wait_ge(expert_done[1], q + 1)
                        for b in range(2):
                            last = nc.scalar.activation(hid2[:, u, k % 2, b, :], chip.bank(u, b)[:, 0:QN], ACT.Relu,
                                                        bias=op["f2_b2"][:, k:k + 1])
                        last.then_inc(hid2_ready[k], 1)

                hidden1(0)
                act.wait_ge(shift_ready, it + 1)
                nc.scalar.activation(power[:, :, :], shift[:, :, :], ACT.Exp).then_inc(power_ready, 1)
                hidden2(0)
                act.wait_ge(gap_ready, it + 1)
                nc.scalar.activation(work["ratio"][:, :], work["gap"][:, :], ACT.Exp).then_inc(ratio_ready, 1)
                for u, q in lanes:
                    act.wait_ge(gates_done, q + 1)
                    nc.scalar.activation(gate_t[:, u, :], chip.bank(u, 3)[0:2 * E2, 0:QN],
                                         ACT.Copy).then_inc(gate_t_ready, 1)
                for k in (1, 2):
                    hidden1(k)
                    hidden2(k)

            chip.loop(act, body)

        @block.vector
        def _(dve):
            for u in range(2):
                last = nc.vector.tensor_copy(rank[:, u, :], op["f2_rank"])
            last.then_inc(rank_ready, 1)
            dve.wait_ge(rank_ready, 1)

            def body(it):
                lanes = [(u, 2 * it + u) for u in range(2)]
                link = [0]

                def step(instruction):
                    instruction.then_inc(steps[link[0]], 1)

                def wait():
                    dve.wait_ge(steps[link[0]], it + 1)
                    link[0] += 1

                def wide(a):
                    return a[:, :].unsqueeze(2).to_broadcast([P, 12, E2])

                def hidden1(k):
                    for u, q in lanes:
                        dve.wait_ge(hid1_done[k], q + 1)
                        nc.vector.tensor_scalar(hid1[:, u, 1, :], chip.bank(u, 1)[:, 0:QN], op["f2_b1"][:, k:k + 1],
                                                0.0, ALU.add, ALU.max).then_inc(hid1_dve[k], 1)

                def gate(e):
                    for u, q in lanes:
                        dve.wait_ge(expert_done[e], q + 1)
                        nc.vector.tensor_tensor(
                            gated[:, u, e % 2, :, :, :].rearrange("p j b d -> p (j b) d"),
                            chip.bank(u, 2)[:, 0:6 * D].rearrange("p (g d) -> p g d", d=D),
                            work["gate"][:, 6 * u:6 * u + 6, e:e + 1].to_broadcast([P, 6, D]),
                            ALU.mult).then_inc(gated_ready[e], 1)

                for u, q in lanes:
                    norm.scale(dve, u, q, xn[:, u, :])
                hidden1(0)
                for u, q in lanes:
                    dve.wait_ge(scored, q + 1)
                    last = nc.vector.tensor_tensor(scores[:, u, :], chip.bank(u, 2)[:, 0:6 * E2], op["f2_rb2"], ALU.add)
                step(last)
                wait()
                flat = scores[:, :, :].rearrange("p u (g e) -> p (u g) e", e=E2)
                ranks = rank[:, :, :].rearrange("p u (g e) -> p (u g) e", e=E2)
                step(nc.vector.tensor_reduce(top[:, :], flat, X, ALU.max))
                wait()
                nc.vector.tensor_tensor(shift[:, :, :], flat, wide(top), ALU.subtract).then_inc(shift_ready, 1)
                dve.wait_ge(power_ready, it + 1)
                step(nc.vector.tensor_reduce(total[:, :], power[:, :, :], X, ALU.add))
                wait()
                step(nc.vector.reciprocal(inverse[:, :], total[:, :]))
                wait()
                step(nc.vector.tensor_tensor(share[:, :, :], power[:, :, :], wide(inverse), ALU.mult))
                wait()
                top_two(chip, dve, step, wait, share[:, :, :], ranks, E2, work)
                gates_of_two(chip, dve, step, wait, E2, work, gap_ready, ratio_ready, gates_ready, it)
                hidden1(1)
                gate(0)
                gate(1)
                hidden1(2)
                for e in range(2, E2):
                    gate(e)
                for u, q in lanes:
                    dve.wait_ge(summed, q + 1)
                    nc.vector.tensor_tensor(chip.h_quad(q), chip.bank(u, 3)[:, 0:QN], chip.h_quad(q),
                                            ALU.add).then_inc(h_ready, 1)

            chip.loop(dve, body)



def heads_attention(chip):
    nc, op, ident = chip.nc, chip.operand, chip.operand["ident"]
    hd = D // HEADS3
    wide = HEADS3 * (P + hd) + 64
    with ExitStack() as ctx:
        def sb(n, shape, dt=F32):
            return ctx.enter_context(nc.sbuf_tensor(f"a3_{n}", shape, dt))

        def sem(n):
            return chip.semaphore(f"a3_{n}")

        norm = Norm(chip, ctx, "a3_norm")
        xn = sb("xn", [P, 2, QN])
        query = sb("query", [P, 2, QN])
        query_b = sb("query_b", [P, 2, HEADS3, 6, 2, 64])
        key = sb("key", [P, 2, QN])
        value = sb("value", [P, 2, 2, wide])
        value_z = sb("value_z", [P, 2, 2, wide])
        peak = sb("peak", [P, 2, 3, 2])
        total = sb("total", [P, 2, 3, 2])
        inverse = sb("inverse", [P, 2, 3, 2])
        prob = sb("prob", [P, 2, 3, 2, T])
        even = sb("even", [P, 2, 3, 2, T])
        prob_t = sb("prob_t", [P, 2, 3, QN])
        mix_b = sb("mix_b", [P, 2, QN], BF16)
        mix = sb("mix", [P, 2, QN])

        cleared, pool_passed = sem("cleared"), sem("pool_passed")
        projected, query_ready, query_b_ready = sem("projected"), sem("query_ready"), sem("query_b_ready")
        key_ready, value_ready = sem("key_ready"), sem("value_ready")
        heads = range(HEADS3)
        scored, peak_ready, exp_ready, inverse_ready, even_ready, prob_done, prob_act, prob_dve, mixed = (
            [sem(f"{n}{h}") for h in heads] for n in (
                "scored", "peak_ready", "exp_ready", "inverse_ready", "even_ready", "prob_done", "prob_act",
                "prob_dve", "mixed"))
        mix_b_ready, mix_ready, left, h_ready = sem("mix_b_ready"), sem("mix_ready"), sem("left"), sem("h_ready")

        def scores_of(u):
            return chip.psum[:, 4 * u:4 * u + 3, 0:QN].rearrange("p c (g t) -> p c g t", t=T)

        block = ctx.enter_context(nc.Block())

        @block.tensor
        def _(pe):
            pe.wait_ge(cleared, 2)

            def body(it):
                lanes = [(u, 2 * it + u) for u in range(2)]
                for u, q in lanes:
                    if not (isinstance(it, int) and it == 0):
                        pe.wait_ge(h_ready, q - 1)
                    norm.centre(u, chip.h_quad(q))
                for u, q in lanes:
                    norm.average(pe, u, q)
                for u, q in lanes:
                    pe.wait_ge(norm.ready, q + 1)
                    nc.tensor.matmul(chip.bank(u, 1)[:, 0:QN], op["a3_wq"], xn[:, u, :], start=True, stop=True)
                    nc.tensor.matmul(chip.bank(u, 2)[:, 0:QN], op["a3_wk"], xn[:, u, :], start=True, stop=True)
                    for s in range(3):
                        last = nc.tensor.matmul(chip.bank(u, 3)[:, s * P:(s + 1) * P], xn[:, u, s * P:(s + 1) * P],
                                                op["a3_wv"], start=True, stop=True)
                    last.then_inc(projected, 1)

                def score(h):
                    for u, q in lanes:
                        if h == 0:
                            pe.wait_ge(query_b_ready, q + 1)
                            pe.wait_ge(key_ready, q + 1)
                        else:
                            pe.wait_ge(prob_act[h - 1], 2 * q + 2)
                            pe.wait_ge(prob_dve[h - 1], q + 1)
                        for c in range(3):
                            for pair in range(2):
                                last = nc.tensor.matmul(scores_of(u)[:, c, pair, :],
                                                        query_b[:, u, h, 3 * pair + c, :, :].rearrange("p b t -> p (b t)"),
                                                        key[:, u, pair * T:(pair + 1) * T], start=True, stop=True)
                        last.then_inc(scored[h], 1)

                def turn(h):
                    for u, q in lanes:
                        pe.wait_ge(even_ready[h], q + 1)
                        for s in range(3):
                            for c in range(3):
                                keys = even[:, u, c, :, :].rearrange("p g t -> p (g t)")[:, s * P:(s + 1) * P]
                                last = nc.tensor.transpose(chip.bank(u, s)[:, c * P:(c + 1) * P], keys, ident)
                        last.then_inc(prob_done[h], 1)

                def mixing(h):
                    for u, q in lanes:
                        pe.wait_ge(prob_act[h], 2 * q + 2)
                        pe.wait_ge(prob_dve[h], q + 1)
                        if h == 0:
                            pe.wait_ge(value_ready, q + 1)
                        for pair in range(2):
                            for middle in (False, True):
                                for b in range(2):
                                    v = (value_z if middle else value)[:, u, pair, h * P + b * D:h * P + (b + 1) * D]
                                    probs = prob_t[:, u, 1 if middle else 2 * pair, :].rearrange(
                                        "p (c b t) -> p b c t", c=3, b=2)[:, b, :, :]
                                    last = nc.tensor.matmul(
                                        chip.bank(u, 3)[64 * b:64 * b + 64, pair * T:(pair + 1) * T]
                                        .rearrange("p (c t) -> p c t", c=3), v, probs,
                                        start=(h == 0 and pair == 0 and not middle),
                                        stop=(h == HEADS3 - 1 and middle), skip_group_check=True)
                        last.then_inc(mixed[h], 1)

                score(0)
                for h in heads:
                    turn(h)
                    if h + 1 < HEADS3:
                        score(h + 1)
                    mixing(h)
                for u, q in lanes:
                    pe.wait_ge(mix_ready, q + 1)
                    nc.tensor.matmul(chip.bank(u, 0)[:, 0:QN], op["a3_wo"], mix[:, u, :],
                                     start=True, stop=True).then_inc(left, 1)

            chip.loop(pe, body)

        @block.scalar
        def _(act):
            nc.scalar.preload_act_table_set("natural_log_exp_and_others")
            def body(it):
                lanes = [(u, 2 * it + u) for u in range(2)]
                for u, q in lanes:
                    norm.squares(act, u, q)
                for u, q in lanes:
                    norm.logs(act, u, q)
                for u, q in lanes:
                    norm.powers(act, u, q)
                for u, q in lanes:
                    act.wait_ge(projected, q + 1)
                    nc.scalar.activation(key[:, u, :], chip.bank(u, 2)[:, 0:QN], ACT.Identity,
                                         bias=op["a3_bk"]).then_inc(key_ready, 1)
                for h in heads:
                    for u, q in lanes:
                        act.wait_ge(peak_ready[h], q + 1)
                        for c in range(3):
                            for pair in range(2):
                                last = nc.scalar.activation(prob[:, u, c, pair, :], scores_of(u)[:, c, pair, :], ACT.Exp,
                                                            bias=peak[:, u, c, pair:pair + 1],
                                                            accum_out=total[:, u, c, pair:pair + 1])
                        last.then_inc(exp_ready[h], 1)
                    for u, q in lanes:
                        act.wait_ge(prob_done[h], q + 1)
                        for s in (0, 2):
                            if h:
                                act.wait_ge(mixed[h - 1], q + 1)
                            nc.scalar.activation(prob_t[:, u, s, :], chip.bank(u, s)[:, 0:QN],
                                                 ACT.Copy).then_inc(prob_act[h], 1)
                for u, q in lanes:
                    act.wait_ge(mixed[HEADS3 - 1], q + 1)
                    nc.scalar.activation(mix_b[:, u, :], chip.bank(u, 3)[:, 0:QN], ACT.Copy).then_inc(mix_b_ready, 1)

            chip.loop(act, body)

        @block.vector
        def _(dve):
            def body(it):
                lanes = [(u, 2 * it + u) for u in range(2)]
                for u, q in lanes:
                    norm.scale(dve, u, q, xn[:, u, :])
                for u, q in lanes:
                    dve.wait_ge(projected, q + 1)
                    nc.vector.tensor_scalar(query[:, u, :], chip.bank(u, 1)[:, 0:QN], op["a3_bq"], hd ** -0.5,
                                            ALU.add, ALU.mult).then_inc(query_ready, 1)
                for u, q in lanes:
                    slices = chip.bank(u, 3)[:, 0:QN].rearrange("p (s b h e) -> p s b h e", s=3, b=2, h=HEADS3)
                    bv = op["a3_bv"].rearrange("p (b h e) -> p b h e", b=2, h=HEADS3)
                    for b in range(2):
                        def heads_of(tile):
                            return tile[:, b * D:b * D + HEADS3 * (P + hd)].rearrange(
                                "p (h c) -> p h c", h=HEADS3)[:, :, 0:hd]

                        for n, s in ((0, 0), (1, 2)):
                            nc.vector.tensor_tensor(heads_of(value[:, u, n, :]), slices[:, s, b, :, :], bv[:, b, :, :], ALU.add)
                        for pair in range(2):
                            half = slice(64 * pair, 64 * pair + 64)
                            last = nc.vector.tensor_tensor(heads_of(value_z[half, u, pair, :]), slices[half, 1, b, :, :],
                                                           bv[half, b, :, :], ALU.add)
                    last.then_inc(value_ready, 1)
                for h in heads:
                    for u, q in lanes:
                        dve.wait_ge(scored[h], q + 1)
                        nc.vector.tensor_reduce(peak[:, u, :, :], scores_of(u), X, ALU.max,
                                                negate=True).then_inc(peak_ready[h], 1)
                    for u, q in lanes:
                        dve.wait_ge(exp_ready[h], q + 1)
                        nc.vector.reciprocal(inverse[:, u, :, :], total[:, u, :, :]).then_inc(inverse_ready[h], 1)
                    for u, q in lanes:
                        dve.wait_ge(inverse_ready[h], q + 1)
                        for c in range(3):
                            for pair in range(2):
                                last = nc.vector.tensor_scalar(even[:, u, c, pair, :], prob[:, u, c, pair, :],
                                                               inverse[:, u, c, pair:pair + 1], None, ALU.mult)
                        last.then_inc(even_ready[h], 1)
                    for u, q in lanes:
                        dve.wait_ge(prob_done[h], q + 1)
                        if h:
                            dve.wait_ge(mixed[h - 1], q + 1)
                        nc.vector.tensor_copy(prob_t[:, u, 1, :], chip.bank(u, 1)[:, 0:QN]).then_inc(prob_dve[h], 1)
                for u, q in lanes:
                    dve.wait_ge(mix_b_ready, q + 1)
                    nc.vector.tensor_copy(mix[:, u, :], mix_b[:, u, :]).then_inc(mix_ready, 1)
                for u, q in lanes:
                    dve.wait_ge(left, q + 1)
                    nc.vector.scalar_tensor_tensor(chip.h_quad(q), chip.bank(u, 0)[:, 0:QN], op["a3_bo"],
                                                   chip.h_quad(q), ALU.add, ALU.add).then_inc(h_ready, 1)

            dve.wait_ge(cleared, 2)
            chip.loop(dve, body)

        @block.gpsimd
        def _(pool):
            nc.gpsimd.memset(value[:, :, :, :], 0.0).then_inc(cleared, 1)
            nc.gpsimd.memset(value_z[:, :, :, :], 0.0).then_inc(cleared, 1)

            def body(it):
                lanes = [(u, 2 * it + u) for u in range(2)]
                for u, q in lanes:
                    pool.wait_ge(query_ready, q + 1)
                    if not (isinstance(it, int) and it == 0):
                        pool.wait_ge(scored[HEADS3 - 1], q - 1)
                    pool.sem_inc(pool_passed, 1)
                    for h in heads:
                        for b in range(2):
                            last = nc.gpsimd.tensor_scalar(query_b[:, u, h, :, b, :],
                                                           query[:, u, :].rearrange("p (c t) -> p c t", t=64),
                                                           op["a3_heads"][:, 2 * h + b:2 * h + b + 1], None, ALU.mult)
                    last.then_inc(query_b_ready, 1)

            chip.loop(pool, body)

def experts3(chip):
    nc, op, ident = chip.nc, chip.operand, chip.operand["ident"]
    groups = E3 * F3 // P
    with ExitStack() as ctx:
        def sb(n, shape, dt=F32):
            return ctx.enter_context(nc.sbuf_tensor(f"f3_{n}", shape, dt))

        def sem(n):
            return chip.semaphore(f"f3_{n}")

        norm = Norm(chip, ctx, "f3_norm")
        xn = sb("xn", [P, 2, QN])
        shut = sb("shut", [P, groups * P], BF16)
        scores = sb("scores", [P, 2, 6 * E3])
        rank = sb("rank", [P, 2, 6 * E3])
        equal, ranked = sb("equal", [P, 12, E3]), sb("ranked", [P, 12, E3])
        best, first = sb("best", [P, 12]), sb("first", [P, 12])
        hot = sb("hot", [P, 12, 2 * E3])
        hot_t = sb("hot_t", [P, 2, QN])
        hot_b = sb("hot_b", [P, 2, QN], BF16)
        hid = sb("hid", [P, 2, 2, 2, QN])
        final = sb("final", [P, 2, QN])
        tokens = sb("tokens", [P, 2, 3, 2, D])

        set_up = sem("set_up")
        scored, hot_ready, hot_done = sem("scored"), sem("hot_ready"), sem("hot_done")
        hot_t_ready, hot_b_ready = sem("hot_t_ready"), sem("hot_b_ready")
        steps = [sem(f"step{n}") for n in range(5)]
        hid_done, hid_act, hid_dve, used = (
            [sem(f"{n}{g}") for g in range(groups)] for n in ("hid_done", "hid_act", "hid_dve", "used"))
        final_ready, final_done, tokens_ready = sem("final_ready"), sem("final_done"), sem("tokens_ready")
        stored = [sem(f"stored{u}") for u in range(2)]

        block = ctx.enter_context(nc.Block())

        @block.tensor
        def _(pe):
            pe.wait_ge(set_up, 3)

            def body(it):
                lanes = [(u, 2 * it + u) for u in range(2)]
                for u, q in lanes:
                    if not (isinstance(it, int) and it == 0):
                        pe.wait_ge(tokens_ready, q - 1)
                    norm.centre(u, chip.h_quad(q))
                for u, q in lanes:
                    norm.average(pe, u, q)
                for u, q in lanes:
                    pe.wait_ge(norm.ready, q + 1)
                    for j in range(3):
                        for b in range(2):
                            last = nc.tensor.matmul(chip.bank(u, 2)[:, (2 * j + b) * E3:(2 * j + b + 1) * E3],
                                                    xn[:, u, j * P:(j + 1) * P],
                                                    op["f3_rw"][:, b * D:b * D + E3], start=True, stop=True)
                    last.then_inc(scored, 1)
                for u, q in lanes:
                    pe.wait_ge(hot_ready, it + 1)
                    for j in range(3):
                        last = nc.tensor.transpose(chip.bank(u, 3)[:, j * P:(j + 1) * P],
                                                   hot[:, 6 * u + 2 * j:6 * u + 2 * j + 2, :]
                                                   .rearrange("p g e -> p (g e)"), ident)
                    last.then_inc(hot_done, 1)

                def hidden(g):
                    for u, q in lanes:
                        if g:
                            pe.wait_ge(hid_act[g - 1], q + 1)
                            pe.wait_ge(hid_dve[g - 1], q + 1)
                        for b in range(2):
                            half = slice(64 * b, 64 * b + 64)
                            nc.tensor.matmul(chip.bank(u, b)[:, 0:QN], op["f3_w1"][half, g * P:(g + 1) * P],
                                             xn[half, u, :], start=True, stop=False)
                            last = nc.tensor.matmul(chip.bank(u, b)[:, 0:QN], shut[half, g * P:(g + 1) * P],
                                                    hot_b[half, u, :], start=False, stop=True)
                        last.then_inc(hid_done[g], 1)

                for u, q in lanes:
                    pe.wait_ge(hot_b_ready, q + 1)
                    pe.wait_ge(hot_t_ready, q + 1)
                    nc.tensor.matmul(chip.bank(u, 3)[:, 0:QN], op["f3_b2"], hot_t[:, u, :],
                                     start=True, stop=False, skip_group_check=True)
                hidden(0)
                for g in range(groups):
                    if g + 1 < groups:
                        hidden(g + 1)
                    for u, q in lanes:
                        pe.wait_ge(hid_act[g], q + 1)
                        pe.wait_ge(hid_dve[g], q + 1)
                        for b in range(2):
                            last = nc.tensor.matmul(chip.bank(u, 3)[64 * b:64 * b + 64, 0:QN],
                                                    op["f3_w2"][:, g * D:(g + 1) * D], hid[:, u, g % 2, b, :],
                                                    start=False, stop=(g == groups - 1), skip_group_check=True)
                        last.then_inc(used[g], 1)
                for u, q in lanes:
                    pe.wait_ge(final_ready, q + 1)
                    for j in range(3):
                        last = nc.tensor.transpose(chip.bank(u, 2)[:, j * P:(j + 1) * P],
                                                   final[:, u, j * P:(j + 1) * P], ident)
                    last.then_inc(final_done, 1)

            chip.loop(pe, body)

        @block.scalar
        def _(act):
            nc.scalar.preload_act_table_set("natural_log_exp_and_others")
            def body(it):
                lanes = [(u, 2 * it + u) for u in range(2)]
                for u, q in lanes:
                    norm.squares(act, u, q)
                for u, q in lanes:
                    norm.logs(act, u, q)
                for u, q in lanes:
                    norm.powers(act, u, q)
                for u, q in lanes:
                    act.wait_ge(hot_done, q + 1)
                    nc.scalar.activation(hot_b[:, u, :], chip.bank(u, 3)[:, 0:QN], ACT.Copy).then_inc(hot_b_ready, 1)
                    nc.scalar.activation(hot_t[:, u, :], chip.bank(u, 3)[:, 0:QN], ACT.Copy).then_inc(hot_t_ready, 1)
                for g in range(groups):
                    for u, q in lanes:
                        act.wait_ge(hid_done[g], q + 1)
                        if g >= 2:
                            act.wait_ge(used[g - 2], q + 1)
                        nc.scalar.activation(hid[:, u, g % 2, 0, :], chip.bank(u, 0)[:, 0:QN], ACT.Relu,
                                             bias=op["f3_b1"][:, g:g + 1]).then_inc(hid_act[g], 1)
                for u, q in lanes:
                    act.wait_ge(final_done, q + 1)
                    if not (isinstance(it, int) and it == 0):
                        act.wait_ge(stored[u], 64 * it)
                    nc.scalar.activation(tokens[:, u, :, :, :], chip.bank(u, 2)[:, 0:QN]
                                         .rearrange("p (j b d) -> p j b d", j=3, b=2), ACT.Copy).then_inc(tokens_ready, 1)

            chip.loop(act, body)

        @block.vector
        def _(dve):
            nc.vector.tensor_copy(shut[:, :], op["f3_shut"]).then_inc(set_up, 1)
            nc.vector.memset(hot[:, :, :], 0.0).then_inc(set_up, 1)
            for u in range(2):
                last = nc.vector.tensor_copy(rank[:, u, :], op["f3_rank"])
            last.then_inc(set_up, 1)
            dve.wait_ge(set_up, 3)

            def body(it):
                lanes = [(u, 2 * it + u) for u in range(2)]
                for u, q in lanes:
                    norm.scale(dve, u, q, xn[:, u, :])
                for u, q in lanes:
                    dve.wait_ge(scored, q + 1)
                    last = nc.vector.tensor_tensor(scores[:, u, :], chip.bank(u, 2)[:, 0:6 * E3], op["f3_rb"], ALU.add)
                last.then_inc(steps[0], 1)
                flat = scores[:, :, :].rearrange("p u (g e) -> p (u g) e", e=E3)
                ranks = rank[:, :, :].rearrange("p u (g e) -> p (u g) e", e=E3)
                dve.wait_ge(steps[0], it + 1)
                nc.vector.tensor_reduce(best[:, :], flat, X, ALU.max).then_inc(steps[1], 1)
                dve.wait_ge(steps[1], it + 1)
                nc.vector.tensor_tensor(equal[:, :, :], flat, best[:, :].unsqueeze(2).to_broadcast([P, 12, E3]),
                                        ALU.is_equal).then_inc(steps[2], 1)
                dve.wait_ge(steps[2], it + 1)
                nc.vector.tensor_tensor(ranked[:, :, :], equal[:, :, :], ranks, ALU.mult).then_inc(steps[3], 1)
                dve.wait_ge(steps[3], it + 1)
                nc.vector.tensor_reduce(first[:, :], ranked[:, :, :], X, ALU.max).then_inc(steps[4], 1)
                dve.wait_ge(steps[4], it + 1)
                nc.vector.tensor_tensor(hot[:, :, 0:E3], ranks, first[:, :].unsqueeze(2).to_broadcast([P, 12, E3]),
                                        ALU.is_equal).then_inc(hot_ready, 1)
                for g in range(groups):
                    for u, q in lanes:
                        dve.wait_ge(hid_done[g], q + 1)
                        if g >= 2:
                            dve.wait_ge(used[g - 2], q + 1)
                        nc.vector.tensor_scalar(hid[:, u, g % 2, 1, :], chip.bank(u, 1)[:, 0:QN],
                                                op["f3_b1"][:, g:g + 1], 0.0, ALU.add, ALU.max).then_inc(hid_dve[g], 1)
                for u, q in lanes:
                    dve.wait_ge(used[groups - 1], q + 1)
                    nc.vector.scalar_tensor_tensor(final[:, u, :], chip.bank(u, 3)[:, 0:QN], 0.0, chip.h_quad(q),
                                                   ALU.max, ALU.add).then_inc(final_ready, 1)

            chip.loop(dve, body)

        @block.sync
        def _(sp):
            def body(it):
                lanes = [(u, 2 * it + u) for u in range(2)]
                for u, q in lanes:
                    sp.wait_ge(tokens_ready, q + 1)
                    for chunk, rows, pair, t in ((0, slice(0, 128), 0, 0), (1, slice(0, 64), 0, 128),
                                                 (1, slice(64, 128), 1, 0), (2, slice(0, 128), 1, 64)):
                        n = rows.stop - rows.start
                        out = chip.out[bass.ds(4 * q + 2 * pair, 2), t:t + n, :].rearrange("b t d -> t b d")
                        sp.dma_start(out, tokens[rows, u, chunk, :, :]).then_inc(stored[u], 16)

            chip.loop(sp, body)
            for u in range(2):
                sp.wait_ge(stored[u], 64 * (chip.quads // 2))


def build(nc, images, tokens, neighbours, embed, pack_a, pack_b, pack_c, routes, out, quads=BATCH // 4):
    with ExitStack() as ctx:
        def sb(n, shape, dt=F32):
            return ctx.enter_context(nc.sbuf_tensor(f"{n}_sbuf", shape, dt))

        hidden = sb("hidden", [P, 2 * quads * T])
        eps = sb("eps", [P, 1])
        weights_b = sb("weights_b", [P, columns(PACK_B)[1]])
        psum = ctx.enter_context(nc.psum_tensor("psum", [P, 8, 512], F32))
        chip = Chip(nc, quads, hidden, psum, eps)
        chip.place(PACK_B, weights_b)
        chip.routes = sb("routes", [1, E1 * 4], I32)
        chip.out = out
        loaded = ctx.enter_context(nc.semaphore("loaded"))

        with ExitStack() as first:
            chip.tokens = first.enter_context(nc.sbuf_tensor("tokens_sbuf", [TT, BATCH], I32))
            chip.embed = first.enter_context(nc.sbuf_tensor("embed_sbuf", [32, 32 * D], F32))
            weights_a = first.enter_context(nc.sbuf_tensor("weights_a", [P, columns(PACK_A)[1]], F32))
            chip.place(PACK_A, weights_a)
            with nc.Block() as block:
                @block.vector
                def _(dve):
                    nc.vector.memset(eps[:, :], EPS)

                @block.sync
                def _(sp):
                    sp.dma_start(chip.tokens[:, :], tokens).then_inc(loaded, 16)
                    sp.dma_start(chip.embed[:, :], embed).then_inc(loaded, 16)
                    sp.dma_start(weights_a[:, :], pack_a).then_inc(loaded, 16)
                    sp.dma_start(weights_b[:, :], pack_b).then_inc(loaded, 16)
                    sp.dma_start(chip.routes[:, :], routes).then_inc(loaded, 16)
                    sp.wait_ge(loaded, 80)
            embedding(chip, images, neighbours)
            chip.end_phase()

        attention(chip, "a0", 1.0, D ** -0.5)
        chip.end_phase()
        experts0(chip)
        chip.end_phase()
        linear_attention(chip)
        chip.end_phase()
        weights_c = sb("weights_c", [P, columns(PACK_C)[1]])
        chip.place(PACK_C, weights_c)
        with nc.Block() as block:
            @block.sync
            def _(sp):
                sp.dma_start(weights_c[:, :], pack_c).then_inc(loaded, 16)
                sp.wait_ge(loaded, 96)
        routed(chip)
        chip.end_phase()
        attention(chip, "a2", D ** -0.5, 1.0)
        chip.end_phase()
        experts2(chip)
        chip.end_phase()
        heads_attention(chip)
        chip.end_phase()
        experts3(chip)
        chip.end_phase()



def twice(a):
    out = np.zeros((P,) + a.shape[1:], np.float32)
    out[:a.shape[0]] = a
    out[64:64 + a.shape[0]] = a
    return out


def diagonal(a, rows=64, cols=None):
    cols = a.shape[1] if cols is None else cols
    out = np.zeros((P, 2 * cols), np.float32)
    for b in range(2):
        out[b * rows:b * rows + a.shape[0], b * cols:b * cols + a.shape[1]] = a
    return out


def placed(a):
    out = np.zeros((P, 4, P), np.float32)
    for g in range(2):
        for b in range(2):
            out[64 * g:64 * g + 64, 2 * g + b, 64 * b:64 * b + 64] = a
    return out.reshape(P, 4 * P)


def spread(a, n=6):
    return np.tile(np.asarray(a).reshape(1, -1), (P, n))


def filters():
    def haar(n, sign):
        m = np.zeros((n // 2, n))
        m[np.arange(n // 2), 2 * np.arange(n // 2)] = 0.7071067811865476
        m[np.arange(n // 2), 2 * np.arange(n // 2) + 1] = sign * 0.7071067811865476
        return m

    def resize(n):
        step = n / 8
        at = (np.arange(8)[:, None] + 0.5) * step - 0.5
        w = np.maximum(0, 1 - np.abs(at - np.arange(n)[None, :]) / step)
        return w / w.sum(axis=1, keepdims=True)

    low = haar(IMG, 1)
    return np.stack([resize(56) @ haar(HALF, 1) @ low, resize(56) @ haar(HALF, -1) @ low,
                     resize(112) @ low, resize(112) @ haar(IMG, -1)])


def pack(which, parts):
    where, width = columns(which)
    out = np.zeros((P, width), np.float32)
    for name, (at, n) in where.items():
        a = np.asarray(parts[name])
        a = a.reshape(a.shape[0], -1)
        assert a.shape[1] == n, (name, a.shape, n)
        out[:a.shape[0], at:at + n] = a
    return out


def pack_operands(**w):
    w = {k: np.asarray(v) for k, v in w.items()}
    f = filters().reshape(32, IMG)
    eye = np.eye(P)
    parts = {
        "rows": f.reshape(32, HALF, 2).transpose(1, 2, 0).reshape(HALF, 64),
        "cols": f.reshape(32, 2, HALF).transpose(2, 1, 0).reshape(HALF, 64),
        "tok_b": twice(w["L0_tok_b"][:, None]),
        "taps": np.concatenate([eye * t for t in (0.1, 0.2, 0.4, 0.2, 0.1)], axis=1),
        "ident": eye,
        "centre": diagonal(np.eye(D) - 1 / D),
        "mean": diagonal(np.full((D, D), 1 / D)),
    }
    for n, layer in (("a0", "L0"), ("a2", "L2")):
        parts[f"{n}_wk"] = diagonal(w[f"{layer}_attn_Wk"])
        parts[f"{n}_wq"] = diagonal(w[f"{layer}_attn_Wq"])
        parts[f"{n}_wv"] = placed(w[f"{layer}_attn_Wv"].T)
    parts |= {
        "f0_gate_w": diagonal(w["L0_ffn_gate_w"]), "f0_gate_b": spread(w["L0_ffn_gate_b"]),
        "f0_rank": spread(np.arange(E0, 0, -1)),
        "f0_w1": twice(w["L0_ffn_w1"].transpose(1, 0, 2).reshape(D, -1)),
        "f0_b1": w["L0_ffn_b1"].T,
        "f0_w2": w["L0_ffn_w2"].transpose(1, 0, 2).reshape(F0, -1),
        "f0_b2": np.tile(diagonal(w["L0_ffn_b2"], rows=E0)[0:2 * E0], (3, 1)),
        "f0_pick": np.tile(np.eye(2 * E0).reshape(2 * E0, 2, E0).transpose(0, 2, 1).reshape(2 * E0, -1), (3, 1)),
        "f0_gamma": twice(w["L0_ffn_gamma"][:, None]), "f0_beta": twice(w["L0_ffn_beta"][:, None]),
        "a1_wq": diagonal(w["L1_attn_Wqkv"][:, 0:64]), "a1_wk": diagonal(w["L1_attn_Wqkv"][:, 64:128]),
        "a1_wv": diagonal(w["L1_attn_Wqkv"][:, 128:192]), 
        "a1_wo": np.stack([diagonal(np.tile(w["L1_attn_Wout"][8 * jr:8 * jr + 8], (8, 1))) for jr in range(8)], axis=1),
        "a1_heads": np.kron(np.eye(16), np.ones((8, 8))),
        "a1_head": np.kron(np.ones((2, 1)), np.kron(np.eye(8), np.ones((8, 1)))),
        "a1_bo": twice(w["L1_attn_bout"][:, None]),
        "a1_gamma": twice(w["L1_attn_gamma"][:, None]), "a1_beta": twice(w["L1_attn_beta"][:, None]),
        "f1_wi": twice(w["L1_ffn_Wi"].T), "f1_bi": w["L1_ffn_bi"][:, None],
        "f1_wr": w["L1_ffn_Wr"].transpose(3, 0, 1, 2).reshape(F1, -1),
        "f1_br": w["L1_ffn_br"].transpose(2, 0, 1).reshape(F1, -1),
        "f1_ws": w["L1_ffn_Ws"][:, 0].transpose(2, 0, 1).reshape(F1, -1),
        "f1_bs": w["L1_ffn_bs"][:, 0].T,
        "f1_wo": w["L1_ffn_Wo"].T, "f1_bo": twice(w["L1_ffn_bo"][:, None]),
        "f2_rw1": diagonal(w["L2_ffn_router_w1"]),
        "f2_rb1": np.concatenate([w["L2_ffn_router_b1"]] * 2)[:, None],
        "f2_rw2": diagonal(w["L2_ffn_router_w2"], rows=R2), "f2_rb2": spread(w["L2_ffn_router_b2"]),
        "f2_rank": spread(np.arange(E2, 0, -1)),
        "f2_w1": twice(w["L2_ffn_expert_w1"].transpose(1, 0, 2).reshape(D, -1)),
        "f2_b1": w["L2_ffn_expert_b1"].reshape(3, P).T, "f2_b2": w["L2_ffn_expert_b2"].reshape(3, P).T,
        "f2_b3": diagonal(w["L2_ffn_expert_b3"], rows=E2),
        "a3_wq": diagonal(w["L3_attn_Wq"].T), "a3_bq": twice(w["L3_attn_bq"][:, None]),
        "a3_wk": diagonal(w["L3_attn_Wk"].T), "a3_bk": twice(w["L3_attn_bk"][:, None]),
        "a3_wv": diagonal(w["L3_attn_Wv"].T), "a3_bv": spread(w["L3_attn_bv"], 2),
        "a3_wo": diagonal(w["L3_attn_Wo"].T), "a3_bo": twice(w["L3_attn_bo"][:, None]),
        "a3_heads": np.eye(2 * HEADS3).reshape(2, HEADS3, 2, HEADS3).transpose(0, 1, 3, 2)
        .reshape(2 * HEADS3, 2 * HEADS3).repeat(D // HEADS3, axis=0),
        "f3_rw": diagonal(w["L3_ffn_router_w"].T, cols=64),
        "f3_rb": spread(w["L3_ffn_router_b"]), "f3_rank": spread(np.arange(E3, 0, -1)),
        "f3_w1": twice(w["L3_ffn_W1"].transpose(1, 0, 2).reshape(D, -1)),
        "f3_b1": w["L3_ffn_b1"].reshape(4, P).T,
        "f3_shut": twice(-BIG * (1 - np.kron(np.eye(E3), np.ones((1, F3))))),
        "f3_w2": w["L3_ffn_W2"].reshape(4, P, D).transpose(1, 0, 2).reshape(P, -1),
        "f3_b2": diagonal(w["L3_ffn_b2"]),
    }
    w2 = np.zeros((3, P, P), np.float32)
    w3 = np.zeros((E2, P, D), np.float32)
    for e in range(E2):
        half = slice(64 * (e % 2), 64 * (e % 2) + 64)
        w2[e // 2, half, half] = w["L2_ffn_expert_w2"][e]
        w3[e, half] = w["L2_ffn_expert_w3"][e]
    parts["f2_w2"], parts["f2_w3"] = w2.transpose(1, 0, 2), w3.transpose(1, 0, 2)
    maps = {(0, 0): 0, (1, 0): 1, (0, 1): 2, (1, 1): 3, (3, 2): 4, (2, 3): 5, (3, 3): 6}
    embed = np.zeros((4, 8, 8, 4, D), np.float32)
    for (rt, ct), m in maps.items():
        for cj in range(8):
            embed[ct, cj, cj, rt] = w["L0_tok_W"][m]
    emb = w["L0_txt_emb"]
    near = np.clip(np.arange(VOCAB)[:, None] + np.arange(TAPS) - TAPS // 2, 0, VOCAB - 1)
    return {
        "images": w["x"], "tokens": np.ascontiguousarray(w["x_txt"].T),
        "neighbours": emb[near].reshape(VOCAB, TAPS * D), "embed": embed.reshape(32, -1),
        "pack_a": pack(PACK_A, parts), "pack_b": pack(PACK_B, parts), "pack_c": pack(PACK_C, parts),
        "routes": w["L1_ffn_route_id"].reshape(1, -1),
    }


def kernel(**inputs):
    import concourse.bacc as bacc
    from concourse.bass_utils import run_bass_kernel_spmd as run

    nc = bacc.Bacc("TRN2", target_bir_lowering=False, num_devices=1)
    operands = pack_operands(**inputs)
    names = ("images", "tokens", "neighbours", "embed", "pack_a", "pack_b", "pack_c", "routes")
    arrays = {n: np.ascontiguousarray(operands[n]) for n in names}
    args = [nc.dram_tensor(n, a.shape, mybir.dt.from_np(a.dtype), kind="ExternalInput").ap()
            for n, a in arrays.items()]
    out = nc.dram_tensor("out", (BATCH, T, D), F32, kind="ExternalOutput").ap()
    build(nc, *args, out)
    return run(nc, [arrays], core_ids=[0]).results[0]["out"]
```

```python
from contextlib import ExitStack

import numpy as np

import concourse.bass as bass
from concourse import mybir

F32 = mybir.dt.float32
BF16 = mybir.dt.bfloat16
I32 = mybir.dt.int32
ALU = mybir.AluOpType
ACT = mybir.ActivationFunctionType
X = mybir.AxisListType.X

P = 128
BATCH, T, D = 128, 192, 64
IMG, TI, TT = 224, 64, 128
HALF = IMG // 2
VOCAB, TAPS = 12500, 5
QN = 2 * T
E0, F0 = 16, 128
E1, F1 = 16, 128
E2, R2 = 6, 32
E3, F3 = 32, 16
HEADS3 = 4
BIG = 1e30
EPS = 1e-5

PACK_A = [("rows", 64), ("cols", 64), ("tok_b", 1), ("taps", TAPS * P)]
PACK_B = [("ident", P), ("centre", P), ("mean", P),
          ("a0_wk", P), ("a0_wq", P), ("a0_wv", 4 * P),
          ("f0_gate_w", 2 * E0), ("f0_gate_b", 6 * E0), ("f0_rank", 6 * E0),
          ("f0_w1", E0 * F0), ("f0_b1", E0), ("f0_w2", E0 * D), ("f0_b2", P), ("f0_pick", 2 * E0),
          ("f0_gamma", 1), ("f0_beta", 1),
          ("a1_wq", P), ("a1_wk", P), ("a1_wv", P), ("a1_wo", 8 * P), ("a1_heads", P), ("a1_head", 8),
          ("a1_bo", 1), ("a1_gamma", 1), ("a1_beta", 1)]
PACK_C = [("f1_wi", F1), ("f1_bi", 1), ("f1_wr", 2 * E1 * F1), ("f1_br", 2 * E1),
          ("f1_ws", 2 * F1), ("f1_bs", 2), ("f1_wo", D), ("f1_bo", 1),
          ("a2_wk", P), ("a2_wq", P), ("a2_wv", 4 * P),
          ("f2_rw1", 2 * R2), ("f2_rb1", 1), ("f2_rw2", 2 * E2), ("f2_rb2", 12 * E2), ("f2_rank", 6 * E2),
          ("f2_w1", 3 * P), ("f2_b1", 3), ("f2_w2", 3 * P), ("f2_b2", 3), ("f2_w3", 3 * D), ("f2_b3", P), ("f2_pick", 2 * E2),
          ("a3_wq", P), ("a3_bq", 1), ("a3_wk", P), ("a3_bk", 1), ("a3_wv", P), ("a3_bv", P),
          ("a3_wo", P), ("a3_bo", 1), ("a3_heads", 2 * HEADS3),
          ("f3_rw", 2 * D), ("f3_rb", 6 * E3), ("f3_rank", 6 * E3),
          ("f3_w1", 4 * P), ("f3_b1", 4), ("f3_shut", 4 * P), ("f3_w2", 4 * D), ("f3_b2", P)]


def columns(pack):
    at, where = 0, {}
    for name, n in pack:
        where[name] = (at, n)
        at += n
    return where, at


class Chip:

    def __init__(self, nc, quads, hidden, psum, eps):
        self.nc, self.quads, self.hidden, self.psum, self.eps = nc, quads, hidden, psum, eps
        self.operand = {}
        self.semaphores = []

    def semaphore(self, name):
        self.semaphores.append(self.nc.alloc_semaphore(name))
        return self.semaphores[-1]

    def end_phase(self):
        self.nc.clear_and_free_semaphores(self.semaphores)
        self.nc.all_engine_barrier()
        self.semaphores = []

    def place(self, pack, tile):
        for name, (at, n) in columns(pack)[0].items():
            self.operand[name] = tile[:, at:at + n]

    def bank(self, u, i):
        return self.psum[:, 4 * u + i, :]

    def h_quad(self, q):
        return self.hidden[:, bass.ds(q * QN, QN)]

    def loop(self, eng, body):
        body(0)
        if self.quads > 2:
            with eng.Fori(1, self.quads // 2) as it:
                body(it)


def embedding(chip, images, neighbours):
    nc, op = chip.nc, chip.operand
    group, side = 16, 8

    with ExitStack() as ctx:
        def sb(n, shape, dt=F32):
            return ctx.enter_context(nc.sbuf_tensor(f"emb_{n}", shape, dt))

        def sem(n):
            return chip.semaphore(f"emb_{n}")

        image = sb("image", [HALF, 4, 8, 2 * IMG])
        gathered = sb("gathered", [P, 2, group, TAPS * D])
        by_row = sb("by_row", [HALF, 2, 2, 512])
        maps = sb("maps", [32, 2, group, 4, side])
        index = sb("index", [TT, 2, group], I32)
        indexed, pool_passed = sem("indexed"), sem("pool_passed")
        loaded = [sem(f"loaded_{s}") for s in range(4)]
        fetched = [sem(f"fetched_{u}") for u in range(2)]
        rows_done, by_row_ready, cols_done, maps_ready = sem("rows_done"), sem("by_row_ready"), sem("cols_done"), sem("maps_ready")
        embedded, image_placed = sem("embedded"), sem("image_placed")
        weighed, text_act, text_dve = sem("weighed"), sem("text_act"), sem("text_dve")

        block = ctx.enter_context(nc.Block())

        def first(it):
            return isinstance(it, int) and it == 0

        def loop(eng, body):
            body(0)
            if chip.quads > 8:
                with eng.Fori(1, chip.quads // 8) as it:
                    body(it)

        def pairs_of(k):
            return chip.hidden[:, bass.ds(k * 8 * T, 8 * T)].rearrange("p (g t) -> p g t", t=T)

        def load(eng, it, half):
            for u in range(2):
                k = 2 * it + u
                if not first(it):
                    eng.wait_ge(rows_done, k - 1)
                some = images[bass.ds(k * group + 8 * half, 8), :, :, :]
                eng.dma_start(image[:, 2 * u + half, :, :],
                              some.rearrange("i o (p a) c -> p (i o) (a c)", a=2)).then_inc(loaded[2 * u + half], 16)

        @block.sync
        def _(sp):
            loop(sp, lambda it: load(sp, it, 0))

        @block.gpsimd
        def _(pool):
            def body(it):
                for u in range(2):
                    k = 2 * it + u
                    if not first(it):
                        pool.wait_ge(weighed, 2 * k - 2)
                    pool.sem_inc(pool_passed, 1)
                    nc.gpsimd.tensor_copy(index[:, u, :], chip.tokens[:, bass.ds(k * group, group)]).then_inc(indexed, 1)
                    pool.wait_ge(indexed, k + 1)
                    pool.sem_inc(pool_passed, 1)
                    for j in range(group):
                        nc.gpsimd.indirect_dma_start(
                            gathered[:, u, j, :], None, neighbours,
                            bass.IndirectOffsetOnAxis(ap=index[:, u, j:j + 1], axis=0),
                        ).then_inc(fetched[u], 16)

            loop(pool, body)

        @block.tensor
        def _(pe):
            def body(it):
                lanes = [(u, 2 * it + u) for u in range(2)]
                for u, k in lanes:
                    if not first(it):
                        pe.wait_ge(image_placed, k - 1)
                        pe.wait_ge(text_dve, k - 1)
                    for half in range(2):
                        pe.wait_ge(loaded[2 * u + half], 16 * (it + 1))
                        for ch in range(2):
                            for i in range(8):
                                for a in range(2):
                                    at = (8 * half + i) * 32
                                    last = nc.tensor.matmul(
                                        chip.bank(u, ch)[0:HALF, at:at + 32],
                                        image[:, 2 * u + half, i, a * IMG + ch * HALF:a * IMG + (ch + 1) * HALF],
                                        op["rows"][0:HALF, a * 32:(a + 1) * 32], start=(a == 0), stop=(a == 1))
                    last.then_inc(rows_done, 1)
                for u, k in lanes:
                    pe.wait_ge(by_row_ready, k + 1)
                    for ch in range(2):
                        last = nc.tensor.matmul(chip.bank(u, 2)[0:32, :], op["cols"][0:HALF, ch * 32:(ch + 1) * 32],
                                                by_row[:, u, ch, :], start=(ch == 0), stop=(ch == 1))
                    last.then_inc(cols_done, 1)
                for u, k in lanes:
                    pe.wait_ge(maps_ready, k + 1)
                    for cj in range(side):
                        for rt in range(4):
                            for b in range(2):
                                last = nc.tensor.matmul(
                                    chip.bank(u, 0)[64 * b:64 * b + 64, cj * 64:(cj + 1) * 64],
                                    chip.embed[0:32, (4 * cj + rt) * D:(4 * cj + rt + 1) * D],
                                    maps[:, u, b::2, rt, :], start=(rt == 0), stop=(rt == 3))
                    last.then_inc(embedded, 1)
                for u, k in lanes:
                    pe.wait_ge(fetched[u], 16 * group * (it + 1))
                    for half, bank in ((0, 3), (1, 1)):
                        if half == 0 and not first(it):
                            pe.wait_ge(text_act, k - 1)
                        for g in range(4):
                            for tap in range(TAPS):
                                for b in range(2):
                                    last = nc.tensor.matmul(
                                        chip.bank(u, bank)[64 * b:64 * b + 64, g * TT:(g + 1) * TT],
                                        gathered[:, u, 8 * half + 2 * g + b, tap * D:(tap + 1) * D],
                                        op["taps"][:, tap * P:(tap + 1) * P], start=(tap == 0), stop=(tap == TAPS - 1))
                        last.then_inc(weighed, 1)

            loop(pe, body)

        @block.scalar
        def _(act):
            def body(it):
                lanes = [(u, 2 * it + u) for u in range(2)]
                load(act, it, 1)
                for u, k in lanes:
                    act.wait_ge(rows_done, k + 1)
                    nc.scalar.activation(by_row[:, u, :, :], chip.psum[0:HALF, 4 * u:4 * u + 2, :],
                                         ACT.Copy).then_inc(by_row_ready, 1)
                for u, k in lanes:
                    act.wait_ge(cols_done, k + 1)
                    nc.scalar.activation(maps[:, u, :, :, :].rearrange("p i r c -> p (i r c)"), chip.bank(u, 2)[0:32, :],
                                         ACT.Copy).then_inc(maps_ready, 1)
                for u, k in lanes:
                    act.wait_ge(weighed, 2 * k + 1)
                    nc.scalar.activation(pairs_of(k)[:, 0:4, TI:T],
                                         chip.bank(u, 3).rearrange("p (g t) -> p g t", t=TT),
                                         ACT.Copy).then_inc(text_act, 1)

            loop(act, body)

        @block.vector
        def _(dve):
            def body(it):
                lanes = [(u, 2 * it + u) for u in range(2)]
                for u, k in lanes:
                    dve.wait_ge(embedded, k + 1)
                    nc.vector.tensor_scalar(pairs_of(k)[:, :, 0:TI].rearrange("p g (r c) -> p g c r", c=side),
                                            chip.bank(u, 0).rearrange("p (c g r) -> p g c r", c=side, g=8),
                                            op["tok_b"], None, ALU.add).then_inc(image_placed, 1)
                for u, k in lanes:
                    dve.wait_ge(weighed, 2 * k + 2)
                    nc.vector.tensor_copy(pairs_of(k)[:, 4:8, TI:T],
                                          chip.bank(u, 1).rearrange("p (g t) -> p g t", t=TT)).then_inc(text_dve, 1)

            loop(dve, body)


class Norm:

    def __init__(self, chip, ctx, tag, bank=None):
        nc = chip.nc
        self.chip, self.bank = chip, bank or chip.bank
        self.square = ctx.enter_context(nc.sbuf_tensor(f"{tag}_square", [P, 2, QN], F32))
        self.log = ctx.enter_context(nc.sbuf_tensor(f"{tag}_log", [P, 2, QN], F32))
        self.rstd = ctx.enter_context(nc.sbuf_tensor(f"{tag}_rstd", [P, 2, QN], F32))
        self.centred = chip.semaphore(f"{tag}_centred")
        self.squared = chip.semaphore(f"{tag}_squared")
        self.averaged = chip.semaphore(f"{tag}_averaged")
        self.logged = chip.semaphore(f"{tag}_logged")
        self.rstd_ready = chip.semaphore(f"{tag}_rstd_ready")
        self.ready = chip.semaphore(f"{tag}_ready")

    def centre(self, u, source):
        c = self.chip
        c.nc.tensor.matmul(self.bank(u, 0)[:, 0:QN], c.operand["centre"], source,
                           start=True, stop=True).then_inc(self.centred, 1)

    def squares(self, act, u, q):
        act.wait_ge(self.centred, q + 1)
        self.chip.nc.scalar.activation(self.square[:, u, :], self.bank(u, 0)[:, 0:QN],
                                       ACT.Square).then_inc(self.squared, 1)

    def average(self, pe, u, q):
        c = self.chip
        pe.wait_ge(self.squared, q + 1)
        c.nc.tensor.matmul(self.bank(u, 1)[:, 0:QN], c.operand["mean"], self.square[:, u, :],
                           start=True, stop=True).then_inc(self.averaged, 1)

    def logs(self, act, u, q):
        act.wait_ge(self.averaged, q + 1)
        self.chip.nc.scalar.activation(self.log[:, u, :], self.bank(u, 1)[:, 0:QN], ACT.Ln,
                                       bias=self.chip.eps[:, 0:1]).then_inc(self.logged, 1)

    def powers(self, act, u, q):
        act.wait_ge(self.logged, q + 1)
        self.chip.nc.scalar.activation(self.rstd[:, u, :], self.log[:, u, :], ACT.Exp,
                                       scale=-0.5).then_inc(self.rstd_ready, 1)

    def scale(self, dve, u, q, out):
        dve.wait_ge(self.rstd_ready, q + 1)
        self.chip.nc.vector.tensor_tensor(out, self.bank(u, 0)[:, 0:QN], self.rstd[:, u, :],
                                          ALU.mult).then_inc(self.ready, 1)


def attention(chip, name, score_scale, value_scale):
    nc, op, ident = chip.nc, chip.operand, chip.operand["ident"]
    with ExitStack() as ctx:
        def sb(n, shape, dt=F32):
            return ctx.enter_context(nc.sbuf_tensor(f"{name}_{n}", shape, dt))

        def sem(n):
            return chip.semaphore(f"{name}_{n}")

        norm = Norm(chip, ctx, f"{name}_norm")
        m_t = sb("m_t", [P, P])
        xn = sb("xn", [P, 2, QN])
        xb = sb("xb", [P, 2, 6, 2, 64])
        ym = sb("ym", [P, 2, QN])
        xt = sb("xt", [P, 2, 2, P])
        xz = sb("xz", [P, 2, 2, P])
        peak = sb("peak", [P, 2, 6])
        total = sb("total", [P, 2, 6])
        inverse = sb("inverse", [P, 2, 6])
        prob = sb("prob", [P, 2, 3, 2, T])
        prob_t = sb("prob_t", [P, 2, 3, QN])
        mix = sb("mix", [P, 2, 3, 2, 64])
        mix_t = sb("mix_t", [P, 2, 2, 3, 64])

        m_done, m_ready = sem("m_done"), sem("m_ready")
        cleared, pool_passed = sem("cleared"), sem("pool_passed")
        xb_ready, ym_done, ym_ready = sem("xb_ready"), sem("ym_done"), sem("ym_ready")
        xt_done, xt_ready, xz_ready = sem("xt_done"), sem("xt_ready"), sem("xz_ready")
        scored, peak_ready, exp_ready = sem("scored"), sem("peak_ready"), sem("exp_ready")
        inverse_ready = sem("inverse_ready")
        prob_done, prob_act, prob_dve = sem("prob_done"), sem("prob_act"), sem("prob_dve")
        mixed, mix_ready, mix_done, mix_t_ready = sem("mixed"), sem("mix_ready"), sem("mix_done"), sem("mix_t_ready")
        valued, h_ready = sem("valued"), sem("h_ready")

        def scores_of(u, pair):
            two = chip.psum[:, 4 * u + 2 * pair:4 * u + 2 * pair + 2, :]
            return two.rearrange("p b (c n) -> p (b c) n", n=256)[:, 0:3, 0:T]

        block = ctx.enter_context(nc.Block())

        @block.tensor
        def _(pe):
            nc.tensor.matmul(chip.bank(0, 3)[:, 0:P], op[f"{name}_wk"], op[f"{name}_wq"],
                             start=True, stop=True).then_inc(m_done, 1)
            pe.wait_ge(m_ready, 1)
            pe.wait_ge(cleared, 2)

            def body(it):
                lanes = [(u, 2 * it + u) for u in range(2)]
                for u, q in lanes:
                    if not (isinstance(it, int) and it == 0):
                        pe.wait_ge(h_ready, q - 1)
                    norm.centre(u, chip.h_quad(q))
                for u, q in lanes:
                    norm.average(pe, u, q)
                for u, q in lanes:
                    pe.wait_ge(norm.ready, q + 1)
                    nc.tensor.matmul(chip.bank(u, 1)[:, 0:QN], m_t[:, :], xn[:, u, :],
                                     start=True, stop=True).then_inc(ym_done, 1)
                    for s, out in ((0, chip.bank(u, 2)[:, 0:P]), (2, chip.bank(u, 2)[:, P:2 * P]),
                                   (1, chip.bank(u, 3)[:, 0:P])):
                        last = nc.tensor.transpose(out, xn[:, u, s * P:(s + 1) * P], ident)
                    last.then_inc(xt_done, 1)
                for u, q in lanes:
                    pe.wait_ge(xb_ready, q + 1)
                    pe.wait_ge(ym_ready, q + 1)
                    pe.wait_ge(xt_ready, q + 1)
                    pe.wait_ge(xz_ready, q + 1)
                    for pair in range(2):
                        for c in range(3):
                            last = nc.tensor.matmul(scores_of(u, pair)[:, c, :],
                                                    xb[:, u, 3 * pair + c, :, :].rearrange("p b t -> p (b t)"),
                                                    ym[:, u, pair * T:(pair + 1) * T], start=True, stop=True)
                        last.then_inc(scored, 1)
                for u, q in lanes:
                    pe.wait_ge(exp_ready, 2 * q + 2)
                    for s in range(3):
                        for c in range(3):
                            keys = prob[:, u, c, :, :].rearrange("p g t -> p (g t)")[:, s * P:(s + 1) * P]
                            last = nc.tensor.transpose(chip.bank(u, s)[:, c * P:(c + 1) * P], keys, ident)
                        last.then_inc(prob_done, 1)
                for u, q in lanes:
                    pe.wait_ge(prob_act, 2 * q + 2)
                    pe.wait_ge(prob_dve, q + 1)
                    for pair in range(2):
                        for c in range(3):
                            out = chip.bank(u, 3 if pair else 0)[:, c * P:(c + 1) * P]
                            nc.tensor.matmul(out, prob_t[:, u, 2 * pair, c * P:(c + 1) * P], xt[:, u, pair, :],
                                             start=True, stop=False)
                            last = nc.tensor.matmul(out, prob_t[:, u, 1, c * P:(c + 1) * P], xz[:, u, pair, :],
                                                    start=False, stop=True)
                    last.then_inc(mixed, 1)
                for u, q in lanes:
                    pe.wait_ge(mix_ready, q + 1)
                    for c in range(3):
                        last = nc.tensor.transpose(chip.bank(u, 1)[:, c * P:(c + 1) * P],
                                                   mix[:, u, c, :, :].rearrange("p g d -> p (g d)"), ident)
                    last.then_inc(mix_done, 1)
                for u, q in lanes:
                    pe.wait_ge(mix_t_ready, q + 1)
                    for pair in range(2):
                        for b in range(2):
                            wv = op[f"{name}_wv"][:, (2 * pair + b) * P:(2 * pair + b + 1) * P]
                            last = nc.tensor.matmul(chip.bank(u, 2)[:, pair * T:(pair + 1) * T], wv,
                                                    mix_t[:, u, b, :, :].rearrange("p c t -> p (c t)"),
                                                    start=(b == 0), stop=(b == 1))
                    last.then_inc(valued, 1)

            chip.loop(pe, body)

        @block.scalar
        def _(act):
            nc.scalar.preload_act_table_set("natural_log_exp_and_others")
            act.wait_ge(m_done, 1)
            nc.scalar.activation(m_t[:, :], chip.bank(0, 3)[:, 0:P], ACT.Copy,
                                 scale=score_scale).then_inc(m_ready, 1)

            def body(it):
                lanes = [(u, 2 * it + u) for u in range(2)]
                for u, q in lanes:
                    norm.squares(act, u, q)
                for u, q in lanes:
                    norm.logs(act, u, q)
                for u, q in lanes:
                    norm.powers(act, u, q)
                for u, q in lanes:
                    act.wait_ge(ym_done, q + 1)
                    nc.scalar.activation(ym[:, u, :], chip.bank(u, 1)[:, 0:QN], ACT.Copy).then_inc(ym_ready, 1)
                    act.wait_ge(xt_done, q + 1)
                    nc.scalar.activation(xt[:, u, :, :], chip.bank(u, 2)[:, 0:2 * P].rearrange("p (g d) -> p g d", g=2),
                                         ACT.Copy).then_inc(xt_ready, 1)
                for u, q in lanes:
                    for pair in range(2):
                        act.wait_ge(peak_ready, 2 * q + pair + 1)
                        for c in range(3):
                            last = nc.scalar.activation(prob[:, u, c, pair, :], scores_of(u, pair)[:, c, :], ACT.Exp,
                                                        bias=peak[:, u, 3 * pair + c:3 * pair + c + 1],
                                                        accum_out=total[:, u, 3 * pair + c:3 * pair + c + 1])
                        last.then_inc(exp_ready, 1)
                for u, q in lanes:
                    for s in (0, 2):
                        act.wait_ge(prob_done, 3 * q + s + 1)
                        nc.scalar.activation(prob_t[:, u, s, :], chip.bank(u, s)[:, 0:QN],
                                             ACT.Copy).then_inc(prob_act, 1)
                for u, q in lanes:
                    act.wait_ge(mix_done, q + 1)
                    nc.scalar.activation(mix_t[:, u, :, :, :].rearrange("p b c t -> p c b t"),
                                         chip.bank(u, 1)[:, 0:QN].rearrange("p (c b t) -> p c b t", c=3, b=2),
                                         ACT.Copy).then_inc(mix_t_ready, 1)

            chip.loop(act, body)

        @block.vector
        def _(dve):
            def body(it):
                lanes = [(u, 2 * it + u) for u in range(2)]
                for u, q in lanes:
                    norm.scale(dve, u, q, xn[:, u, :])
                for u, q in lanes:
                    dve.wait_ge(xt_done, q + 1)
                    for pair in range(2):
                        half = slice(64 * pair, 64 * pair + 64)
                        last = nc.vector.tensor_copy(xz[half, u, pair, :], chip.bank(u, 3)[half, 0:P])
                    last.then_inc(xz_ready, 1)
                for u, q in lanes:
                    for pair in range(2):
                        dve.wait_ge(scored, 2 * q + pair + 1)
                        nc.vector.tensor_reduce(peak[:, u, 3 * pair:3 * pair + 3], scores_of(u, pair), X, ALU.max,
                                                negate=True).then_inc(peak_ready, 1)
                for u, q in lanes:
                    dve.wait_ge(exp_ready, 2 * q + 2)
                    nc.vector.reciprocal(inverse[:, u, :], total[:, u, :]).then_inc(inverse_ready, 1)
                for u, q in lanes:
                    dve.wait_ge(prob_done, 3 * q + 2)
                    nc.vector.tensor_copy(prob_t[:, u, 1, :], chip.bank(u, 1)[:, 0:QN]).then_inc(prob_dve, 1)
                for u, q in lanes:
                    dve.wait_ge(mixed, q + 1)
                    dve.wait_ge(inverse_ready, q + 1)
                    for b in range(2):
                        half = slice(64 * b, 64 * b + 64)
                        for pair in range(2):
                            out = chip.bank(u, 3 if pair else 0)[half, 0:QN].rearrange("p (c b d) -> p c b d", c=3, b=2)
                            last = nc.vector.tensor_tensor(
                                mix[half, u, :, pair, :], out[:, :, b, :],
                                inverse[half, u, 3 * pair:3 * pair + 3].unsqueeze(2).to_broadcast([64, 3, 64]), ALU.mult)
                    last.then_inc(mix_ready, 1)
                for u, q in lanes:
                    dve.wait_ge(valued, q + 1)
                    nc.vector.scalar_tensor_tensor(chip.h_quad(q), chip.bank(u, 2)[:, 0:QN], value_scale,
                                                   chip.h_quad(q), ALU.mult, ALU.add).then_inc(h_ready, 1)

            chip.loop(dve, body)

        @block.gpsimd
        def _(pool):
            nc.gpsimd.memset(xb[:, :, :, :, :], 0.0).then_inc(cleared, 1)
            nc.gpsimd.memset(xz[:, :, :, :], 0.0).then_inc(cleared, 1)

            def body(it):
                lanes = [(u, 2 * it + u) for u in range(2)]
                for u, q in lanes:
                    pool.wait_ge(norm.ready, q + 1)
                    if not (isinstance(it, int) and it == 0):
                        pool.wait_ge(scored, 2 * q - 2)
                    pool.wait_ge(cleared, 2)
                    pool.sem_inc(pool_passed, 1)
                    for b in range(2):
                        half = slice(64 * b, 64 * b + 64)
                        last = nc.gpsimd.tensor_copy(xb[half, u, :, b, :],
                                                     xn[half, u, :].rearrange("p (c t) -> p c t", t=64))
                    last.then_inc(xb_ready, 1)

            chip.loop(pool, body)



def top_two(chip, dve, step, wait, scores, rank, experts, w, groups=12):
    nc = chip.nc

    def wide(a):
        return a.unsqueeze(2).to_broadcast([P, groups, experts])

    source = scores
    for n, (best, hot) in enumerate(((w["best1"], w["hot1"]), (w["best2"], w["hot2"]))):
        step(nc.vector.tensor_reduce(best[:, :], source, X, ALU.max))
        wait()
        step(nc.vector.tensor_tensor(w["equal"][:, :, :], source, wide(best[:, :]), ALU.is_equal))
        wait()
        step(nc.vector.tensor_tensor(w["ranked"][:, :, :], w["equal"][:, :, :], rank, ALU.mult))
        wait()
        step(nc.vector.tensor_reduce(w["first"][:, :], w["ranked"][:, :, :], X, ALU.max))
        wait()
        step(nc.vector.tensor_tensor(hot[:, :, :], rank, wide(w["first"][:, :]), ALU.is_equal))
        wait()
        if n == 0:
            step(nc.vector.scalar_tensor_tensor(w["rest"][:, :, :], hot[:, :, :], -3e38, source, ALU.mult, ALU.add))
            wait()
            source = w["rest"][:, :, :]


def gates_of_two(chip, dve, step, wait, experts, w, gap_ready, ratio_ready, gates_ready, it, groups=12):
    nc = chip.nc

    def wide(a):
        return a[:, :].unsqueeze(2).to_broadcast([P, groups, experts])

    nc.vector.tensor_tensor(w["gap"][:, :], w["best2"][:, :], w["best1"][:, :], ALU.subtract).then_inc(gap_ready, 1)
    dve.wait_ge(ratio_ready, it + 1)
    step(nc.vector.tensor_scalar(w["whole"][:, :], w["ratio"][:, :], 1.0, None, ALU.add))
    wait()
    step(nc.vector.reciprocal(w["w1"][:, :], w["whole"][:, :]))
    wait()
    step(nc.vector.tensor_tensor(w["w2"][:, :], w["ratio"][:, :], w["w1"][:, :], ALU.mult))
    wait()
    step(nc.vector.tensor_tensor(w["gate1"][:, :, :], w["hot1"][:, :, :], wide(w["w1"]), ALU.mult))
    wait()
    step(nc.vector.tensor_tensor(w["ranked"][:, :, :], w["hot2"][:, :, :], wide(w["w2"]), ALU.mult))
    wait()
    nc.vector.tensor_tensor(w["gate"][:, :, :], w["gate1"][:, :, :], w["ranked"][:, :, :],
                            ALU.add).then_inc(gates_ready, 1)
    dve.wait_ge(gates_ready, it + 1)


def experts0(chip):
    nc, op = chip.nc, chip.operand
    with ExitStack() as ctx:
        def sb(n, shape, dt=F32):
            return ctx.enter_context(nc.sbuf_tensor(f"f0_{n}", shape, dt))

        def sem(n):
            return chip.semaphore(f"f0_{n}")

        rows = 3 * 2 * E0
        norm = Norm(chip, ctx, "f0_norm", lambda u, i: chip.psum[:, 6 + i, :])
        post = Norm(chip, ctx, "f0_post", lambda u, i: chip.psum[:, 6 + i, :])
        xn = sb("xn", [P, 2, QN])
        y = sb("y", [P, 2, QN])
        yn = sb("yn", [P, 2, QN])
        yg = sb("yg", [P, 2, QN])
        scores = sb("scores", [P, 6, E0])
        work = {n: sb(n, [P, 6, E0]) for n in ("equal", "ranked", "rest", "hot1", "hot2", "gate1", "gate")}
        work |= {n: sb(n, [P, 6]) for n in ("best1", "best2", "first", "gap", "ratio", "whole", "w1", "w2")}
        remains = sb("remains", [P, 2, 3, 2 * E0])
        parts = sb("parts", [P, 3, 3, 2 * E0], BF16)
        parts_t = sb("parts_t", [rows, 2, QN], BF16)
        parts_t32 = sb("parts_t32", [rows, 2, QN])
        ident_b = sb("ident_b", [P, P], BF16)
        pick = sb("pick", [rows, E0, 2, D], BF16)
        hid = sb("hid", [P, 2, 2, QN])
        spread = sb("spread", [P, 2, QN])
        share = sb("share", [P, 2, QN])

        set_up, scored = sem("set_up"), sem("scored")
        steps = [sem(f"step{n}") for n in range(23)]
        gap_ready, ratio_ready = sem("gap_ready"), sem("ratio_ready")
        gates_ready, parts_ready, parts_done, parts_t_ready = (
            sem("gates_ready"), sem("parts_ready"), sem("parts_done"), sem("parts_t_ready"))
        base_done, base_ready = sem("base_done"), sem("base_ready")
        hid_done = [sem(f"hid_done{e}") for e in range(E0)]
        hid_ready = [sem(f"hid_ready{e}") for e in range(E0)]
        expert_done = [sem(f"expert_done{e}") for e in range(E0)]
        share_ready = [sem(f"share_ready{e}") for e in range(E0)]
        spread_done = [sem(f"spread_done{e}") for e in range(E0)]
        spread_ready = [sem(f"spread_ready{e}") for e in range(E0)]
        added = sem("added")
        yg_ready, h_ready = sem("yg_ready"), sem("h_ready")

        def at_start(q):
            return isinstance(q, int) and q == 0

        def loop(eng, quad):
            def both(it, last):
                for u in range(2):
                    quad(u, 2 * it + u, not (last and u == 1))

            pairs = chip.quads // 2
            both(0, pairs == 1)
            if pairs > 2:
                with eng.Fori(1, pairs - 1) as it:
                    both(it, False)
            if pairs > 1:
                both(pairs - 1, True)

        block = ctx.enter_context(nc.Block())

        @block.tensor
        def _(pe):
            def score(u, q):
                pe.wait_ge(norm.ready, q + 1)
                for j in range(3):
                    last = nc.tensor.matmul(chip.psum[:, 7, 2 * E0 * j:2 * E0 * (j + 1)],
                                            xn[:, u, j * P:(j + 1) * P], op["f0_gate_w"], start=True, stop=True)
                last.then_inc(scored, 1)

            def turn_gates(q):
                pe.wait_ge(parts_ready, q + 1)
                for j in range(3):
                    last = nc.tensor.matmul(chip.psum[0:rows, 6, j * P:(j + 1) * P],
                                            parts[:, j, :, :].rearrange("p a e -> p (a e)"), ident_b[:, :],
                                            start=True, stop=True)
                last.then_inc(parts_done, 1)

            def hidden(u, q, e):
                if e >= 2:
                    pe.wait_ge(hid_ready[e - 2], q + 1)
                elif not at_start(q):
                    pe.wait_ge(hid_ready[E0 - 2 + e], q)
                for b in range(2):
                    half = slice(64 * b, 64 * b + 64)
                    last = nc.tensor.matmul(chip.psum[:, 2 * (e % 2) + b, 0:QN], op["f0_w1"][half, e * F0:(e + 1) * F0],
                                            xn[half, u, :], start=True, stop=True)
                last.then_inc(hid_done[e], 1)

            def base(u, q):
                pe.wait_ge(parts_t_ready, 2 * q + 2)
                if not at_start(q):
                    pe.wait_ge(share_ready[E0 - 1], q)
                nc.tensor.matmul(chip.psum[:, 4, 0:QN], op["f0_b2"][0:rows, :], parts_t32[:, u, :],
                                 start=True, stop=True).then_inc(base_done, 1)

            def output(u, q, e):
                if e:
                    pe.wait_ge(share_ready[e - 1], q + 1)
                else:
                    pe.wait_ge(base_ready, q + 1)
                pe.wait_ge(hid_ready[e], q + 1)
                for b in range(2):
                    last = nc.tensor.matmul(chip.psum[64 * b:64 * b + 64, 4, 0:QN], op["f0_w2"][:, e * D:(e + 1) * D],
                                            hid[:, e % 2, b, :], start=True, stop=True)
                last.then_inc(expert_done[e], 1)

            def spread_gates(u, q, e):
                if e:
                    pe.wait_ge(spread_ready[e - 1], q + 1)
                elif not at_start(q):
                    pe.wait_ge(spread_ready[E0 - 1], q)
                nc.tensor.matmul(chip.psum[:, 5, 0:QN], pick[:, e, :, :].rearrange("p b d -> p (b d)"),
                                 parts_t[:, u, :], start=True, stop=True).then_inc(spread_done[e], 1)

            def quad(u, q, more):
                for e in range(E0):
                    hidden(u, q, e)
                    if e == 0:
                        base(u, q)
                    spread_gates(u, q, e)
                    if e == 1 and not at_start(q):
                        pe.wait_ge(added, E0 * q)
                        post.centre(1 - u, y[:, 1 - u, :])
                    if e == 2 and not at_start(q):
                        post.average(pe, 1 - u, q - 1)
                    if e == 5 and more:
                        if not at_start(q):
                            pe.wait_ge(post.ready, q)
                        norm.centre(1 - u, chip.h_quad(q + 1))
                    if e == 6 and more:
                        norm.average(pe, 1 - u, q + 1)
                    if e == 8 and more:
                        score(1 - u, q + 1)
                    if e:
                        output(u, q, e - 1)
                if more:
                    turn_gates(q + 1)
                output(u, q, E0 - 1)

            pe.wait_ge(set_up, 2)
            norm.centre(0, chip.h_quad(0))
            norm.average(pe, 0, 0)
            score(0, 0)
            turn_gates(0)
            loop(pe, quad)
            pe.wait_ge(added, E0 * chip.quads)
            post.centre(1, y[:, 1, :])
            post.average(pe, 1, chip.quads - 1)

        @block.scalar
        def _(act):
            nc.scalar.preload_act_table_set("natural_log_exp_and_others")
            def exponentiate(q):
                act.wait_ge(gap_ready, q + 1)
                nc.scalar.activation(work["ratio"][:, :], work["gap"][:, :], ACT.Exp).then_inc(ratio_ready, 1)

            def keep_gates(u, q):
                act.wait_ge(parts_done, q + 1)
                for copy in (parts_t, parts_t32):
                    nc.scalar.activation(copy[:, u, :], chip.psum[0:rows, 6, 0:QN], ACT.Copy).then_inc(parts_t_ready, 1)

            def quad(u, q, more):
                for e in range(E0):
                    act.wait_ge(hid_done[e], q + 1)
                    if e >= 2:
                        act.wait_ge(expert_done[e - 2], q + 1)
                    elif not at_start(q):
                        act.wait_ge(expert_done[E0 - 2 + e], q)
                    for b in range(2):
                        last = nc.scalar.activation(hid[:, e % 2, b, :], chip.psum[:, 2 * (e % 2) + b, 0:QN], ACT.Relu,
                                                    bias=op["f0_b1"][:, e:e + 1])
                    last.then_inc(hid_ready[e], 1)
                    if e == 1 and not at_start(q):
                        post.squares(act, 1 - u, q - 1)
                    if e == 3 and not at_start(q):
                        post.logs(act, 1 - u, q - 1)
                        post.powers(act, 1 - u, q - 1)
                    if e == 5 and more:
                        norm.squares(act, 1 - u, q + 1)
                    if e == 6 and more:
                        norm.logs(act, 1 - u, q + 1)
                        norm.powers(act, 1 - u, q + 1)
                    if e == 11 and more:
                        exponentiate(q + 1)
                if more:
                    keep_gates(1 - u, q + 1)

            norm.squares(act, 0, 0)
            norm.logs(act, 0, 0)
            norm.powers(act, 0, 0)
            exponentiate(0)
            keep_gates(0, 0)
            loop(act, quad)
            post.squares(act, 1, chip.quads - 1)
            post.logs(act, 1, chip.quads - 1)
            post.powers(act, 1, chip.quads - 1)

        @block.vector
        def _(dve):
            nc.vector.tensor_copy(ident_b[:, :], op["ident"]).then_inc(set_up, 1)
            nc.vector.tensor_copy(pick[:, :, :, :].rearrange("p e b d -> p (e b) d"),
                                  op["f0_pick"][0:rows, :].unsqueeze(2).to_broadcast([rows, 2 * E0, D])
                                  ).then_inc(set_up, 1)

            def gates(q, between):
                link = [0]

                def step(instruction):
                    instruction.then_inc(steps[link[0]], 1)

                def wait():
                    dve.wait_ge(steps[link[0]], q + 1)
                    link[0] += 1
                    if link[0] % 5 == 0:
                        between()

                dve.wait_ge(scored, q + 1)
                flat = scores[:, :, :]
                step(nc.vector.tensor_tensor(flat.rearrange("p g e -> p (g e)"), chip.psum[:, 7, 0:6 * E0],
                                             op["f0_gate_b"], ALU.add))
                wait()
                top_two(chip, dve, step, wait, flat, op["f0_rank"].rearrange("p (g e) -> p g e", e=E0), E0, work, 6)
                gates_of_two(chip, dve, step, wait, E0, work, gap_ready, ratio_ready, gates_ready, q, 6)
                gate = work["gate"][:, :, :].rearrange("p (j b) e -> p j (b e)", b=2)
                if not at_start(q):
                    dve.wait_ge(parts_done, q)
                step(nc.vector.tensor_copy(parts[:, :, 0, :], gate))
                wait()
                step(nc.vector.tensor_tensor(remains[:, 0, :, :], gate, parts[:, :, 0, :], ALU.subtract))
                wait()
                step(nc.vector.tensor_copy(parts[:, :, 1, :], remains[:, 0, :, :]))
                wait()
                nc.vector.tensor_tensor(parts[:, :, 2, :], remains[:, 0, :, :], parts[:, :, 1, :],
                                        ALU.subtract).then_inc(parts_ready, 1)

            def finish(u, q):
                yield post.scale(dve, u, q, yn[:, u, :])
                dve.wait_ge(post.ready, q + 1)
                yield nc.vector.tensor_scalar(yg[:, u, :], yn[:, u, :], op["f0_gamma"], op["f0_beta"],
                                              ALU.mult, ALU.add).then_inc(yg_ready, 1)
                dve.wait_ge(yg_ready, q + 1)
                yield nc.vector.tensor_tensor(chip.h_quad(q), chip.h_quad(q), yg[:, u, :], ALU.add)

            def quad(u, q, more):
                at = [0]

                def copy_gates(e):
                    dve.wait_ge(spread_done[e], q + 1)
                    nc.vector.tensor_copy(spread[:, e % 2, :], chip.psum[:, 5, 0:QN]).then_inc(spread_ready[e], 1)

                def share_of_next_expert():
                    e = at[0]
                    at[0] += 1
                    dve.wait_ge(expert_done[e], q + 1)
                    dve.wait_ge(spread_ready[e], q + 1)
                    if e >= 2 or not at_start(q):
                        dve.wait_ge(added, E0 * q + e - 1)
                    nc.vector.tensor_tensor(share[:, e % 2, :], chip.psum[:, 4, 0:QN], spread[:, e % 2, :],
                                            ALU.mult).then_inc(share_ready[e], 1)
                    if e + 1 < E0:
                        copy_gates(e + 1)

                dve.wait_ge(base_done, q + 1)
                nc.vector.tensor_tensor(y[:, u, :], chip.psum[:, 4, 0:QN], xn[:, u, :], ALU.add).then_inc(base_ready, 1)
                copy_gates(0)
                closing = iter(()) if at_start(q) else finish(1 - u, q - 1)
                while at[0] < 8:
                    share_of_next_expert()
                    if at[0] >= 4:
                        next(closing, None)
                    if at[0] == 7 and more:
                        norm.scale(dve, 1 - u, q + 1, xn[:, 1 - u, :])
                if more:
                    gates(q + 1, share_of_next_expert)
                while at[0] < E0:
                    share_of_next_expert()

            norm.scale(dve, 0, 0, xn[:, 0, :])
            gates(0, lambda: None)
            loop(dve, quad)
            for _ in finish(1, chip.quads - 1):
                pass

        @block.gpsimd
        def _(pool):
            def quad(u, q, more):
                pool.wait_ge(base_ready, q + 1)
                for e in range(E0):
                    if e:
                        pool.wait_ge(added, E0 * q + e)
                    pool.wait_ge(share_ready[e], q + 1)
                    nc.gpsimd.tensor_tensor(y[:, u, :], y[:, u, :], share[:, e % 2, :], ALU.add).then_inc(added, 1)

            loop(pool, quad)


def linear_attention(chip):
    nc, op, ident = chip.nc, chip.operand, chip.operand["ident"]
    with ExitStack() as ctx:
        def sb(n, shape, dt=F32):
            return ctx.enter_context(nc.sbuf_tensor(f"a1_{n}", shape, dt))

        def sem(n):
            return chip.semaphore(f"a1_{n}")

        norm = Norm(chip, ctx, "a1_norm")
        post = Norm(chip, ctx, "a1_post")
        xn = sb("xn", [P, 2, QN])
        value = sb("value", [P, 2, QN])
        query = sb("query", [P, 2, 3, P])
        peak = sb("peak", [P, 2, 2])
        total = sb("total", [P, 2, 2])
        inverse = sb("inverse", [P, 2, 2])
        key = sb("key", [P, 2, QN])
        key_t = sb("key_t", [P, 2, 2, P])
        key_z = sb("key_z", [P, 2, 2, P])
        outer = sb("outer", [P, 2, 2, P])
        o = sb("o", [P, 2, QN])
        spread_o = sb("spread", [P, 2, 2, 8, T])
        y = sb("y", [P, 2, QN])
        yn = sb("yn", [P, 2, QN])
        yg = sb("yg", [P, 2, QN])

        cleared = sem("cleared")
        projected, value_ready, query_ready = sem("projected"), sem("value_ready"), sem("query_ready")
        peak_ready, key_ready, inverse_ready = sem("peak_ready"), sem("key_ready"), sem("inverse_ready")
        key_done, key_t_ready, key_z_ready = sem("key_done"), sem("key_t_ready"), sem("key_z_ready")
        outer_done, outer_ready = sem("outer_done"), sem("outer_ready")
        o_done, o_ready, spread_ready = sem("o_done"), sem("o_ready"), sem("spread_ready")
        mixed, y_ready, yg_ready = sem("mixed"), sem("y_ready"), sem("yg_ready")

        block = ctx.enter_context(nc.Block())

        @block.tensor
        def _(pe):
            pe.wait_ge(cleared, 1)

            def body(it):
                lanes = [(u, 2 * it + u) for u in range(2)]
                for u, q in lanes:
                    if not (isinstance(it, int) and it == 0):
                        pe.wait_ge(post.ready, q - 1)
                    norm.centre(u, chip.h_quad(q))
                for u, q in lanes:
                    norm.average(pe, u, q)
                for u, q in lanes:
                    pe.wait_ge(norm.ready, q + 1)
                    nc.tensor.matmul(chip.bank(u, 1)[:, 0:QN], op["a1_wk"], xn[:, u, :], start=True, stop=True)
                    nc.tensor.matmul(chip.bank(u, 2)[:, 0:QN], op["a1_wv"], xn[:, u, :], start=True, stop=True)
                    for j in range(3):
                        last = nc.tensor.matmul(chip.bank(u, 3)[:, j * P:(j + 1) * P], xn[:, u, j * P:(j + 1) * P],
                                                op["a1_wq"], start=True, stop=True)
                    last.then_inc(projected, 1)
                for u, q in lanes:
                    pe.wait_ge(key_ready, q + 1)
                    pe.wait_ge(value_ready, q + 1)
                    for s, out in ((0, chip.bank(u, 0)[:, 0:P]), (2, chip.bank(u, 0)[:, P:2 * P]),
                                   (1, chip.bank(u, 2)[:, 0:P])):
                        last = nc.tensor.transpose(out, key[:, u, s * P:(s + 1) * P], ident)
                    last.then_inc(key_done, 1)
                for u, q in lanes:
                    pe.wait_ge(key_t_ready, q + 1)
                    pe.wait_ge(key_z_ready, q + 1)
                    pe.wait_ge(query_ready, q + 1)
                    for pair in range(2):
                        out = chip.bank(u, 1)[:, pair * P:(pair + 1) * P]
                        nc.tensor.matmul(out, key_t[:, u, pair, :], query[:, u, 2 * pair, :], start=True, stop=False)
                        last = nc.tensor.matmul(out, key_z[:, u, pair, :], query[:, u, 1, :], start=False, stop=True)
                    last.then_inc(outer_done, 1)
                for u, q in lanes:
                    pe.wait_ge(outer_ready, q + 1)
                    for pair in range(2):
                        last = nc.tensor.matmul(chip.bank(u, 3)[:, pair * T:(pair + 1) * T], outer[:, u, pair, :],
                                                value[:, u, pair * T:(pair + 1) * T], start=True, stop=True)
                    last.then_inc(o_done, 1)
                for u, q in lanes:
                    pe.wait_ge(spread_ready, q + 1)
                    tokens = spread_o[:, u, :, :, :].rearrange("p g h (j r) -> p r (g h j)", r=8)
                    for jr in range(8):
                        last = nc.tensor.matmul(chip.bank(u, 2)[:, 0:QN], op["a1_wo"][:, jr * P:(jr + 1) * P],
                                                tokens[:, jr, :], start=(jr == 0), stop=(jr == 7))
                    last.then_inc(mixed, 1)
                for u, q in lanes:
                    pe.wait_ge(y_ready, q + 1)
                    post.centre(u, y[:, u, :])
                for u, q in lanes:
                    post.average(pe, u, q)

            chip.loop(pe, body)

        @block.scalar
        def _(act):
            nc.scalar.preload_act_table_set("natural_log_exp_and_others")
            def body(it):
                lanes = [(u, 2 * it + u) for u in range(2)]
                for u, q in lanes:
                    norm.squares(act, u, q)
                for u, q in lanes:
                    norm.logs(act, u, q)
                for u, q in lanes:
                    norm.powers(act, u, q)
                for u, q in lanes:
                    act.wait_ge(projected, q + 1)
                    nc.scalar.activation(query[:, u, :, :], chip.bank(u, 3)[:, 0:QN].rearrange("p (s e) -> p s e", s=3),
                                         ACT.Copy, scale=D ** -0.5).then_inc(query_ready, 1)
                for u, q in lanes:
                    act.wait_ge(peak_ready, q + 1)
                    for pair in range(2):
                        cols = slice(pair * T, (pair + 1) * T)
                        last = nc.scalar.activation(key[:, u, cols], chip.bank(u, 1)[:, cols], ACT.Exp,
                                                    bias=peak[:, u, pair:pair + 1], accum_out=total[:, u, pair:pair + 1])
                    last.then_inc(key_ready, 1)
                for u, q in lanes:
                    act.wait_ge(key_done, q + 1)
                    nc.scalar.activation(key_t[:, u, :, :], chip.bank(u, 0)[:, 0:2 * P].rearrange("p (g d) -> p g d", g=2),
                                         ACT.Copy).then_inc(key_t_ready, 1)
                for u, q in lanes:
                    act.wait_ge(o_done, q + 1)
                    nc.scalar.activation(o[:, u, :], chip.bank(u, 3)[:, 0:QN], ACT.Copy).then_inc(o_ready, 1)
                for u, q in lanes:
                    act.wait_ge(mixed, q + 1)
                    nc.scalar.activation(y[:, u, :], chip.bank(u, 2)[:, 0:QN], ACT.Identity,
                                         bias=op["a1_bo"]).then_inc(y_ready, 1)
                for u, q in lanes:
                    post.squares(act, u, q)
                for u, q in lanes:
                    post.logs(act, u, q)
                for u, q in lanes:
                    post.powers(act, u, q)

            chip.loop(act, body)

        @block.vector
        def _(dve):
            nc.vector.memset(key_z[:, :, :, :], 0.0).then_inc(cleared, 1)
            dve.wait_ge(cleared, 1)

            def body(it):
                lanes = [(u, 2 * it + u) for u in range(2)]
                for u, q in lanes:
                    norm.scale(dve, u, q, xn[:, u, :])
                for u, q in lanes:
                    dve.wait_ge(projected, q + 1)
                    nc.vector.tensor_reduce(peak[:, u, :], chip.bank(u, 1)[:, 0:QN].rearrange("p (g t) -> p g t", t=T),
                                            X, ALU.max, negate=True).then_inc(peak_ready, 1)
                    nc.vector.tensor_copy(value[:, u, :], chip.bank(u, 2)[:, 0:QN]).then_inc(value_ready, 1)
                for u, q in lanes:
                    dve.wait_ge(key_ready, q + 1)
                    nc.vector.reciprocal(inverse[:, u, :], total[:, u, :]).then_inc(inverse_ready, 1)
                for u, q in lanes:
                    dve.wait_ge(key_done, q + 1)
                    for pair in range(2):
                        half = slice(64 * pair, 64 * pair + 64)
                        last = nc.vector.tensor_copy(key_z[half, u, pair, :], chip.bank(u, 2)[half, 0:P])
                    last.then_inc(key_z_ready, 1)
                for u, q in lanes:
                    dve.wait_ge(outer_done, q + 1)
                    dve.wait_ge(inverse_ready, q + 1)
                    for pair in range(2):
                        last = nc.vector.scalar_tensor_tensor(
                            outer[:, u, pair, :], chip.bank(u, 1)[:, pair * P:(pair + 1) * P],
                            inverse[:, u, pair:pair + 1], op["a1_heads"], ALU.mult, ALU.mult)
                    last.then_inc(outer_ready, 1)
                for u, q in lanes:
                    dve.wait_ge(o_ready, q + 1)
                    for h in range(8):
                        last = nc.vector.tensor_scalar(spread_o[:, u, :, h, :],
                                                       o[:, u, :].rearrange("p (g t) -> p g t", t=T),
                                                       op["a1_head"][:, h:h + 1], None, ALU.mult)
                    last.then_inc(spread_ready, 1)
                for u, q in lanes:
                    post.scale(dve, u, q, yn[:, u, :])
                for u, q in lanes:
                    dve.wait_ge(post.ready, q + 1)
                    nc.vector.tensor_scalar(yg[:, u, :], yn[:, u, :], op["a1_gamma"], op["a1_beta"],
                                            ALU.mult, ALU.add).then_inc(yg_ready, 1)
                for u, q in lanes:
                    dve.wait_ge(yg_ready, q + 1)
                    nc.vector.tensor_tensor(chip.h_quad(q), chip.h_quad(q), yg[:, u, :], ALU.add)

            chip.loop(dve, body)


def routed(chip):
    nc, op = chip.nc, chip.operand
    with ExitStack() as ctx:
        def sb(n, shape, dt=F32):
            return ctx.enter_context(nc.sbuf_tensor(f"f1_{n}", shape, dt))

        def sem(n):
            return chip.semaphore(f"f1_{n}")

        norm = Norm(chip, ctx, "f1_norm")
        xn = sb("xn", [P, 2, QN])
        shared = sb("shared", [P, 2, F1])
        weight = sb("weight", [P, 2, 2, 2, F1])
        bias = sb("bias", [P, 2, 2, 2])
        hid = [sb(f"hid{n}", [P, 2, 2, 2, T]) for n in range(3)]
        shared_ready = sem("shared_ready")
        weight_ready = sem("weight_ready")
        entered = sem("entered")
        hid_act = [sem(f"hid_act{n}") for n in range(3)]
        hid_dve = [sem(f"hid_dve{n}") for n in range(3)]
        layered = [sem(f"layered{n}") for n in range(2)]
        left, h_ready = sem("left"), sem("h_ready")

        block = ctx.enter_context(nc.Block())

        @block.tensor
        def _(pe):
            def body(it):
                lanes = [(u, 2 * it + u) for u in range(2)]
                for u, q in lanes:
                    if not (isinstance(it, int) and it == 0):
                        pe.wait_ge(h_ready, q - 1)
                    norm.centre(u, chip.h_quad(q))
                for u, q in lanes:
                    norm.average(pe, u, q)
                for u, q in lanes:
                    pe.wait_ge(norm.ready, q + 1)
                    for b in range(2):
                        half = slice(64 * b, 64 * b + 64)
                        last = nc.tensor.matmul(chip.bank(u, 2 + b)[:, 0:QN], op["f1_wi"][half, :], xn[half, u, :],
                                                start=True, stop=True)
                    last.then_inc(entered, 1)
                for layer in range(2):
                    for u, q in lanes:
                        pe.wait_ge(hid_act[layer], q + 1)
                        pe.wait_ge(hid_dve[layer], q + 1)
                        if layer == 0:
                            pe.wait_ge(weight_ready, q + 1)
                        for pair in range(2):
                            out = chip.bank(u, (2 * layer + pair) % 4)[:, 0:QN]
                            last = nc.tensor.matmul(out, weight[:, u, layer, pair, :],
                                                    hid[layer][:, u, pair, :, :].rearrange("p b t -> p (b t)"),
                                                    start=True, stop=True)
                        last.then_inc(layered[layer], 1)
                for u, q in lanes:
                    pe.wait_ge(hid_act[2], q + 1)
                    pe.wait_ge(hid_dve[2], q + 1)
                    for b in range(2):
                        for pair in range(2):
                            last = nc.tensor.matmul(
                                chip.bank(u, 0)[64 * b:64 * b + 64, pair * T:(pair + 1) * T], op["f1_wo"],
                                hid[2][:, u, pair, b, :], start=True, stop=True)
                    last.then_inc(left, 1)

            chip.loop(pe, body)

        @block.scalar
        def _(act):
            nc.scalar.preload_act_table_set("natural_log_exp_and_others")
            def body(it):
                lanes = [(u, 2 * it + u) for u in range(2)]
                for u, q in lanes:
                    norm.squares(act, u, q)
                for u, q in lanes:
                    norm.logs(act, u, q)
                for u, q in lanes:
                    norm.powers(act, u, q)
                for u, q in lanes:
                    act.wait_ge(entered, q + 1)
                    nc.scalar.activation(hid[0][:, u, :, 0, :], chip.bank(u, 2)[:, 0:QN].rearrange("p (g t) -> p g t", g=2),
                                         ACT.Relu, bias=op["f1_bi"]).then_inc(hid_act[0], 1)
                for layer in range(2):
                    for u, q in lanes:
                        act.wait_ge(layered[layer], q + 1)
                        nc.scalar.activation(hid[layer + 1][:, u, 0, :, :].rearrange("p b t -> p (b t)"),
                                             chip.bank(u, 2 * layer)[:, 0:QN], ACT.Relu,
                                             bias=bias[:, u, layer, 0:1]).then_inc(hid_act[layer + 1], 1)

            chip.loop(act, body)

        @block.vector
        def _(dve):
            def body(it):
                lanes = [(u, 2 * it + u) for u in range(2)]
                for u, q in lanes:
                    norm.scale(dve, u, q, xn[:, u, :])
                for u, q in lanes:
                    dve.wait_ge(entered, q + 1)
                    nc.vector.tensor_scalar(hid[0][:, u, :, 1, :], chip.bank(u, 3)[:, 0:QN].rearrange("p (g t) -> p g t", g=2),
                                            op["f1_bi"], 0.0, ALU.add, ALU.max).then_inc(hid_dve[0], 1)
                for layer in range(2):
                    for u, q in lanes:
                        dve.wait_ge(layered[layer], q + 1)
                        nc.vector.tensor_scalar(hid[layer + 1][:, u, 1, :, :].rearrange("p b t -> p (b t)"),
                                                chip.bank(u, 2 * layer + 1)[:, 0:QN], bias[:, u, layer, 1:2], 0.0,
                                                ALU.add, ALU.max).then_inc(hid_dve[layer + 1], 1)
                for u, q in lanes:
                    dve.wait_ge(left, q + 1)
                    nc.vector.scalar_tensor_tensor(chip.h_quad(q), chip.bank(u, 0)[:, 0:QN], op["f1_bo"],
                                                   chip.h_quad(q), ALU.add, ALU.add).then_inc(h_ready, 1)

            chip.loop(dve, body)

        @block.gpsimd
        def _(pool):
            for layer in range(2):
                last = nc.gpsimd.tensor_tensor(shared[:, layer, :], op["f1_ws"][:, layer * F1:(layer + 1) * F1],
                                               op["ident"], ALU.add)
                last.then_inc(shared_ready, 1)
            pool.wait_ge(shared_ready, 2)

            def body(it):
                lanes = [(u, 2 * it + u) for u in range(2)]
                for u, q in lanes:
                    if not (isinstance(it, int) and it == 0):
                        pool.wait_ge(h_ready, q - 1)
                    for pair in range(2):
                        route = pool.value_load(chip.routes[0:1, bass.ds(2 * q + pair, 1)], min_val=0, max_val=E1 - 1)
                        for layer in range(2):
                            nc.gpsimd.tensor_tensor(weight[:, u, layer, pair, :],
                                                    op["f1_wr"][:, bass.ds(route * F1 + layer * E1 * F1, F1)],
                                                    shared[:, layer, :], ALU.add)
                            last = nc.gpsimd.tensor_tensor(bias[:, u, layer, pair:pair + 1],
                                                           op["f1_br"][:, bass.ds(route + layer * E1, 1)],
                                                           op["f1_bs"][:, layer:layer + 1], ALU.add)
                    last.then_inc(weight_ready, 1)

            chip.loop(pool, body)


def experts2(chip):
    nc, op = chip.nc, chip.operand
    with ExitStack() as ctx:
        def sb(n, shape, dt=F32):
            return ctx.enter_context(nc.sbuf_tensor(f"f2_{n}", shape, dt))

        def sem(n):
            return chip.semaphore(f"f2_{n}")

        pairs = E2 // 2
        step_count = 2 * pairs
        gate_lag, sum_lag = 3, 4
        rows = 3 * 2 * E2
        norm = Norm(chip, ctx, "f2_norm", lambda u, i: chip.psum[:, 6 + i, :])
        xn = sb("xn", [P, 2, 2, QN])
        router = sb("router", [2 * R2, 2, QN])
        scores = sb("scores", [P, 2, 6 * E2])
        rank = sb("rank", [P, 2, 6 * E2])
        shift, power, share = (sb(n, [P, 12, E2]) for n in ("shift", "power", "share"))
        top, total, inverse = (sb(n, [P, 12]) for n in ("top", "total", "inverse"))
        work = {n: sb(n, [P, 12, E2]) for n in ("equal", "ranked", "rest", "hot1", "hot2", "gate1", "gate")}
        work |= {n: sb(n, [P, 12]) for n in ("best1", "best2", "first", "gap", "ratio", "whole", "w1", "w2")}
        remains = sb("remains", [P, 6, 2 * E2])
        parts = sb("parts", [P, 6, 3, 2 * E2], BF16)
        parts_t = sb("parts_t", [rows, 2, QN], BF16)
        parts_t32 = sb("parts_t32", [rows, 2, QN])
        ident_b = sb("ident_b", [P, P], BF16)
        pick = sb("pick", [rows, pairs, 2, 2 * D], BF16)
        hid1 = sb("hid1", [P, 2, QN])
        hid2 = sb("hid2", [P, step_count, 2, QN])
        gated = sb("gated", [P, 2, 2, QN])

        def by_step(n):
            return [[sem(f"{n}{s}_{b}") for b in range(2)] for s in range(step_count)]

        set_up, routed_done, router_ready, scored = sem("set_up"), sem("routed_done"), sem("router_ready"), sem("scored")
        shift_ready, power_ready = sem("shift_ready"), sem("power_ready")
        steps = [sem(f"step{n}") for n in range(26)]
        gap_ready, ratio_ready, gates_ready = sem("gap_ready"), sem("ratio_ready"), sem("gates_ready")
        parts_ready, parts_done, parts_t_ready = sem("parts_ready"), sem("parts_done"), sem("parts_t_ready")
        hid1_done, hid1_ready, hid2_done, hid2_ready, spread_done, gated_ready = map(
            by_step, ("hid1_done", "hid1_ready", "hid2_done", "hid2_ready", "spread_done", "gated_ready"))
        summed, h_ready = sem("summed"), sem("h_ready")

        def at_start(it):
            return isinstance(it, int) and it == 0

        def loop(eng, body):
            turns = chip.quads // 4

            def turn(it, last):
                for parity in range(2):
                    body(2 * it + parity, parity, not (last and parity == 1))

            turn(0, turns == 1)
            if turns > 2:
                with eng.Fori(1, turns - 1) as it:
                    turn(it, False)
            if turns > 1:
                turn(turns - 1, True)

        def earlier(s, n, it):
            if s >= n:
                return s - n, it
            return None if at_start(it) else (s - n + step_count, it - 1)

        def wait_step(eng, signals, at, b):
            if at is not None:
                eng.wait_ge(signals[at[0]][b], at[1] + 1)

        block = ctx.enter_context(nc.Block())

        @block.tensor
        def _(pe):
            def route(v, q, parity):
                pe.wait_ge(norm.ready, q + 1)
                nc.tensor.matmul(chip.psum[0:2 * R2, 7, 0:QN], op["f2_rw1"], xn[:, parity, v, :],
                                 start=True, stop=True).then_inc(routed_done, 1)

            def score(v, q):
                pe.wait_ge(router_ready, q + 1)
                for j in range(3):
                    at = 2 * E2 * (3 * v + j)
                    last = nc.tensor.matmul(chip.psum[:, 6, at:at + 2 * E2], router[:, v, j * P:(j + 1) * P],
                                            op["f2_rw2"][0:2 * R2, :], start=True, stop=True)
                last.then_inc(scored, 1)

            def prepare(i, it, parity):
                quads = [2 * it, 2 * it + 1]
                if i == 0:
                    pe.wait_ge(steps[0], it)
                    norm.centre(0, chip.h_quad(quads[0]))
                if i == 1:
                    norm.average(pe, 0, quads[0])
                if i == 3:
                    route(0, quads[0], parity)
                    norm.centre(1, chip.h_quad(quads[1]))
                if i == 4:
                    pe.wait_ge(router_ready, quads[0] + 1)
                    norm.average(pe, 1, quads[1])
                if i == 6:
                    route(1, quads[1], parity)
                    score(0, quads[0])
                if i == 8:
                    score(1, quads[1])

            def turn_gates(it):
                pe.wait_ge(parts_ready, it + 1)
                wait_step(pe, gated_ready, earlier(2, gate_lag, it), 1)
                for j in range(6):
                    at = 64 * (j // 3)
                    last = nc.tensor.matmul(chip.psum[at:at + rows, 4, j % 3 * P:(j % 3 + 1) * P],
                                            parts[:, j, :, :].rearrange("p a e -> p (a e)"), ident_b[:, :],
                                            start=True, stop=True)
                last.then_inc(parts_done, 1)

            def spread_gates(at, b):
                if at is None:
                    return
                s, it = at
                if b:
                    wait_step(pe, gated_ready, at, 0)
                else:
                    wait_step(pe, gated_ready, earlier(s, 1, it), 1)
                    pe.wait_ge(parts_t_ready, 4 * it + 4)
                nc.tensor.matmul(chip.psum[:, 4, 0:QN], pick[:, s % pairs, b, :], parts_t[:, s // pairs, :],
                                 start=True, stop=True).then_inc(spread_done[s][b], 1)

            def third(at):
                if at is None:
                    return
                s, it = at
                k, v = s % pairs, s // pairs
                if k == 0:
                    if v or not at_start(it):
                        pe.wait_ge(h_ready, 2 * it + v)
                    nc.tensor.matmul(chip.psum[:, 5, 0:QN], op["f2_b3"][0:rows, :], parts_t32[:, v, :],
                                     start=True, stop=False, skip_group_check=True)
                for b in range(2):
                    wait_step(pe, gated_ready, at, b)
                    last = nc.tensor.matmul(chip.psum[64 * b:64 * b + 64, 5, 0:QN], op["f2_w3"][:, k * D:(k + 1) * D],
                                            gated[:, s % 2, b, :], start=False, stop=(k == pairs - 1),
                                            skip_group_check=True)
                if k == pairs - 1:
                    last.then_inc(summed, 1)

            def body(it, parity, more):
                for s in range(step_count):
                    k, v = s % pairs, s // pairs
                    for b in range(2):
                        half = slice(64 * b, 64 * b + 64)
                        wait_step(pe, hid1_ready, earlier(s, 1, it), b)
                        nc.tensor.matmul(chip.psum[:, b, 0:QN], op["f2_w1"][half, k * P:(k + 1) * P],
                                         xn[half, parity, v, :], start=True, stop=True).then_inc(hid1_done[s][b], 1)
                    spread_gates(earlier(s, gate_lag, it), 0)
                    third(earlier(s, sum_lag, it))
                    if more:
                        prepare(2 * s, it + 1, 1 - parity)
                    for b in range(2):
                        pe.wait_ge(hid1_ready[s][b], it + 1)
                        wait_step(pe, hid2_ready, earlier(s, 1, it), b)
                        nc.tensor.matmul(chip.psum[:, 2 + b, 0:QN], op["f2_w2"][:, k * P:(k + 1) * P],
                                         hid1[:, b, :], start=True, stop=True).then_inc(hid2_done[s][b], 1)
                    spread_gates(earlier(s, gate_lag, it), 1)
                    if more:
                        prepare(2 * s + 1, it + 1, 1 - parity)
                    if s == gate_lag - 1:
                        turn_gates(it)

            pe.wait_ge(set_up, 4)
            for v in range(2):
                if v:
                    pe.wait_ge(router_ready, v)
                norm.centre(v, chip.h_quad(v))
                norm.average(pe, v, v)
                route(v, v, 0)
            score(0, 0)
            score(1, 1)
            loop(pe, body)
            for s in range(sum_lag):
                spread_gates(earlier(s, gate_lag, chip.quads // 2) if s < gate_lag else None, 0)
                third(earlier(s, sum_lag, chip.quads // 2))
                spread_gates(earlier(s, gate_lag, chip.quads // 2) if s < gate_lag else None, 1)

        @block.scalar
        def _(act):
            nc.scalar.preload_act_table_set("natural_log_exp_and_others")

            def router_units(v, q):
                act.wait_ge(routed_done, q + 1)
                nc.scalar.activation(router[:, v, :], chip.psum[0:2 * R2, 7, 0:QN], ACT.Relu,
                                     bias=op["f2_rb1"][0:2 * R2, :]).then_inc(router_ready, 1)

            def softmax_exp(it):
                act.wait_ge(shift_ready, it + 1)
                nc.scalar.activation(power[:, :, :], shift[:, :, :], ACT.Exp).then_inc(power_ready, 1)

            def prepare(i, it):
                quads = [2 * it, 2 * it + 1]
                if i == 0:
                    norm.squares(act, 0, quads[0])
                if i == 1:
                    norm.logs(act, 0, quads[0])
                    norm.powers(act, 0, quads[0])
                if i == 3:
                    router_units(0, quads[0])
                    norm.squares(act, 1, quads[1])
                if i == 4:
                    norm.logs(act, 1, quads[1])
                    norm.powers(act, 1, quads[1])
                if i == 6:
                    router_units(1, quads[1])
                if i == 9:
                    softmax_exp(it)

            def body(it, parity, more):
                for s in range(step_count):
                    k = s % pairs
                    for b in range(2):
                        act.wait_ge(hid1_done[s][b], it + 1)
                        nc.scalar.activation(hid1[:, b, :], chip.psum[:, b, 0:QN], ACT.Relu,
                                             bias=op["f2_b1"][:, k:k + 1]).then_inc(hid1_ready[s][b], 1)
                    if s == 0:
                        act.wait_ge(gap_ready, it + 1)
                        nc.scalar.activation(work["ratio"][:, :], work["gap"][:, :], ACT.Exp).then_inc(ratio_ready, 1)
                    if more:
                        prepare(2 * s, it + 1)
                    for b in range(2):
                        act.wait_ge(hid2_done[s][b], it + 1)
                        wait_step(act, gated_ready, earlier(s, step_count, it), b)
                        nc.scalar.activation(hid2[:, s, b, :], chip.psum[:, 2 + b, 0:QN], ACT.Relu,
                                             bias=op["f2_b2"][:, k:k + 1]).then_inc(hid2_ready[s][b], 1)
                    if more:
                        prepare(2 * s + 1, it + 1)
                    if s == gate_lag - 1:
                        act.wait_ge(parts_done, it + 1)
                        for copy in (parts_t, parts_t32):
                            for v in range(2):
                                nc.scalar.activation(copy[:, v, :], chip.psum[64 * v:64 * v + rows, 4, 0:QN],
                                                     ACT.Copy).then_inc(parts_t_ready, 1)

            for v in range(2):
                norm.squares(act, v, v)
                norm.logs(act, v, v)
                norm.powers(act, v, v)
                router_units(v, v)
            softmax_exp(0)
            loop(act, body)

        @block.vector
        def _(dve):
            nc.vector.tensor_copy(ident_b[:, :], op["ident"]).then_inc(set_up, 1)
            nc.vector.tensor_copy(pick[:, :, :, :].rearrange("p k b (e d) -> p (k b e) d", d=D),
                                  op["f2_pick"][0:rows, :].unsqueeze(2).to_broadcast([rows, 2 * E2, D])
                                  ).then_inc(set_up, 1)
            for v in range(2):
                nc.vector.tensor_copy(rank[:, v, :], op["f2_rank"]).then_inc(set_up, 1)
            dve.wait_ge(set_up, 4)

            def links(it, start, between):
                at = [start]

                def step(instruction):
                    instruction.then_inc(steps[at[0]], 1)

                def wait():
                    dve.wait_ge(steps[at[0]], it + 1)
                    at[0] += 1
                    if (at[0] - start) % 4 == 0:
                        between()

                return step, wait

            def choose(it, between):
                step, wait = links(it, 0, between)

                def wide(a):
                    return a[:, :].unsqueeze(2).to_broadcast([P, 12, E2])

                dve.wait_ge(scored, 2 * it + 2)
                step(nc.vector.tensor_tensor(scores[:, :, :].rearrange("p v e -> p (v e)"), chip.psum[:, 6, 0:12 * E2],
                                             op["f2_rb2"], ALU.add))
                wait()
                flat = scores[:, :, :].rearrange("p v (g e) -> p (v g) e", e=E2)
                ranks = rank[:, :, :].rearrange("p v (g e) -> p (v g) e", e=E2)
                step(nc.vector.tensor_reduce(top[:, :], flat, X, ALU.max))
                wait()
                nc.vector.tensor_tensor(shift[:, :, :], flat, wide(top), ALU.subtract).then_inc(shift_ready, 1)
                between()
                dve.wait_ge(power_ready, it + 1)
                step(nc.vector.tensor_reduce(total[:, :], power[:, :, :], X, ALU.add))
                wait()
                step(nc.vector.reciprocal(inverse[:, :], total[:, :]))
                wait()
                step(nc.vector.tensor_tensor(share[:, :, :], power[:, :, :], wide(inverse), ALU.mult))
                wait()
                top_two(chip, dve, step, wait, share[:, :, :], ranks, E2, work)

            def gates(it, between):
                step, wait = links(it, 16, between)
                gates_of_two(chip, dve, step, wait, E2, work, gap_ready, ratio_ready, gates_ready, it)
                gate = work["gate"][:, :, :].rearrange("p (j b) e -> p j (b e)", b=2)
                if not at_start(it):
                    dve.wait_ge(parts_done, it)
                step(nc.vector.tensor_copy(parts[:, :, 0, :], gate))
                wait()
                step(nc.vector.tensor_tensor(remains[:, :, :], gate, parts[:, :, 0, :], ALU.subtract))
                wait()
                step(nc.vector.tensor_copy(parts[:, :, 1, :], remains[:, :, :]))
                wait()
                nc.vector.tensor_tensor(parts[:, :, 2, :], remains[:, :, :], parts[:, :, 1, :],
                                        ALU.subtract).then_inc(parts_ready, 1)

            def product(at, b):
                if at is None:
                    return
                s, it = at
                wait_step(dve, spread_done, at, b)
                wait_step(dve, hid2_ready, at, b)
                nc.vector.tensor_tensor(gated[:, s % 2, b, :], hid2[:, s, b, :], chip.psum[:, 4, 0:QN],
                                        ALU.mult).then_inc(gated_ready[s][b], 1)

            def add(at):
                if at is None or at[0] % pairs != pairs - 1:
                    return
                q = 2 * at[1] + at[0] // pairs
                dve.wait_ge(summed, q + 1)
                nc.vector.tensor_tensor(chip.h_quad(q), chip.psum[:, 5, 0:QN], chip.h_quad(q),
                                        ALU.add).then_inc(h_ready, 1)

            def body(it, parity, more):
                products = [(s, b) for s in range(step_count) for b in range(2)]

                def multiply():
                    if not products:
                        return
                    s, b = products.pop(0)
                    product(earlier(s, gate_lag, it), b)
                    if b == 0:
                        add(earlier(s, sum_lag, it))
                    if more and (s, b) == (1, 0):
                        norm.scale(dve, 0, 2 * it + 2, xn[:, 1 - parity, 0, :])
                    if more and (s, b) == (2, 1):
                        norm.scale(dve, 1, 2 * it + 3, xn[:, 1 - parity, 1, :])

                gates(it, multiply)
                while len(products) > 4:
                    multiply()
                if more:
                    choose(it + 1, multiply)
                while products:
                    multiply()

            for v in range(2):
                norm.scale(dve, v, v, xn[:, 0, v, :])
            choose(0, lambda: None)
            loop(dve, body)
            for s in range(sum_lag):
                if s < gate_lag:
                    product(earlier(s, gate_lag, chip.quads // 2), 0)
                add(earlier(s, sum_lag, chip.quads // 2))
                if s < gate_lag:
                    product(earlier(s, gate_lag, chip.quads // 2), 1)


def heads_attention(chip):
    nc, op, ident = chip.nc, chip.operand, chip.operand["ident"]
    hd = D // HEADS3
    wide = HEADS3 * (P + hd) + 64
    with ExitStack() as ctx:
        def sb(n, shape, dt=F32):
            return ctx.enter_context(nc.sbuf_tensor(f"a3_{n}", shape, dt))

        def sem(n):
            return chip.semaphore(f"a3_{n}")

        square, centred, log, rstd = sb("square", [P, QN]), sb("centred", [P, QN]), sb("log", [P, QN]), sb("rstd", [P, QN])
        xn = sb("xn", [P, 2, QN])
        query = sb("query", [P, QN])
        query_b = sb("query_b", [P, 2, HEADS3, 6, 2, 64])
        key = sb("key", [P, 2, QN])
        value = sb("value", [P, 2, 2, wide])
        value_z = sb("value_z", [P, 2, 2, wide])
        peak = sb("peak", [P, 2, 3, 2])
        total = sb("total", [P, 2, 3, 2])
        inverse = sb("inverse", [P, 2, 3, 2])
        prob = sb("prob", [P, 2, 3, 2, T])
        even = sb("even", [P, 2, 3, 2, T])
        prob_t = sb("prob_t", [P, 2, 3, QN])
        mix_b = sb("mix_b", [P, QN], BF16)
        mix = sb("mix", [P, QN])

        cleared, pool_passed = sem("cleared"), sem("pool_passed")
        centre_done, centre_kept, average_done, log_ready, rstd_ready, xn_ready = (sem(n) for n in (
            "centre_done", "centre_kept", "average_done", "log_ready", "rstd_ready", "xn_ready"))
        query_done, query_ready, query_b_ready = sem("query_done"), sem("query_ready"), sem("query_b_ready")
        key_done, key_ready, value_done, value_ready = sem("key_done"), sem("key_ready"), sem("value_done"), sem("value_ready")
        heads = range(HEADS3)
        scored, peak_ready, exp_ready, inverse_ready, even_act, even_dve, prob_done, prob_act, prob_dve, mixed = (
            [sem(f"{n}{h}") for h in heads] for n in (
                "scored", "peak_ready", "exp_ready", "inverse_ready", "even_act", "even_dve", "prob_done",
                "prob_act", "prob_dve", "mixed"))
        mix_b_ready, mix_ready, left, h_ready = sem("mix_b_ready"), sem("mix_ready"), sem("left"), sem("h_ready")

        spare = chip.psum[:, 7, 0:QN]

        def scores_of(h):
            at = 3 * (h % 2)
            return chip.psum[:, at:at + 3, 0:QN].rearrange("p c (g t) -> p c g t", t=T)

        def turned_of(h, s):
            return chip.psum[:, 3 * (h % 2) + s, 0:QN]

        def at_start(q):
            return isinstance(q, int) and q == 0

        def earlier(u, q, h, n):
            if h >= n:
                return u, q, h - n
            return None if at_start(q) else (1 - u, q - 1, h - n + HEADS3)

        def loop(eng, quad):
            turns = chip.quads // 2

            def both(it, last):
                for u in range(2):
                    quad(u, 2 * it + u, not (last and u == 1), not last)

            both(0, turns == 1)
            if turns > 2:
                with eng.Fori(1, turns - 1) as it:
                    both(it, False)
            if turns > 1:
                both(turns - 1, True)

        after_last = (0, chip.quads)

        block = ctx.enter_context(nc.Block())

        @block.tensor
        def _(pe):
            def centre(q):
                nc.tensor.matmul(spare, op["centre"], chip.h_quad(q), start=True, stop=True).then_inc(centre_done, 1)

            def average(q):
                pe.wait_ge(centre_kept, 2 * q + 2)
                nc.tensor.matmul(spare, op["mean"], square[:, :], start=True, stop=True).then_inc(average_done, 1)

            def queries(u, q):
                pe.wait_ge(xn_ready, q + 1)
                nc.tensor.matmul(spare, op["a3_wq"], xn[:, u, :], start=True, stop=True).then_inc(query_done, 1)

            def keys(u, q):
                pe.wait_ge(query_ready, q + 1)
                nc.tensor.matmul(spare, op["a3_wk"], xn[:, u, :], start=True, stop=True).then_inc(key_done, 1)

            def values(u, q):
                pe.wait_ge(key_ready, q + 1)
                for s in range(3):
                    last = nc.tensor.matmul(spare[:, s * P:(s + 1) * P], xn[:, u, s * P:(s + 1) * P],
                                            op["a3_wv"], start=True, stop=True)
                last.then_inc(value_done, 1)

            def leave(q):
                pe.wait_ge(mix_ready, q + 1)
                nc.tensor.matmul(spare, op["a3_wo"], mix[:, :], start=True, stop=True).then_inc(left, 1)

            def score(u, q, h):
                if h == 0:
                    pe.wait_ge(query_b_ready, q + 1)
                    pe.wait_ge(key_ready, q + 1)
                before = earlier(u, q, h, 2)
                if before:
                    pe.wait_ge(prob_act[before[2]], 2 * before[1] + 2)
                    pe.wait_ge(prob_dve[before[2]], before[1] + 1)
                for c in range(3):
                    for pair in range(2):
                        last = nc.tensor.matmul(scores_of(h)[:, c, pair, :],
                                                query_b[:, u, h, 3 * pair + c, :, :].rearrange("p b t -> p (b t)"),
                                                key[:, u, pair * T:(pair + 1) * T], start=True, stop=True)
                last.then_inc(scored[h], 1)

            def turn(step):
                if step is None:
                    return
                u, q, h = step
                pe.wait_ge(even_dve[h], q + 1)
                pe.wait_ge(even_act[h], q + 1)
                for s in range(3):
                    for c in range(3):
                        probs = even[:, h % 2, c, :, :].rearrange("p g t -> p (g t)")[:, s * P:(s + 1) * P]
                        last = nc.tensor.transpose(turned_of(h, s)[:, c * P:(c + 1) * P], probs, ident)
                last.then_inc(prob_done[h], 1)

            def mixing(step):
                if step is None:
                    return
                u, q, h = step
                pe.wait_ge(prob_act[h], 2 * q + 2)
                pe.wait_ge(prob_dve[h], q + 1)
                if h == 0:
                    pe.wait_ge(value_ready, q + 1)
                    if not at_start(q):
                        pe.wait_ge(mix_b_ready, q)
                for pair in range(2):
                    for middle in (False, True):
                        for b in range(2):
                            v = (value_z if middle else value)[:, u, pair, h * P + b * D:h * P + (b + 1) * D]
                            probs = prob_t[:, h % 2, 1 if middle else 2 * pair, :].rearrange(
                                "p (c b t) -> p b c t", c=3, b=2)[:, b, :, :]
                            last = nc.tensor.matmul(
                                chip.psum[64 * b:64 * b + 64, 6, pair * T:(pair + 1) * T]
                                .rearrange("p (c t) -> p c t", c=3), v, probs,
                                start=(h == 0 and pair == 0 and not middle),
                                stop=(h == HEADS3 - 1 and middle), skip_group_check=True)
                last.then_inc(mixed[h], 1)

            def quad(u, q, more, more2):
                for h in heads:
                    score(u, q, h)
                    if h == 0 and more:
                        if not (isinstance(q, int) and q < 2):
                            pe.wait_ge(h_ready, q - 1)
                        queries(1 - u, q + 1)
                    if h == 2 and more2:
                        pe.wait_ge(value_ready, q + 2)
                        centre(q + 2)
                    turn(earlier(u, q, h, 1))
                    if h == 1 and more:
                        values(1 - u, q + 1)
                    if h == 3 and not at_start(q):
                        if more2:
                            pe.wait_ge(log_ready, q + 3)
                        leave(q - 1)
                    mixing(earlier(u, q, h, 2))
                    if h == 0 and more:
                        keys(1 - u, q + 1)
                    if h == 2 and more2:
                        average(q + 2)

            pe.wait_ge(cleared, 2)
            for q in range(2):
                if q:
                    pe.wait_ge(log_ready, q)
                centre(q)
                average(q)
            pe.wait_ge(log_ready, 2)
            queries(0, 0)
            keys(0, 0)
            values(0, 0)
            pe.wait_ge(value_ready, 1)
            loop(pe, quad)
            turn(earlier(*after_last, 0, 1))
            mixing(earlier(*after_last, 0, 2))
            mixing(earlier(*after_last, 1, 2))
            leave(chip.quads - 1)

        @block.scalar
        def _(act):
            nc.scalar.preload_act_table_set("natural_log_exp_and_others")

            def keep_centre(q):
                act.wait_ge(centre_done, q + 1)
                nc.scalar.activation(square[:, :], spare, ACT.Square).then_inc(centre_kept, 1)
                if not at_start(q):
                    act.wait_ge(xn_ready, q)
                nc.scalar.activation(centred[:, :], spare, ACT.Copy).then_inc(centre_kept, 1)

            def deviation(q):
                act.wait_ge(average_done, q + 1)
                nc.scalar.activation(log[:, :], spare, ACT.Ln, bias=chip.eps[:, 0:1]).then_inc(log_ready, 1)
                act.wait_ge(log_ready, q + 1)
                nc.scalar.activation(rstd[:, :], log[:, :], ACT.Exp, scale=-0.5).then_inc(rstd_ready, 1)

            def keep_keys(u, q):
                act.wait_ge(key_done, q + 1)
                nc.scalar.activation(key[:, u, :], spare, ACT.Identity, bias=op["a3_bk"]).then_inc(key_ready, 1)

            def keep_turned(step):
                if step is None:
                    return
                u, q, h = step
                act.wait_ge(prob_done[h], q + 1)
                before = earlier(u, q, h, 2)
                if before:
                    act.wait_ge(mixed[before[2]], before[1] + 1)
                for s in (0, 2):
                    nc.scalar.activation(prob_t[:, h % 2, s, :], turned_of(h, s), ACT.Copy).then_inc(prob_act[h], 1)

            def round_mix(q):
                act.wait_ge(mixed[HEADS3 - 1], q + 1)
                nc.scalar.activation(mix_b[:, :], chip.psum[:, 6, 0:QN], ACT.Copy).then_inc(mix_b_ready, 1)

            def quad(u, q, more, more2):
                for h in heads:
                    keep_turned(earlier(u, q, h, 1))
                    if h == 2 and more2:
                        keep_centre(q + 2)
                    act.wait_ge(peak_ready[h], q + 1)
                    for c in range(3):
                        for pair in range(2):
                            last = nc.scalar.activation(prob[:, h % 2, c, pair, :], scores_of(h)[:, c, pair, :], ACT.Exp,
                                                        bias=peak[:, h % 2, c, pair:pair + 1],
                                                        accum_out=total[:, h % 2, c, pair:pair + 1])
                    last.then_inc(exp_ready[h], 1)
                    act.wait_ge(inverse_ready[h], q + 1)
                    for pair in range(2):
                        last = nc.scalar.activation(even[:, h % 2, 2, pair, :], prob[:, h % 2, 2, pair, :], ACT.Copy,
                                                    scale=inverse[:, h % 2, 2, pair:pair + 1])
                    last.then_inc(even_act[h], 1)
                    if h == 0 and more:
                        keep_keys(1 - u, q + 1)
                    if h == 1 and not at_start(q):
                        round_mix(q - 1)
                    if h == 2 and more2:
                        deviation(q + 2)

            for q in range(2):
                keep_centre(q)
                deviation(q)
            keep_keys(0, 0)
            loop(act, quad)
            keep_turned(earlier(*after_last, 0, 1))
            round_mix(chip.quads - 1)

        @block.vector
        def _(dve):
            def normed(u, q):
                dve.wait_ge(rstd_ready, q + 1)
                nc.vector.tensor_tensor(xn[:, u, :], centred[:, :], rstd[:, :], ALU.mult).then_inc(xn_ready, 1)

            def keep_queries(q):
                dve.wait_ge(query_done, q + 1)
                if not at_start(q):
                    dve.wait_ge(query_b_ready, q)
                nc.vector.tensor_scalar(query[:, :], spare, op["a3_bq"], hd ** -0.5,
                                        ALU.add, ALU.mult).then_inc(query_ready, 1)

            def keep_values(u, q):
                dve.wait_ge(value_done, q + 1)
                if not (isinstance(q, int) and q < 2):
                    dve.wait_ge(mixed[HEADS3 - 1], q - 1)
                slices = spare.rearrange("p (s b h e) -> p s b h e", s=3, b=2, h=HEADS3)
                bv = op["a3_bv"].rearrange("p (b h e) -> p b h e", b=2, h=HEADS3)
                for b in range(2):
                    def heads_of(tile):
                        return tile[:, b * D:b * D + HEADS3 * (P + hd)].rearrange(
                            "p (h c) -> p h c", h=HEADS3)[:, :, 0:hd]

                    for n, s in ((0, 0), (1, 2)):
                        nc.vector.tensor_tensor(heads_of(value[:, u, n, :]), slices[:, s, b, :, :], bv[:, b, :, :], ALU.add)
                    for pair in range(2):
                        half = slice(64 * pair, 64 * pair + 64)
                        last = nc.vector.tensor_tensor(heads_of(value_z[half, u, pair, :]), slices[half, 1, b, :, :],
                                                       bv[half, b, :, :], ALU.add)
                last.then_inc(value_ready, 1)

            def keep_turned(step):
                if step is None:
                    return
                u, q, h = step
                dve.wait_ge(prob_done[h], q + 1)
                before = earlier(u, q, h, 2)
                if before:
                    dve.wait_ge(mixed[before[2]], before[1] + 1)
                nc.vector.tensor_copy(prob_t[:, h % 2, 1, :], turned_of(h, 1)).then_inc(prob_dve[h], 1)

            def widen_mix(q):
                dve.wait_ge(mix_b_ready, q + 1)
                nc.vector.tensor_copy(mix[:, :], mix_b[:, :]).then_inc(mix_ready, 1)

            def finish(q):
                dve.wait_ge(left, q + 1)
                nc.vector.scalar_tensor_tensor(chip.h_quad(q), spare, op["a3_bo"],
                                               chip.h_quad(q), ALU.add, ALU.add).then_inc(h_ready, 1)

            def quad(u, q, more, more2):
                for h in heads:
                    dve.wait_ge(scored[h], q + 1)
                    nc.vector.tensor_reduce(peak[:, h % 2, :, :], scores_of(h), X, ALU.max,
                                            negate=True).then_inc(peak_ready[h], 1)
                    keep_turned(earlier(u, q, h, 1))
                    if h == 0 and more:
                        keep_queries(q + 1)
                    if h == 1 and more:
                        keep_values(1 - u, q + 1)
                    if h == 2 and not at_start(q):
                        widen_mix(q - 1)
                    if h == 3:
                        if not at_start(q):
                            finish(q - 1)
                        if more2:
                            normed(u, q + 2)
                    dve.wait_ge(exp_ready[h], q + 1)
                    nc.vector.reciprocal(inverse[:, h % 2, :, :], total[:, h % 2, :, :]).then_inc(inverse_ready[h], 1)
                    dve.wait_ge(inverse_ready[h], q + 1)
                    for c in range(2):
                        for pair in range(2):
                            last = nc.vector.tensor_scalar(even[:, h % 2, c, pair, :], prob[:, h % 2, c, pair, :],
                                                           inverse[:, h % 2, c, pair:pair + 1], None, ALU.mult)
                    last.then_inc(even_dve[h], 1)

            for q in range(2):
                normed(q, q)
            keep_queries(0)
            dve.wait_ge(cleared, 2)
            keep_values(0, 0)
            loop(dve, quad)
            keep_turned(earlier(*after_last, 0, 1))
            widen_mix(chip.quads - 1)
            finish(chip.quads - 1)

        @block.gpsimd
        def _(pool):
            nc.gpsimd.memset(value[:, :, :, :], 0.0).then_inc(cleared, 1)
            nc.gpsimd.memset(value_z[:, :, :, :], 0.0).then_inc(cleared, 1)

            def spread_queries(u, q):
                pool.wait_ge(query_ready, q + 1)
                if not (isinstance(q, int) and q < 2):
                    pool.wait_ge(scored[HEADS3 - 1], q - 1)
                pool.sem_inc(pool_passed, 1)
                for h in heads:
                    for b in range(2):
                        last = nc.gpsimd.tensor_scalar(query_b[:, u, h, :, b, :],
                                                       query[:, :].rearrange("p (c t) -> p c t", t=64),
                                                       op["a3_heads"][:, 2 * h + b:2 * h + b + 1], None, ALU.mult)
                last.then_inc(query_b_ready, 1)

            def quad(u, q, more, more2):
                if more:
                    spread_queries(1 - u, q + 1)

            spread_queries(0, 0)
            loop(pool, quad)


def experts3(chip):
    nc, op, ident = chip.nc, chip.operand, chip.operand["ident"]
    groups = E3 * F3 // P
    with ExitStack() as ctx:
        def sb(n, shape, dt=F32):
            return ctx.enter_context(nc.sbuf_tensor(f"f3_{n}", shape, dt))

        def sem(n):
            return chip.semaphore(f"f3_{n}")

        norm = Norm(chip, ctx, "f3_norm")
        xn = sb("xn", [P, 2, QN])
        shut = sb("shut", [P, groups * P], BF16)
        scores = sb("scores", [P, 2, 6 * E3])
        rank = sb("rank", [P, 2, 6 * E3])
        equal, ranked = sb("equal", [P, 12, E3]), sb("ranked", [P, 12, E3])
        best, first = sb("best", [P, 12]), sb("first", [P, 12])
        hot = sb("hot", [P, 12, 2 * E3])
        hot_t = sb("hot_t", [P, 2, QN])
        hot_b = sb("hot_b", [P, 2, QN], BF16)
        hid = sb("hid", [P, 2, 2, 2, QN])
        final = sb("final", [P, 2, QN])
        tokens = sb("tokens", [P, 2, 3, 2, D])

        set_up = sem("set_up")
        scored, hot_ready, hot_done = sem("scored"), sem("hot_ready"), sem("hot_done")
        hot_t_ready, hot_b_ready = sem("hot_t_ready"), sem("hot_b_ready")
        steps = [sem(f"step{n}") for n in range(5)]
        hid_done, hid_act, hid_dve, used = (
            [sem(f"{n}{g}") for g in range(groups)] for n in ("hid_done", "hid_act", "hid_dve", "used"))
        final_ready, final_done, tokens_ready = sem("final_ready"), sem("final_done"), sem("tokens_ready")
        stored = [sem(f"stored{u}") for u in range(2)]

        block = ctx.enter_context(nc.Block())

        @block.tensor
        def _(pe):
            pe.wait_ge(set_up, 3)

            def body(it):
                lanes = [(u, 2 * it + u) for u in range(2)]
                for u, q in lanes:
                    if not (isinstance(it, int) and it == 0):
                        pe.wait_ge(tokens_ready, q - 1)
                    norm.centre(u, chip.h_quad(q))
                for u, q in lanes:
                    norm.average(pe, u, q)
                for u, q in lanes:
                    pe.wait_ge(norm.ready, q + 1)
                    for j in range(3):
                        for b in range(2):
                            last = nc.tensor.matmul(chip.bank(u, 2)[:, (2 * j + b) * E3:(2 * j + b + 1) * E3],
                                                    xn[:, u, j * P:(j + 1) * P],
                                                    op["f3_rw"][:, b * D:b * D + E3], start=True, stop=True)
                    last.then_inc(scored, 1)
                for u, q in lanes:
                    pe.wait_ge(hot_ready, it + 1)
                    for j in range(3):
                        last = nc.tensor.transpose(chip.bank(u, 3)[:, j * P:(j + 1) * P],
                                                   hot[:, 6 * u + 2 * j:6 * u + 2 * j + 2, :]
                                                   .rearrange("p g e -> p (g e)"), ident)
                    last.then_inc(hot_done, 1)

                def hidden(g):
                    for u, q in lanes:
                        if g:
                            pe.wait_ge(hid_act[g - 1], q + 1)
                            pe.wait_ge(hid_dve[g - 1], q + 1)
                        for b in range(2):
                            half = slice(64 * b, 64 * b + 64)
                            nc.tensor.matmul(chip.bank(u, b)[:, 0:QN], op["f3_w1"][half, g * P:(g + 1) * P],
                                             xn[half, u, :], start=True, stop=False)
                            last = nc.tensor.matmul(chip.bank(u, b)[:, 0:QN], shut[half, g * P:(g + 1) * P],
                                                    hot_b[half, u, :], start=False, stop=True)
                        last.then_inc(hid_done[g], 1)

                for u, q in lanes:
                    pe.wait_ge(hot_b_ready, q + 1)
                    pe.wait_ge(hot_t_ready, q + 1)
                    nc.tensor.matmul(chip.bank(u, 3)[:, 0:QN], op["f3_b2"], hot_t[:, u, :],
                                     start=True, stop=False, skip_group_check=True)
                hidden(0)
                for g in range(groups):
                    if g + 1 < groups:
                        hidden(g + 1)
                    for u, q in lanes:
                        pe.wait_ge(hid_act[g], q + 1)
                        pe.wait_ge(hid_dve[g], q + 1)
                        for b in range(2):
                            last = nc.tensor.matmul(chip.bank(u, 3)[64 * b:64 * b + 64, 0:QN],
                                                    op["f3_w2"][:, g * D:(g + 1) * D], hid[:, u, g % 2, b, :],
                                                    start=False, stop=(g == groups - 1), skip_group_check=True)
                        last.then_inc(used[g], 1)
                for u, q in lanes:
                    pe.wait_ge(final_ready, q + 1)
                    for j in range(3):
                        last = nc.tensor.transpose(chip.bank(u, 2)[:, j * P:(j + 1) * P],
                                                   final[:, u, j * P:(j + 1) * P], ident)
                    last.then_inc(final_done, 1)

            chip.loop(pe, body)

        @block.scalar
        def _(act):
            nc.scalar.preload_act_table_set("natural_log_exp_and_others")
            def body(it):
                lanes = [(u, 2 * it + u) for u in range(2)]
                for u, q in lanes:
                    norm.squares(act, u, q)
                for u, q in lanes:
                    norm.logs(act, u, q)
                for u, q in lanes:
                    norm.powers(act, u, q)
                for u, q in lanes:
                    act.wait_ge(hot_done, q + 1)
                    nc.scalar.activation(hot_b[:, u, :], chip.bank(u, 3)[:, 0:QN], ACT.Copy).then_inc(hot_b_ready, 1)
                    nc.scalar.activation(hot_t[:, u, :], chip.bank(u, 3)[:, 0:QN], ACT.Copy).then_inc(hot_t_ready, 1)
                for g in range(groups):
                    for u, q in lanes:
                        act.wait_ge(hid_done[g], q + 1)
                        if g >= 2:
                            act.wait_ge(used[g - 2], q + 1)
                        nc.scalar.activation(hid[:, u, g % 2, 0, :], chip.bank(u, 0)[:, 0:QN], ACT.Relu,
                                             bias=op["f3_b1"][:, g:g + 1]).then_inc(hid_act[g], 1)
                for u, q in lanes:
                    act.wait_ge(final_done, q + 1)
                    if not (isinstance(it, int) and it == 0):
                        act.wait_ge(stored[u], 64 * it)
                    nc.scalar.activation(tokens[:, u, :, :, :], chip.bank(u, 2)[:, 0:QN]
                                         .rearrange("p (j b d) -> p j b d", j=3, b=2), ACT.Copy).then_inc(tokens_ready, 1)

            chip.loop(act, body)

        @block.vector
        def _(dve):
            nc.vector.tensor_copy(shut[:, :], op["f3_shut"]).then_inc(set_up, 1)
            nc.vector.memset(hot[:, :, :], 0.0).then_inc(set_up, 1)
            for u in range(2):
                last = nc.vector.tensor_copy(rank[:, u, :], op["f3_rank"])
            last.then_inc(set_up, 1)
            dve.wait_ge(set_up, 3)

            def body(it):
                lanes = [(u, 2 * it + u) for u in range(2)]
                for u, q in lanes:
                    norm.scale(dve, u, q, xn[:, u, :])
                for u, q in lanes:
                    dve.wait_ge(scored, q + 1)
                    last = nc.vector.tensor_tensor(scores[:, u, :], chip.bank(u, 2)[:, 0:6 * E3], op["f3_rb"], ALU.add)
                last.then_inc(steps[0], 1)
                flat = scores[:, :, :].rearrange("p u (g e) -> p (u g) e", e=E3)
                ranks = rank[:, :, :].rearrange("p u (g e) -> p (u g) e", e=E3)
                dve.wait_ge(steps[0], it + 1)
                nc.vector.tensor_reduce(best[:, :], flat, X, ALU.max).then_inc(steps[1], 1)
                dve.wait_ge(steps[1], it + 1)
                nc.vector.tensor_tensor(equal[:, :, :], flat, best[:, :].unsqueeze(2).to_broadcast([P, 12, E3]),
                                        ALU.is_equal).then_inc(steps[2], 1)
                dve.wait_ge(steps[2], it + 1)
                nc.vector.tensor_tensor(ranked[:, :, :], equal[:, :, :], ranks, ALU.mult).then_inc(steps[3], 1)
                dve.wait_ge(steps[3], it + 1)
                nc.vector.tensor_reduce(first[:, :], ranked[:, :, :], X, ALU.max).then_inc(steps[4], 1)
                dve.wait_ge(steps[4], it + 1)
                nc.vector.tensor_tensor(hot[:, :, 0:E3], ranks, first[:, :].unsqueeze(2).to_broadcast([P, 12, E3]),
                                        ALU.is_equal).then_inc(hot_ready, 1)
                for g in range(groups):
                    for u, q in lanes:
                        dve.wait_ge(hid_done[g], q + 1)
                        if g >= 2:
                            dve.wait_ge(used[g - 2], q + 1)
                        nc.vector.tensor_scalar(hid[:, u, g % 2, 1, :], chip.bank(u, 1)[:, 0:QN],
                                                op["f3_b1"][:, g:g + 1], 0.0, ALU.add, ALU.max).then_inc(hid_dve[g], 1)
                for u, q in lanes:
                    dve.wait_ge(used[groups - 1], q + 1)
                    nc.vector.scalar_tensor_tensor(final[:, u, :], chip.bank(u, 3)[:, 0:QN], 0.0, chip.h_quad(q),
                                                   ALU.max, ALU.add).then_inc(final_ready, 1)

            chip.loop(dve, body)

        @block.sync
        def _(sp):
            def body(it):
                lanes = [(u, 2 * it + u) for u in range(2)]
                for u, q in lanes:
                    sp.wait_ge(tokens_ready, q + 1)
                    for chunk, rows, pair, t in ((0, slice(0, 128), 0, 0), (1, slice(0, 64), 0, 128),
                                                 (1, slice(64, 128), 1, 0), (2, slice(0, 128), 1, 64)):
                        n = rows.stop - rows.start
                        out = chip.out[bass.ds(4 * q + 2 * pair, 2), t:t + n, :].rearrange("b t d -> t b d")
                        sp.dma_start(out, tokens[rows, u, chunk, :, :]).then_inc(stored[u], 16)

            chip.loop(sp, body)
            for u in range(2):
                sp.wait_ge(stored[u], 64 * (chip.quads // 2))


def build(nc, images, tokens, neighbours, embed, pack_a, pack_b, pack_c, routes, out, quads=BATCH // 4):
    with ExitStack() as ctx:
        def sb(n, shape, dt=F32):
            return ctx.enter_context(nc.sbuf_tensor(f"{n}_sbuf", shape, dt))

        hidden = sb("hidden", [P, 2 * quads * T])
        eps = sb("eps", [P, 1])
        weights_b = sb("weights_b", [P, columns(PACK_B)[1]])
        psum = ctx.enter_context(nc.psum_tensor("psum", [P, 8, 512], F32))
        chip = Chip(nc, quads, hidden, psum, eps)
        chip.place(PACK_B, weights_b)
        chip.routes = sb("routes", [1, E1 * 4], I32)
        chip.out = out
        loaded = ctx.enter_context(nc.semaphore("loaded"))

        with ExitStack() as first:
            chip.tokens = first.enter_context(nc.sbuf_tensor("tokens_sbuf", [TT, BATCH], I32))
            chip.embed = first.enter_context(nc.sbuf_tensor("embed_sbuf", [32, 32 * D], F32))
            weights_a = first.enter_context(nc.sbuf_tensor("weights_a", [P, columns(PACK_A)[1]], F32))
            chip.place(PACK_A, weights_a)
            with nc.Block() as block:
                @block.vector
                def _(dve):
                    nc.vector.memset(eps[:, :], EPS)

                @block.sync
                def _(sp):
                    sp.dma_start(chip.tokens[:, :], tokens).then_inc(loaded, 16)
                    sp.dma_start(chip.embed[:, :], embed).then_inc(loaded, 16)
                    sp.dma_start(weights_a[:, :], pack_a).then_inc(loaded, 16)
                    sp.dma_start(weights_b[:, :], pack_b).then_inc(loaded, 16)
                    sp.dma_start(chip.routes[:, :], routes).then_inc(loaded, 16)
                    sp.wait_ge(loaded, 80)
            embedding(chip, images, neighbours)
            chip.end_phase()

        attention(chip, "a0", 1.0, D ** -0.5)
        chip.end_phase()
        experts0(chip)
        chip.end_phase()
        linear_attention(chip)
        chip.end_phase()
        weights_c = sb("weights_c", [P, columns(PACK_C)[1]])
        chip.place(PACK_C, weights_c)
        with nc.Block() as block:
            @block.sync
            def _(sp):
                sp.dma_start(weights_c[:, :], pack_c).then_inc(loaded, 16)
                sp.wait_ge(loaded, 96)
        routed(chip)
        chip.end_phase()
        attention(chip, "a2", D ** -0.5, 1.0)
        chip.end_phase()
        experts2(chip)
        chip.end_phase()
        heads_attention(chip)
        chip.end_phase()
        experts3(chip)
        chip.end_phase()



def twice(a):
    out = np.zeros((P,) + a.shape[1:], np.float32)
    out[:a.shape[0]] = a
    out[64:64 + a.shape[0]] = a
    return out


def diagonal(a, rows=64, cols=None):
    cols = a.shape[1] if cols is None else cols
    out = np.zeros((P, 2 * cols), np.float32)
    for b in range(2):
        out[b * rows:b * rows + a.shape[0], b * cols:b * cols + a.shape[1]] = a
    return out


def placed(a):
    out = np.zeros((P, 4, P), np.float32)
    for g in range(2):
        for b in range(2):
            out[64 * g:64 * g + 64, 2 * g + b, 64 * b:64 * b + 64] = a
    return out.reshape(P, 4 * P)


def spread(a, n=6):
    return np.tile(np.asarray(a).reshape(1, -1), (P, n))


def filters():
    def haar(n, sign):
        m = np.zeros((n // 2, n))
        m[np.arange(n // 2), 2 * np.arange(n // 2)] = 0.7071067811865476
        m[np.arange(n // 2), 2 * np.arange(n // 2) + 1] = sign * 0.7071067811865476
        return m

    def resize(n):
        step = n / 8
        at = (np.arange(8)[:, None] + 0.5) * step - 0.5
        w = np.maximum(0, 1 - np.abs(at - np.arange(n)[None, :]) / step)
        return w / w.sum(axis=1, keepdims=True)

    low = haar(IMG, 1)
    return np.stack([resize(56) @ haar(HALF, 1) @ low, resize(56) @ haar(HALF, -1) @ low,
                     resize(112) @ low, resize(112) @ haar(IMG, -1)])


def pack(which, parts):
    where, width = columns(which)
    out = np.zeros((P, width), np.float32)
    for name, (at, n) in where.items():
        a = np.asarray(parts[name])
        a = a.reshape(a.shape[0], -1)
        assert a.shape[1] == n, (name, a.shape, n)
        out[:a.shape[0], at:at + n] = a
    return out


def pack_operands(**w):
    w = {k: np.asarray(v) for k, v in w.items()}
    f = filters().reshape(32, IMG)
    eye = np.eye(P)
    parts = {
        "rows": f.reshape(32, HALF, 2).transpose(1, 2, 0).reshape(HALF, 64),
        "cols": f.reshape(32, 2, HALF).transpose(2, 1, 0).reshape(HALF, 64),
        "tok_b": twice(w["L0_tok_b"][:, None]),
        "taps": np.concatenate([eye * t for t in (0.1, 0.2, 0.4, 0.2, 0.1)], axis=1),
        "ident": eye,
        "centre": diagonal(np.eye(D) - 1 / D),
        "mean": diagonal(np.full((D, D), 1 / D)),
    }
    for n, layer in (("a0", "L0"), ("a2", "L2")):
        parts[f"{n}_wk"] = diagonal(w[f"{layer}_attn_Wk"])
        parts[f"{n}_wq"] = diagonal(w[f"{layer}_attn_Wq"])
        parts[f"{n}_wv"] = placed(w[f"{layer}_attn_Wv"].T)
    parts |= {
        "f0_gate_w": diagonal(w["L0_ffn_gate_w"]), "f0_gate_b": spread(w["L0_ffn_gate_b"]),
        "f0_rank": spread(np.arange(E0, 0, -1)),
        "f0_w1": twice(w["L0_ffn_w1"].transpose(1, 0, 2).reshape(D, -1)),
        "f0_b1": w["L0_ffn_b1"].T,
        "f0_w2": w["L0_ffn_w2"].transpose(1, 0, 2).reshape(F0, -1),
        "f0_b2": np.tile(diagonal(w["L0_ffn_b2"], rows=E0)[0:2 * E0], (3, 1)),
        "f0_pick": np.tile(np.eye(2 * E0).reshape(2 * E0, 2, E0).transpose(0, 2, 1).reshape(2 * E0, -1), (3, 1)),
        "f0_gamma": twice(w["L0_ffn_gamma"][:, None]), "f0_beta": twice(w["L0_ffn_beta"][:, None]),
        "a1_wq": diagonal(w["L1_attn_Wqkv"][:, 0:64]), "a1_wk": diagonal(w["L1_attn_Wqkv"][:, 64:128]),
        "a1_wv": diagonal(w["L1_attn_Wqkv"][:, 128:192]), 
        "a1_wo": np.stack([diagonal(np.tile(w["L1_attn_Wout"][8 * jr:8 * jr + 8], (8, 1))) for jr in range(8)], axis=1),
        "a1_heads": np.kron(np.eye(16), np.ones((8, 8))),
        "a1_head": np.kron(np.ones((2, 1)), np.kron(np.eye(8), np.ones((8, 1)))),
        "a1_bo": twice(w["L1_attn_bout"][:, None]),
        "a1_gamma": twice(w["L1_attn_gamma"][:, None]), "a1_beta": twice(w["L1_attn_beta"][:, None]),
        "f1_wi": twice(w["L1_ffn_Wi"].T), "f1_bi": w["L1_ffn_bi"][:, None],
        "f1_wr": w["L1_ffn_Wr"].transpose(3, 0, 1, 2).reshape(F1, -1),
        "f1_br": w["L1_ffn_br"].transpose(2, 0, 1).reshape(F1, -1),
        "f1_ws": w["L1_ffn_Ws"][:, 0].transpose(2, 0, 1).reshape(F1, -1),
        "f1_bs": w["L1_ffn_bs"][:, 0].T,
        "f1_wo": w["L1_ffn_Wo"].T, "f1_bo": twice(w["L1_ffn_bo"][:, None]),
        "f2_rw1": diagonal(w["L2_ffn_router_w1"]),
        "f2_rb1": np.concatenate([w["L2_ffn_router_b1"]] * 2)[:, None],
        "f2_rw2": diagonal(w["L2_ffn_router_w2"], rows=R2), "f2_rb2": spread(w["L2_ffn_router_b2"], 12),
        "f2_rank": spread(np.arange(E2, 0, -1)),
        "f2_w1": twice(w["L2_ffn_expert_w1"].transpose(1, 0, 2).reshape(D, -1)),
        "f2_b1": w["L2_ffn_expert_b1"].reshape(3, P).T, "f2_b2": w["L2_ffn_expert_b2"].reshape(3, P).T,
        "f2_b3": np.tile(diagonal(w["L2_ffn_expert_b3"], rows=E2)[0:2 * E2], (3, 1)),
        "f2_pick": np.tile(np.eye(2 * E2).reshape(2 * E2, 2, 3, 2).transpose(0, 2, 1, 3).reshape(2 * E2, -1), (3, 1)),
        "a3_wq": diagonal(w["L3_attn_Wq"].T), "a3_bq": twice(w["L3_attn_bq"][:, None]),
        "a3_wk": diagonal(w["L3_attn_Wk"].T), "a3_bk": twice(w["L3_attn_bk"][:, None]),
        "a3_wv": diagonal(w["L3_attn_Wv"].T), "a3_bv": spread(w["L3_attn_bv"], 2),
        "a3_wo": diagonal(w["L3_attn_Wo"].T), "a3_bo": twice(w["L3_attn_bo"][:, None]),
        "a3_heads": np.eye(2 * HEADS3).reshape(2, HEADS3, 2, HEADS3).transpose(0, 1, 3, 2)
        .reshape(2 * HEADS3, 2 * HEADS3).repeat(D // HEADS3, axis=0),
        "f3_rw": diagonal(w["L3_ffn_router_w"].T, cols=64),
        "f3_rb": spread(w["L3_ffn_router_b"]), "f3_rank": spread(np.arange(E3, 0, -1)),
        "f3_w1": twice(w["L3_ffn_W1"].transpose(1, 0, 2).reshape(D, -1)),
        "f3_b1": w["L3_ffn_b1"].reshape(4, P).T,
        "f3_shut": twice(-BIG * (1 - np.kron(np.eye(E3), np.ones((1, F3))))),
        "f3_w2": w["L3_ffn_W2"].reshape(4, P, D).transpose(1, 0, 2).reshape(P, -1),
        "f3_b2": diagonal(w["L3_ffn_b2"]),
    }
    w2 = np.zeros((3, P, P), np.float32)
    for e in range(E2):
        half = slice(64 * (e % 2), 64 * (e % 2) + 64)
        w2[e // 2, half, half] = w["L2_ffn_expert_w2"][e]
    parts["f2_w2"] = w2.transpose(1, 0, 2)
    parts["f2_w3"] = w["L2_ffn_expert_w3"].reshape(3, P, D).transpose(1, 0, 2)
    maps = {(0, 0): 0, (1, 0): 1, (0, 1): 2, (1, 1): 3, (3, 2): 4, (2, 3): 5, (3, 3): 6}
    embed = np.zeros((4, 8, 8, 4, D), np.float32)
    for (rt, ct), m in maps.items():
        for cj in range(8):
            embed[ct, cj, cj, rt] = w["L0_tok_W"][m]
    emb = w["L0_txt_emb"]
    near = np.clip(np.arange(VOCAB)[:, None] + np.arange(TAPS) - TAPS // 2, 0, VOCAB - 1)
    return {
        "images": w["x"], "tokens": np.ascontiguousarray(w["x_txt"].T),
        "neighbours": emb[near].reshape(VOCAB, TAPS * D), "embed": embed.reshape(32, -1),
        "pack_a": pack(PACK_A, parts), "pack_b": pack(PACK_B, parts), "pack_c": pack(PACK_C, parts),
        "routes": w["L1_ffn_route_id"].reshape(1, -1),
    }


def kernel(**inputs):
    import concourse.bacc as bacc
    from concourse.bass_utils import run_bass_kernel_spmd as run

    nc = bacc.Bacc("TRN2", target_bir_lowering=False, num_devices=1)
    operands = pack_operands(**inputs)
    names = ("images", "tokens", "neighbours", "embed", "pack_a", "pack_b", "pack_c", "routes")
    arrays = {n: np.ascontiguousarray(operands[n]) for n in names}
    args = [nc.dram_tensor(n, a.shape, mybir.dt.from_np(a.dtype), kind="ExternalInput").ap()
            for n, a in arrays.items()]
    out = nc.dram_tensor("out", (BATCH, T, D), F32, kind="ExternalOutput").ap()
    build(nc, *args, out)
    return run(nc, [arrays], core_ids=[0]).results[0]["out"]
```

```python
from contextlib import ExitStack

import numpy as np

import concourse.bass as bass
from concourse import mybir

F32 = mybir.dt.float32
BF16 = mybir.dt.bfloat16
I32 = mybir.dt.int32
ALU = mybir.AluOpType
ACT = mybir.ActivationFunctionType
X = mybir.AxisListType.X

P = 128
BATCH, T, D = 128, 192, 64
IMG, TI, TT = 224, 64, 128
HALF = IMG // 2
VOCAB, TAPS = 12500, 5
TAP_WEIGHTS = (0.1, 0.2, 0.4, 0.2, 0.1)
QN = 2 * T
E0, F0 = 16, 128
E1, F1 = 16, 128
E2, R2 = 6, 32
E3, F3 = 32, 16
HEADS3 = 4
BIG = 1e30
EPS = 1e-5

PACK_A = [("rows", 64), ("cols", 64), ("tok_b", 1), ("ident_a", P)]
PACK_B = [("ident", P), ("centre", P), ("mean", P),
          ("a0_wk", P), ("a0_wq", P), ("a0_wv", P),
          ("f0_gate_w", 2 * E0), ("f0_gate_b", 6 * E0), ("f0_rank", 6 * E0),
          ("f0_w1", E0 * F0), ("f0_b1", E0), ("f0_w2", E0 * D), ("f0_b2", P), ("f0_pick", 2 * E0),
          ("f0_gamma", 1), ("f0_beta", 1),
          ("a1_wq", P), ("a1_wk", P), ("a1_wv", P), ("a1_wo", 8 * P), ("a1_heads", P), ("a1_head", 8),
          ("a1_bo", 1), ("a1_gamma", 1), ("a1_beta", 1)]
PACK_C = [("f1_wi", F1), ("f1_bi", 1), ("f1_wr", 2 * E1 * F1), ("f1_br", 2 * E1),
          ("f1_ws", 2 * F1), ("f1_bs", 2), ("f1_wo", D), ("f1_bo", 1),
          ("a2_wk", P), ("a2_wq", P), ("a2_wv", P),
          ("f2_rw1", 2 * R2), ("f2_rb1", 1), ("f2_rw2", 2 * E2), ("f2_rb2", 12 * E2), ("f2_rank", 6 * E2),
          ("f2_w1", 3 * P), ("f2_b1", 3), ("f2_w2", 3 * P), ("f2_b2", 3), ("f2_w3", 3 * D), ("f2_b3", P), ("f2_pick", 2 * E2),
          ("a3_wq", P), ("a3_bq", 1), ("a3_wk", P), ("a3_bk", 1), ("a3_wv", P), ("a3_bv", P),
          ("a3_wo", P), ("a3_bo", 1), ("a3_heads", 2 * HEADS3),
          ("f3_rw", 2 * D), ("f3_rb", 6 * E3), ("f3_rank", 6 * E3),
          ("f3_w1", 4 * P), ("f3_b1", 4), ("f3_shut", 4 * P), ("f3_w2", 4 * D), ("f3_b2", P)]


def columns(pack):
    at, where = 0, {}
    for name, n in pack:
        where[name] = (at, n)
        at += n
    return where, at


class Chip:

    def __init__(self, nc, quads, hidden, psum, eps):
        self.nc, self.quads, self.hidden, self.psum, self.eps = nc, quads, hidden, psum, eps
        self.operand = {}
        self.semaphores = []

    def semaphore(self, name):
        self.semaphores.append(self.nc.alloc_semaphore(name))
        return self.semaphores[-1]

    def end_phase(self):
        self.nc.clear_and_free_semaphores(self.semaphores)
        self.nc.all_engine_barrier()
        self.semaphores = []

    def place(self, pack, tile):
        for name, (at, n) in columns(pack)[0].items():
            self.operand[name] = tile[:, at:at + n]

    def bank(self, u, i):
        return self.psum[:, 4 * u + i, :]

    def h_quad(self, q):
        return self.hidden[:, bass.ds(q * QN, QN)]

    def loop(self, eng, body):
        body(0)
        if self.quads > 2:
            with eng.Fori(1, self.quads // 2) as it:
                body(it)


def embedding(chip, images, neighbours):
    nc, op, ident = chip.nc, chip.operand, chip.operand["ident_a"]
    group, side = 16, 8

    with ExitStack() as ctx:
        def sb(n, shape, dt=F32):
            return ctx.enter_context(nc.sbuf_tensor(f"emb_{n}", shape, dt))

        def sem(n):
            return chip.semaphore(f"emb_{n}")

        image = sb("image", [HALF, 4, 8, 2 * IMG])
        by_row = sb("by_row", [P, 2, 2, 2 * IMG])
        columns_of = sb("columns_of", [HALF, 2, 2, 512])
        maps = sb("maps", [P, 2, 2, 2, 4, side])
        gathered = sb("gathered", [P, 2, group, TAPS * D])
        text = sb("text", [P, 2, group, D])
        index = sb("index", [TT, 2, group], I32)
        indexed, pool_passed = sem("indexed"), sem("pool_passed")
        loaded = [sem(f"loaded_{s}") for s in range(4)]
        fetched = [sem(f"fetched_{u}") for u in range(2)]
        rows_done, by_row_act, by_row_dve = sem("rows_done"), sem("by_row_act"), sem("by_row_dve")
        turned, columns_act, columns_dve = sem("turned"), sem("columns_act"), sem("columns_dve")
        cols_done, maps_ready, embedded, image_placed = (
            sem("cols_done"), sem("maps_ready"), sem("embedded"), sem("image_placed"))
        summed, text_ready, text_turned = sem("summed"), sem("text_ready"), sem("text_turned")
        text_act, text_dve = sem("text_act"), sem("text_dve")

        block = ctx.enter_context(nc.Block())

        def first(it):
            return isinstance(it, int) and it == 0

        def loop(eng, body):
            body(0)
            if chip.quads > 8:
                with eng.Fori(1, chip.quads // 8) as it:
                    body(it)

        def pairs_of(k):
            return chip.hidden[:, bass.ds(k * 8 * T, 8 * T)].rearrange("p (g t) -> p g t", t=T)

        def load(eng, it, half):
            for u in range(2):
                k = 2 * it + u
                if not first(it):
                    eng.wait_ge(rows_done, k - 1)
                some = images[bass.ds(k * group + 8 * half, 8), :, :, :]
                eng.dma_start(image[:, 2 * u + half, :, :],
                              some.rearrange("i o (p a) c -> p (i o) (a c)", a=2)).then_inc(loaded[2 * u + half], 16)

        @block.sync
        def _(sp):
            loop(sp, lambda it: load(sp, it, 0))

        @block.gpsimd
        def _(pool):
            def body(it):
                for u in range(2):
                    k = 2 * it + u
                    if not first(it):
                        pool.wait_ge(text_ready, k - 1)
                    pool.sem_inc(pool_passed, 1)
                    nc.gpsimd.tensor_copy(index[:, u, :], chip.tokens[:, bass.ds(k * group, group)]).then_inc(indexed, 1)
                    pool.wait_ge(indexed, k + 1)
                    pool.sem_inc(pool_passed, 1)
                    for j in range(group):
                        nc.gpsimd.indirect_dma_start(
                            gathered[:, u, j, :], None, neighbours,
                            bass.IndirectOffsetOnAxis(ap=index[:, u, j:j + 1], axis=0),
                        ).then_inc(fetched[u], 16)

            loop(pool, body)

        @block.tensor
        def _(pe):
            def body(it):
                lanes = [(u, 2 * it + u) for u in range(2)]
                for u, k in lanes:
                    if not first(it):
                        pe.wait_ge(text_act, k - 1)
                        pe.wait_ge(text_dve, k - 1)
                    for h in range(2):
                        pe.wait_ge(loaded[2 * u + h], 16 * (it + 1))
                        for t in range(4):
                            for a in range(2):
                                last = nc.tensor.matmul(
                                    chip.bank(u, h)[32 * t:32 * t + 32, 0:2 * IMG]
                                    .rearrange("p (b c) -> p b c", b=2), op["rows"][0:HALF, a * 32:(a + 1) * 32],
                                    image[:, 2 * u + h, 2 * t:2 * t + 2, a * IMG:(a + 1) * IMG],
                                    start=(a == 0), stop=(a == 1))
                    last.then_inc(rows_done, 1)
                for u, k in lanes:
                    pe.wait_ge(by_row_act, k + 1)
                    pe.wait_ge(by_row_dve, k + 1)
                    if not first(it):
                        pe.wait_ge(image_placed, k - 1)
                    for ch in range(2):
                        for h in range(2):
                            for b in range(2):
                                last = nc.tensor.transpose(
                                    chip.bank(u, 2 + ch)[0:HALF, (2 * h + b) * P:(2 * h + b + 1) * P],
                                    by_row[:, u, h, b * IMG + ch * HALF:b * IMG + (ch + 1) * HALF], ident)
                    last.then_inc(turned, 1)
                for u, k in lanes:
                    pe.wait_ge(columns_act, k + 1)
                    pe.wait_ge(columns_dve, k + 1)
                    for rt in range(4):
                        for ch in range(2):
                            filtered = columns_of[:, u, ch, :].rearrange("p (i r c) -> p r i c", r=4, c=side)[:, rt, :, :]
                            last = nc.tensor.matmul(chip.bank(u, 2)[32 * rt:32 * rt + 32, 0:P],
                                                    op["cols"][0:HALF, ch * 32:(ch + 1) * 32], filtered,
                                                    start=(ch == 0), stop=(ch == 1))
                    last.then_inc(cols_done, 1)
                for u, k in lanes:
                    pe.wait_ge(maps_ready, k + 1)
                    for cj in range(side):
                        for b in range(2):
                            last = nc.tensor.matmul(chip.bank(u, 3)[64 * b:64 * b + 64, cj * 64:(cj + 1) * 64],
                                                    chip.embed[:, cj * D:(cj + 1) * D], maps[:, u, :, b, :, :],
                                                    start=True, stop=True)
                    last.then_inc(embedded, 1)
                for u, k in lanes:
                    pe.wait_ge(text_ready, k + 1)
                    for g in range(8):
                        last = nc.tensor.transpose(chip.bank(u, g // 4)[:, g % 4 * TT:(g % 4 + 1) * TT],
                                                   text[:, u, 2 * g:2 * g + 2, :].rearrange("p b d -> p (b d)"), ident)
                    last.then_inc(text_turned, 1)

            loop(pe, body)

        @block.scalar
        def _(act):
            def body(it):
                lanes = [(u, 2 * it + u) for u in range(2)]
                load(act, it, 1)
                for u, k in lanes:
                    act.wait_ge(rows_done, k + 1)
                    nc.scalar.activation(by_row[:, u, 0, :], chip.bank(u, 0)[:, 0:2 * IMG], ACT.Copy).then_inc(by_row_act, 1)
                for u, k in lanes:
                    act.wait_ge(turned, k + 1)
                    nc.scalar.activation(columns_of[:, u, 0, :], chip.bank(u, 2)[0:HALF, :], ACT.Copy).then_inc(columns_act, 1)
                for u, k in lanes:
                    act.wait_ge(cols_done, k + 1)
                    nc.scalar.activation(maps[:, u, :, :, :, :].rearrange("p h b t r -> p (h b t r)"),
                                         chip.bank(u, 2)[:, 0:P], ACT.Copy).then_inc(maps_ready, 1)
                for u, k in lanes:
                    act.wait_ge(text_turned, k + 1)
                    nc.scalar.activation(pairs_of(k)[:, 0:4, TI:T],
                                         chip.bank(u, 0).rearrange("p (g t) -> p g t", t=TT),
                                         ACT.Copy).then_inc(text_act, 1)

            loop(act, body)

        @block.vector
        def _(dve):
            def body(it):
                lanes = [(u, 2 * it + u) for u in range(2)]
                for u, k in lanes:
                    dve.wait_ge(rows_done, k + 1)
                    nc.vector.tensor_copy(by_row[:, u, 1, :], chip.bank(u, 1)[:, 0:2 * IMG]).then_inc(by_row_dve, 1)
                for u, k in lanes:
                    dve.wait_ge(turned, k + 1)
                    nc.vector.tensor_copy(columns_of[:, u, 1, :], chip.bank(u, 3)[0:HALF, :]).then_inc(columns_dve, 1)
                for u, k in lanes:
                    dve.wait_ge(embedded, k + 1)
                    nc.vector.tensor_scalar(pairs_of(k)[:, :, 0:TI].rearrange("p g (r c) -> p g c r", c=side),
                                            chip.bank(u, 3).rearrange("p (c g r) -> p g c r", c=side, g=8),
                                            op["tok_b"], None, ALU.add).then_inc(image_placed, 1)
                for u, k in lanes:
                    dve.wait_ge(fetched[u], 16 * group * (it + 1))
                    if not first(it):
                        dve.wait_ge(text_turned, k - 1)
                    for tap, weight in enumerate(TAP_WEIGHTS):
                        row = gathered[:, u, :, tap * D:(tap + 1) * D]
                        if tap == 0:
                            last = nc.vector.tensor_scalar(text[:, u, :, :], row, weight, None, ALU.mult)
                        else:
                            dve.wait_ge(summed, (TAPS - 1) * k + tap)
                            last = nc.vector.scalar_tensor_tensor(text[:, u, :, :], row, weight, text[:, u, :, :],
                                                                  ALU.mult, ALU.add)
                        last.then_inc(summed if tap < TAPS - 1 else text_ready, 1)
                for u, k in lanes:
                    dve.wait_ge(text_turned, k + 1)
                    nc.vector.tensor_copy(pairs_of(k)[:, 4:8, TI:T],
                                          chip.bank(u, 1).rearrange("p (g t) -> p g t", t=TT)).then_inc(text_dve, 1)

            loop(dve, body)


class Norm:

    def __init__(self, chip, ctx, tag, bank=None):
        nc = chip.nc
        self.chip, self.bank = chip, bank or chip.bank
        self.square = ctx.enter_context(nc.sbuf_tensor(f"{tag}_square", [P, 2, QN], F32))
        self.log = ctx.enter_context(nc.sbuf_tensor(f"{tag}_log", [P, 2, QN], F32))
        self.rstd = ctx.enter_context(nc.sbuf_tensor(f"{tag}_rstd", [P, 2, QN], F32))
        self.centred = chip.semaphore(f"{tag}_centred")
        self.squared = chip.semaphore(f"{tag}_squared")
        self.averaged = chip.semaphore(f"{tag}_averaged")
        self.logged = chip.semaphore(f"{tag}_logged")
        self.rstd_ready = chip.semaphore(f"{tag}_rstd_ready")
        self.ready = chip.semaphore(f"{tag}_ready")

    def centre(self, u, source):
        c = self.chip
        c.nc.tensor.matmul(self.bank(u, 0)[:, 0:QN], c.operand["centre"], source,
                           start=True, stop=True).then_inc(self.centred, 1)

    def squares(self, act, u, q):
        act.wait_ge(self.centred, q + 1)
        self.chip.nc.scalar.activation(self.square[:, u, :], self.bank(u, 0)[:, 0:QN],
                                       ACT.Square).then_inc(self.squared, 1)

    def average(self, pe, u, q):
        c = self.chip
        pe.wait_ge(self.squared, q + 1)
        c.nc.tensor.matmul(self.bank(u, 1)[:, 0:QN], c.operand["mean"], self.square[:, u, :],
                           start=True, stop=True).then_inc(self.averaged, 1)

    def logs(self, act, u, q):
        act.wait_ge(self.averaged, q + 1)
        self.chip.nc.scalar.activation(self.log[:, u, :], self.bank(u, 1)[:, 0:QN], ACT.Ln,
                                       bias=self.chip.eps[:, 0:1]).then_inc(self.logged, 1)

    def powers(self, act, u, q):
        act.wait_ge(self.logged, q + 1)
        self.chip.nc.scalar.activation(self.rstd[:, u, :], self.log[:, u, :], ACT.Exp,
                                       scale=-0.5).then_inc(self.rstd_ready, 1)

    def scale(self, dve, u, q, out):
        dve.wait_ge(self.rstd_ready, q + 1)
        self.chip.nc.vector.tensor_tensor(out, self.bank(u, 0)[:, 0:QN], self.rstd[:, u, :],
                                          ALU.mult).then_inc(self.ready, 1)


class Split:

    def __init__(self, chip, ctx, tag, weight):
        nc = chip.nc
        self.chip, self.weight = chip, weight
        width = weight.shape[1]

        def sb(n, shape, dt=BF16):
            return ctx.enter_context(nc.sbuf_tensor(f"{tag}_{n}", shape, dt))

        self.x_high, self.x_middle, self.x_low = (sb(n, [P, QN]) for n in ("x_high", "x_middle", "x_low"))
        self.x_rest = sb("x_rest", [P, QN], F32)
        self.x_parts = sb("x_parts", [P, 2, 2, 2, QN])
        self.w_rest = sb("w_rest", [P, width], F32)
        self.w_high, self.w_middle = sb("w_high", [P, width]), sb("w_middle", [P, width])
        self.w_mixed = sb("w_mixed", [P, 2, width])
        self.w_split, self.w_swapped = chip.semaphore(f"{tag}_w_split"), chip.semaphore(f"{tag}_w_swapped")
        self.x_split, self.passed = chip.semaphore(f"{tag}_x_split"), chip.semaphore(f"{tag}_passed")
        self.placed_act, self.placed_dve = chip.semaphore(f"{tag}_placed_act"), chip.semaphore(f"{tag}_placed_dve")

    def split_weight(self, dve):
        nc = self.chip.nc
        nc.vector.tensor_copy(self.w_high[:, :], self.weight).then_inc(self.w_split, 1)
        dve.wait_ge(self.w_split, 1)
        nc.vector.tensor_tensor(self.w_rest[:, :], self.weight, self.w_high[:, :], ALU.subtract).then_inc(self.w_split, 1)
        dve.wait_ge(self.w_split, 2)
        nc.vector.tensor_copy(self.w_middle[:, :], self.w_rest[:, :]).then_inc(self.w_split, 1)
        dve.wait_ge(self.w_split, 3)
        for b in range(2):
            half = slice(64 * b, 64 * b + 64)
            nc.vector.tensor_tensor(self.w_mixed[half, b, :], self.w_rest[half, :], self.w_middle[half, :],
                                    ALU.subtract).then_inc(self.w_split, 1)

    def swap_weight(self, act):
        act.wait_ge(self.w_split, 1)
        for b in range(2):
            half = slice(64 - 64 * b, 128 - 64 * b)
            self.chip.nc.scalar.activation(self.w_mixed[half, b, :], self.w_high[half, :],
                                           ACT.Copy).then_inc(self.w_swapped, 1)

    def split(self, pool, x, q):
        nc = self.chip.nc
        pool.sem_inc(self.passed, 1)
        yield nc.gpsimd.tensor_copy(self.x_high[:, :], x).then_inc(self.x_split, 1)
        pool.wait_ge(self.x_split, 4 * q + 1)
        yield nc.gpsimd.tensor_tensor(self.x_rest[:, :], x, self.x_high[:, :], ALU.subtract).then_inc(self.x_split, 1)
        pool.wait_ge(self.x_split, 4 * q + 2)
        pool.sem_inc(self.passed, 1)
        yield nc.gpsimd.tensor_copy(self.x_middle[:, :], self.x_rest[:, :]).then_inc(self.x_split, 1)
        pool.wait_ge(self.x_split, 4 * q + 3)
        yield nc.gpsimd.tensor_tensor(self.x_low[:, :], self.x_rest[:, :], self.x_middle[:, :],
                                      ALU.subtract).then_inc(self.x_split, 1)

    def place_high(self, dve, u, q):
        dve.wait_ge(self.x_split, 4 * q + 1)
        for b in range(2):
            half = slice(64 * b, 64 * b + 64)
            self.chip.nc.vector.tensor_copy(self.x_parts[half, u, b, :, :], self.x_high[half, :].unsqueeze(1)
                                            .to_broadcast([64, 2, QN])).then_inc(self.placed_dve, 1)

    def place_other(self, act, u, q, low):
        act.wait_ge(self.x_split, 4 * q + 3 + low)
        source = self.x_low if low else self.x_middle
        for b in range(2):
            self.chip.nc.scalar.activation(self.x_parts[64 - 64 * b:128 - 64 * b, u, b, low, :],
                                           source[64 * b:64 * b + 64, :], ACT.Copy).then_inc(self.placed_act, 1)

    def wait_weight(self, pe):
        pe.wait_ge(self.w_split, 5)
        pe.wait_ge(self.w_swapped, 2)

    def wait_x(self, pe, q):
        pe.wait_ge(self.placed_act, 4 * q + 4)
        pe.wait_ge(self.placed_dve, 2 * q + 2)

    def product(self, out, u, b, cols, stop):
        for n, (w, x) in enumerate(((self.w_high[:, cols], 0), (self.w_middle[:, cols], 0), (self.w_mixed[:, b, cols], 1))):
            last = self.chip.nc.tensor.matmul(out, w, self.x_parts[:, u, b, x, :], start=(n == 0), stop=(stop and n == 2))
        return last


def attention(chip, name, score_scale, value_scale):
    nc, op, ident = chip.nc, chip.operand, chip.operand["ident"]
    with ExitStack() as ctx:
        def sb(n, shape, dt=F32):
            return ctx.enter_context(nc.sbuf_tensor(f"{name}_{n}", shape, dt))

        def sem(n):
            return chip.semaphore(f"{name}_{n}")

        m_t = sb("m_t", [P, P])
        square, centred, log, rstd = sb("square", [P, QN]), sb("centred", [P, QN]), sb("log", [P, QN]), sb("rstd", [P, QN])
        xn = sb("xn", [P, 2, QN])
        xb = sb("xb", [P, 2, 6, 2, 64])
        ym = sb("ym", [P, 2, QN])
        value = sb("value", [P, 2, 2, P])
        value_z = sb("value_z", [P, 2, 2, P])
        peak = sb("peak", [P, 2, 3, 2])
        total = sb("total", [P, 2, 3, 2])
        inverse = sb("inverse", [P, 2, 3, 2])
        prob = sb("prob", [P, 2, 3, 2, T])
        even = sb("even", [P, 2, 3, 2, T])
        prob_t = sb("prob_t", [P, 2, 3, QN])

        m_done, m_ready, cleared, pool_passed = sem("m_done"), sem("m_ready"), sem("cleared"), sem("pool_passed")
        centre_done, square_ready, centred_ready, average_done, log_ready, rstd_ready, xn_ready = (sem(n) for n in (
            "centre_done", "square_ready", "centred_ready", "average_done", "log_ready", "rstd_ready", "xn_ready"))
        xb_ready, ym_done, ym_ready, value_done, value_ready = (sem(n) for n in (
            "xb_ready", "ym_done", "ym_ready", "value_done", "value_ready"))
        scored, peak_ready, exp_ready, inverse_ready, even_act, even_dve = (sem(n) for n in (
            "scored", "peak_ready", "exp_ready", "inverse_ready", "even_act", "even_dve"))
        prob_done, prob_act, prob_dve, mixed, h_ready = (sem(n) for n in (
            "prob_done", "prob_act", "prob_dve", "mixed", "h_ready"))

        spare = chip.psum[:, 7, 0:QN]

        def scores_of(u):
            return chip.psum[:, 3 * u:3 * u + 3, 0:QN].rearrange("p c (g t) -> p c g t", t=T)

        def below(q, n):
            return isinstance(q, int) and q < n

        def loop(eng, quad):
            turns = chip.quads // 2

            def both(it, last):
                for u in range(2):
                    quad(u, 2 * it + u, not (last and u == 1), not last)

            both(0, turns == 1)
            if turns > 2:
                with eng.Fori(1, turns - 1) as it:
                    both(it, False)
            if turns > 1:
                both(turns - 1, True)

        block = ctx.enter_context(nc.Block())

        @block.tensor
        def _(pe):
            def centre(q):
                if not below(q, 1):
                    pe.wait_ge(ym_ready, q)
                nc.tensor.matmul(spare, op["centre"], chip.h_quad(q), start=True, stop=True).then_inc(centre_done, 1)

            def average(q):
                pe.wait_ge(square_ready, q + 1)
                nc.tensor.matmul(spare, op["mean"], square[:, :], start=True, stop=True).then_inc(average_done, 1)

            def multiply_m(u, q):
                pe.wait_ge(xn_ready, q + 1)
                nc.tensor.matmul(spare, m_t[:, :], xn[:, u, :], start=True, stop=True).then_inc(ym_done, 1)

            def score(u, q):
                pe.wait_ge(xb_ready, q + 1)
                pe.wait_ge(ym_ready, q + 1)
                if not below(q, 2):
                    pe.wait_ge(prob_act, 2 * q - 2)
                    pe.wait_ge(prob_dve, q - 1)
                for c in range(3):
                    for pair in range(2):
                        last = nc.tensor.matmul(scores_of(u)[:, c, pair, :],
                                                xb[:, u, 3 * pair + c, :, :].rearrange("p b t -> p (b t)"),
                                                ym[:, u, pair * T:(pair + 1) * T], start=True, stop=True)
                last.then_inc(scored, 1)

            def turn(u, q):
                pe.wait_ge(even_dve, q + 1)
                pe.wait_ge(even_act, q + 1)
                for s in range(3):
                    for c in range(3):
                        probs = even[:, u, c, :, :].rearrange("p g t -> p (g t)")[:, s * P:(s + 1) * P]
                        last = nc.tensor.transpose(chip.psum[:, 3 * u + s, c * P:(c + 1) * P], probs, ident)
                last.then_inc(prob_done, 1)

            def mixing(u, q):
                pe.wait_ge(prob_act, 2 * q + 2)
                pe.wait_ge(prob_dve, q + 1)
                if below(q, chip.quads - 1) or not isinstance(q, int):
                    pe.wait_ge(value_ready, q + 2)
                for pair in range(2):
                    for middle in (False, True):
                        for b in range(2):
                            v = (value_z if middle else value)[:, u, pair, b * D:(b + 1) * D]
                            probs = prob_t[:, u, 1 if middle else 2 * pair, :].rearrange(
                                "p (c b t) -> p b c t", c=3, b=2)[:, b, :, :]
                            last = nc.tensor.matmul(
                                chip.psum[64 * b:64 * b + 64, 6, pair * T:(pair + 1) * T]
                                .rearrange("p (c t) -> p c t", c=3), v, probs,
                                start=(pair == 0 and not middle), stop=middle, skip_group_check=True)
                last.then_inc(mixed, 1)

            def values(u, q):
                if not below(q, 2):
                    pe.wait_ge(h_ready, q - 1)
                elif q == 1:
                    pe.wait_ge(value_ready, 1)
                for s in range(3):
                    last = nc.tensor.matmul(chip.psum[:, 6, s * P:(s + 1) * P], xn[:, u, s * P:(s + 1) * P],
                                            op[f"{name}_wv"], start=True, stop=True)
                last.then_inc(value_done, 1)

            def quad(u, q, more, more2):
                score(u, q)
                if more:
                    multiply_m(1 - u, q + 1)
                if not below(q, 2):
                    mixing(u, q - 2)
                if more2:
                    centre(q + 2)
                if not below(q, 1):
                    turn(1 - u, q - 1)
                values(u, q)
                if more2:
                    average(q + 2)

            nc.tensor.matmul(spare[:, 0:P], op[f"{name}_wk"], op[f"{name}_wq"], start=True, stop=True).then_inc(m_done, 1)
            pe.wait_ge(m_ready, 1)
            centre(0)
            average(0)
            multiply_m(0, 0)
            centre(1)
            average(1)
            loop(pe, quad)
            turn(1, chip.quads - 1)
            pe.wait_ge(value_ready, chip.quads)
            mixing(0, chip.quads - 2)
            pe.wait_ge(h_ready, chip.quads - 1)
            mixing(1, chip.quads - 1)

        @block.scalar
        def _(act):
            nc.scalar.preload_act_table_set("natural_log_exp_and_others")

            def squares(q):
                act.wait_ge(centred_ready, q + 1)
                nc.scalar.activation(square[:, :], centred[:, :], ACT.Square).then_inc(square_ready, 1)

            def deviation(q):
                act.wait_ge(average_done, q + 1)
                nc.scalar.activation(log[:, :], spare, ACT.Ln, bias=chip.eps[:, 0:1]).then_inc(log_ready, 1)
                act.wait_ge(log_ready, q + 1)
                nc.scalar.activation(rstd[:, :], log[:, :], ACT.Exp, scale=-0.5).then_inc(rstd_ready, 1)

            def keep_ym(u, q):
                act.wait_ge(ym_done, q + 1)
                nc.scalar.activation(ym[:, u, :], spare, ACT.Copy).then_inc(ym_ready, 1)

            def keep_turned(u, q):
                act.wait_ge(prob_done, q + 1)
                for s in (0, 2):
                    nc.scalar.activation(prob_t[:, u, s, :], chip.psum[:, 3 * u + s, 0:QN], ACT.Copy).then_inc(prob_act, 1)

            def quad(u, q, more, more2):
                if more:
                    deviation(q + 1)
                    keep_ym(1 - u, q + 1)
                act.wait_ge(peak_ready, q + 1)
                for c in range(3):
                    for pair in range(2):
                        last = nc.scalar.activation(prob[:, u, c, pair, :], scores_of(u)[:, c, pair, :], ACT.Exp,
                                                    bias=peak[:, u, c, pair:pair + 1],
                                                    accum_out=total[:, u, c, pair:pair + 1])
                last.then_inc(exp_ready, 1)
                if more2:
                    squares(q + 2)
                if not below(q, 1):
                    keep_turned(1 - u, q - 1)
                act.wait_ge(inverse_ready, q + 1)
                for pair in range(2):
                    last = nc.scalar.activation(even[:, u, 2, pair, :], prob[:, u, 2, pair, :], ACT.Copy,
                                                scale=inverse[:, u, 2, pair:pair + 1])
                last.then_inc(even_act, 1)

            act.wait_ge(m_done, 1)
            nc.scalar.activation(m_t[:, :], spare[:, 0:P], ACT.Copy, scale=score_scale).then_inc(m_ready, 1)
            squares(0)
            deviation(0)
            keep_ym(0, 0)
            squares(1)
            loop(act, quad)
            keep_turned(1, chip.quads - 1)

        @block.vector
        def _(dve):
            def keep_centred(q):
                dve.wait_ge(centre_done, q + 1)
                nc.vector.tensor_copy(centred[:, :], spare).then_inc(centred_ready, 1)

            def normed(u, q):
                dve.wait_ge(rstd_ready, q + 1)
                dve.wait_ge(centred_ready, q + 1)
                nc.vector.tensor_tensor(xn[:, u, :], centred[:, :], rstd[:, :], ALU.mult).then_inc(xn_ready, 1)

            def keep_turned(u, q):
                dve.wait_ge(prob_done, q + 1)
                nc.vector.tensor_copy(prob_t[:, u, 1, :], chip.psum[:, 3 * u + 1, 0:QN]).then_inc(prob_dve, 1)

            def finish(q):
                dve.wait_ge(mixed, q + 1)
                nc.vector.scalar_tensor_tensor(chip.h_quad(q), chip.psum[:, 6, 0:QN], value_scale,
                                               chip.h_quad(q), ALU.mult, ALU.add).then_inc(h_ready, 1)

            def keep_values(u, q):
                dve.wait_ge(value_done, q + 1)
                slices = chip.psum[:, 6, 0:QN].rearrange("p (s d) -> p s d", d=P)
                nc.vector.tensor_copy(value[:, u, :, :], slices[:, 0:3:2, :])
                for pair in range(2):
                    half = slice(64 * pair, 64 * pair + 64)
                    last = nc.vector.tensor_copy(value_z[half, u, pair, :], slices[half, 1, :])
                last.then_inc(value_ready, 1)

            def quad(u, q, more, more2):
                if more:
                    normed(1 - u, q + 1)
                dve.wait_ge(scored, q + 1)
                nc.vector.tensor_reduce(peak[:, u, :, :], scores_of(u), X, ALU.max, negate=True).then_inc(peak_ready, 1)
                if not below(q, 2):
                    finish(q - 2)
                if more2:
                    keep_centred(q + 2)
                if not below(q, 1):
                    keep_turned(1 - u, q - 1)
                dve.wait_ge(exp_ready, q + 1)
                nc.vector.reciprocal(inverse[:, u, :, :], total[:, u, :, :]).then_inc(inverse_ready, 1)
                keep_values(u, q)
                dve.wait_ge(inverse_ready, q + 1)
                for c in range(2):
                    for pair in range(2):
                        last = nc.vector.tensor_scalar(even[:, u, c, pair, :], prob[:, u, c, pair, :],
                                                       inverse[:, u, c, pair:pair + 1], None, ALU.mult)
                last.then_inc(even_dve, 1)

            keep_centred(0)
            normed(0, 0)
            keep_centred(1)
            dve.wait_ge(cleared, 2)
            loop(dve, quad)
            keep_turned(1, chip.quads - 1)
            finish(chip.quads - 2)
            finish(chip.quads - 1)

        @block.gpsimd
        def _(pool):
            nc.gpsimd.memset(value_z[:, :, :, :], 0.0).then_inc(cleared, 1)
            nc.gpsimd.memset(xb[:, :, :, :, :], 0.0).then_inc(cleared, 1)
            pool.wait_ge(cleared, 2)

            def spread_queries(u, q):
                pool.wait_ge(xn_ready, q + 1)
                if not below(q, 2):
                    pool.wait_ge(scored, q - 1)
                pool.sem_inc(pool_passed, 1)
                for b in range(2):
                    half = slice(64 * b, 64 * b + 64)
                    last = nc.gpsimd.tensor_copy(xb[half, u, :, b, :],
                                                 xn[half, u, :].rearrange("p (c t) -> p c t", t=64))
                last.then_inc(xb_ready, 1)

            spread_queries(0, 0)
            loop(pool, lambda u, q, more, more2: spread_queries(1 - u, q + 1) if more else None)


def top_two(chip, dve, step, wait, scores, rank, experts, w, groups=12):
    nc = chip.nc

    def wide(a):
        return a.unsqueeze(2).to_broadcast([P, groups, experts])

    source = scores
    for n, (best, hot) in enumerate(((w["best1"], w["hot1"]), (w["best2"], w["hot2"]))):
        step(nc.vector.tensor_reduce(best[:, :], source, X, ALU.max))
        wait()
        step(nc.vector.tensor_tensor(w["equal"][:, :, :], source, wide(best[:, :]), ALU.is_equal))
        wait()
        step(nc.vector.tensor_tensor(w["ranked"][:, :, :], w["equal"][:, :, :], rank, ALU.mult))
        wait()
        step(nc.vector.tensor_reduce(w["first"][:, :], w["ranked"][:, :, :], X, ALU.max))
        wait()
        step(nc.vector.tensor_tensor(hot[:, :, :], rank, wide(w["first"][:, :]), ALU.is_equal))
        wait()
        if n == 0:
            step(nc.vector.scalar_tensor_tensor(w["rest"][:, :, :], hot[:, :, :], -3e38, source, ALU.mult, ALU.add))
            wait()
            source = w["rest"][:, :, :]


def gates_of_two(chip, dve, step, wait, experts, w, gap_ready, ratio_ready, gates_ready, it, groups=12):
    nc = chip.nc

    def wide(a):
        return a[:, :].unsqueeze(2).to_broadcast([P, groups, experts])

    nc.vector.tensor_tensor(w["gap"][:, :], w["best2"][:, :], w["best1"][:, :], ALU.subtract).then_inc(gap_ready, 1)
    dve.wait_ge(ratio_ready, it + 1)
    step(nc.vector.tensor_scalar(w["whole"][:, :], w["ratio"][:, :], 1.0, None, ALU.add))
    wait()
    step(nc.vector.reciprocal(w["w1"][:, :], w["whole"][:, :]))
    wait()
    step(nc.vector.tensor_tensor(w["w2"][:, :], w["ratio"][:, :], w["w1"][:, :], ALU.mult))
    wait()
    step(nc.vector.tensor_tensor(w["gate1"][:, :, :], w["hot1"][:, :, :], wide(w["w1"]), ALU.mult))
    wait()
    step(nc.vector.tensor_tensor(w["ranked"][:, :, :], w["hot2"][:, :, :], wide(w["w2"]), ALU.mult))
    wait()
    nc.vector.tensor_tensor(w["gate"][:, :, :], w["gate1"][:, :, :], w["ranked"][:, :, :],
                            ALU.add).then_inc(gates_ready, 1)
    dve.wait_ge(gates_ready, it + 1)


def experts0(chip):
    nc, op = chip.nc, chip.operand
    with ExitStack() as ctx:
        def sb(n, shape, dt=F32):
            return ctx.enter_context(nc.sbuf_tensor(f"f0_{n}", shape, dt))

        def sem(n):
            return chip.semaphore(f"f0_{n}")

        rows = 3 * 2 * E0
        norm = Norm(chip, ctx, "f0_norm", lambda u, i: chip.psum[:, 6 + i, :])
        post = Norm(chip, ctx, "f0_post", lambda u, i: chip.psum[:, 6 + i, :])
        xn = sb("xn", [P, 2, QN])
        first_layer = Split(chip, ctx, "f0_split", op["f0_w1"])
        y = sb("y", [P, 2, QN])
        yn = sb("yn", [P, 2, QN])
        yg = sb("yg", [P, 2, QN])
        scores = sb("scores", [P, 6, E0])
        work = {n: sb(n, [P, 6, E0]) for n in ("equal", "ranked", "rest", "hot1", "hot2", "gate1", "gate")}
        work |= {n: sb(n, [P, 6]) for n in ("best1", "best2", "first", "gap", "ratio", "whole", "w1", "w2")}
        remains = sb("remains", [P, 2, 3, 2 * E0])
        parts = sb("parts", [P, 3, 3, 2 * E0], BF16)
        parts_t = sb("parts_t", [rows, 2, QN], BF16)
        parts_t32 = sb("parts_t32", [rows, 2, QN])
        ident_b = sb("ident_b", [P, P], BF16)
        pick = sb("pick", [rows, E0, 2, D], BF16)
        hid = sb("hid", [P, 2, 2, QN])
        spread = sb("spread", [P, 2, QN])
        share = sb("share", [P, 2, QN])

        set_up, scored = sem("set_up"), sem("scored")
        steps = [sem(f"step{n}") for n in range(23)]
        gap_ready, ratio_ready = sem("gap_ready"), sem("ratio_ready")
        gates_ready, parts_ready, parts_done, parts_t_ready = (
            sem("gates_ready"), sem("parts_ready"), sem("parts_done"), sem("parts_t_ready"))
        base_done, base_ready = sem("base_done"), sem("base_ready")
        hid_done = [sem(f"hid_done{e}") for e in range(E0)]
        hid_ready = [sem(f"hid_ready{e}") for e in range(E0)]
        expert_done = [sem(f"expert_done{e}") for e in range(E0)]
        share_ready = [sem(f"share_ready{e}") for e in range(E0)]
        spread_done = [sem(f"spread_done{e}") for e in range(E0)]
        spread_ready = [sem(f"spread_ready{e}") for e in range(E0)]
        added = sem("added")
        yg_ready, h_ready = sem("yg_ready"), sem("h_ready")

        def at_start(q):
            return isinstance(q, int) and q == 0

        def loop(eng, quad):
            def both(it, last):
                for u in range(2):
                    quad(u, 2 * it + u, not (last and u == 1))

            pairs = chip.quads // 2
            both(0, pairs == 1)
            if pairs > 2:
                with eng.Fori(1, pairs - 1) as it:
                    both(it, False)
            if pairs > 1:
                both(pairs - 1, True)

        block = ctx.enter_context(nc.Block())

        @block.tensor
        def _(pe):
            def score(u, q):
                pe.wait_ge(norm.ready, q + 1)
                for j in range(3):
                    last = nc.tensor.matmul(chip.psum[:, 7, 2 * E0 * j:2 * E0 * (j + 1)],
                                            xn[:, u, j * P:(j + 1) * P], op["f0_gate_w"], start=True, stop=True)
                last.then_inc(scored, 1)

            def turn_gates(q):
                pe.wait_ge(parts_ready, q + 1)
                for j in range(3):
                    last = nc.tensor.matmul(chip.psum[0:rows, 6, j * P:(j + 1) * P],
                                            parts[:, j, :, :].rearrange("p a e -> p (a e)"), ident_b[:, :],
                                            start=True, stop=True)
                last.then_inc(parts_done, 1)

            def hidden(u, q, e):
                if e >= 2:
                    pe.wait_ge(hid_ready[e - 2], q + 1)
                elif not at_start(q):
                    pe.wait_ge(hid_ready[E0 - 2 + e], q)
                if e == 0:
                    first_layer.wait_x(pe, q)
                for b in range(2):
                    first_layer.product(chip.psum[:, 2 * (e % 2) + b, 0:QN], u, b, slice(e * F0, (e + 1) * F0),
                                        True).then_inc(hid_done[e], 1)

            def base(u, q):
                pe.wait_ge(parts_t_ready, 2 * q + 2)
                if not at_start(q):
                    pe.wait_ge(share_ready[E0 - 1], q)
                nc.tensor.matmul(chip.psum[:, 4, 0:QN], op["f0_b2"][0:rows, :], parts_t32[:, u, :],
                                 start=True, stop=True).then_inc(base_done, 1)

            def output(u, q, e):
                if e:
                    pe.wait_ge(share_ready[e - 1], q + 1)
                else:
                    pe.wait_ge(base_ready, q + 1)
                pe.wait_ge(hid_ready[e], q + 1)
                for b in range(2):
                    last = nc.tensor.matmul(chip.psum[64 * b:64 * b + 64, 4, 0:QN], op["f0_w2"][:, e * D:(e + 1) * D],
                                            hid[:, e % 2, b, :], start=True, stop=True)
                last.then_inc(expert_done[e], 1)

            def spread_gates(u, q, e):
                if e:
                    pe.wait_ge(spread_ready[e - 1], q + 1)
                elif not at_start(q):
                    pe.wait_ge(spread_ready[E0 - 1], q)
                nc.tensor.matmul(chip.psum[:, 5, 0:QN], pick[:, e, :, :].rearrange("p b d -> p (b d)"),
                                 parts_t[:, u, :], start=True, stop=True).then_inc(spread_done[e], 1)

            def quad(u, q, more):
                for e in range(E0):
                    hidden(u, q, e)
                    if e == 0:
                        base(u, q)
                    spread_gates(u, q, e)
                    if e == 1 and not at_start(q):
                        pe.wait_ge(added, E0 * q)
                        post.centre(1 - u, y[:, 1 - u, :])
                    if e == 2 and not at_start(q):
                        post.average(pe, 1 - u, q - 1)
                    if e == 5 and more:
                        if not at_start(q):
                            pe.wait_ge(post.ready, q)
                        norm.centre(1 - u, chip.h_quad(q + 1))
                    if e == 6 and more:
                        norm.average(pe, 1 - u, q + 1)
                    if e == 8 and more:
                        score(1 - u, q + 1)
                    if e:
                        output(u, q, e - 1)
                if more:
                    turn_gates(q + 1)
                output(u, q, E0 - 1)

            pe.wait_ge(set_up, 2)
            norm.centre(0, chip.h_quad(0))
            norm.average(pe, 0, 0)
            score(0, 0)
            turn_gates(0)
            first_layer.wait_weight(pe)
            loop(pe, quad)
            pe.wait_ge(added, E0 * chip.quads)
            post.centre(1, y[:, 1, :])
            post.average(pe, 1, chip.quads - 1)

        @block.scalar
        def _(act):
            nc.scalar.preload_act_table_set("natural_log_exp_and_others")
            def exponentiate(q):
                act.wait_ge(gap_ready, q + 1)
                nc.scalar.activation(work["ratio"][:, :], work["gap"][:, :], ACT.Exp).then_inc(ratio_ready, 1)

            def keep_gates(u, q):
                act.wait_ge(parts_done, q + 1)
                for copy in (parts_t, parts_t32):
                    nc.scalar.activation(copy[:, u, :], chip.psum[0:rows, 6, 0:QN], ACT.Copy).then_inc(parts_t_ready, 1)

            def quad(u, q, more):
                for e in range(E0):
                    if e == 14 and more:
                        first_layer.place_other(act, 1 - u, q + 1, 0)
                    if e == 15 and more:
                        first_layer.place_other(act, 1 - u, q + 1, 1)
                    if e >= 2:
                        act.wait_ge(expert_done[e - 2], q + 1)
                    elif not at_start(q):
                        act.wait_ge(expert_done[E0 - 2 + e], q)
                    for b in range(2):
                        act.wait_ge(hid_done[e], 2 * q + b + 1)
                        last = nc.scalar.activation(hid[:, e % 2, b, :], chip.psum[:, 2 * (e % 2) + b, 0:QN], ACT.Relu,
                                                    bias=op["f0_b1"][:, e:e + 1])
                    last.then_inc(hid_ready[e], 1)
                    act.wait_ge(spread_done[e], q + 1)
                    if e >= 2:
                        act.wait_ge(share_ready[e - 2], q + 1)
                    elif not at_start(q):
                        act.wait_ge(share_ready[E0 - 2 + e], q)
                    nc.scalar.activation(spread[:, e % 2, :], chip.psum[:, 5, 0:QN], ACT.Copy).then_inc(spread_ready[e], 1)
                    if e == 1 and not at_start(q):
                        post.squares(act, 1 - u, q - 1)
                    if e == 3 and not at_start(q):
                        post.logs(act, 1 - u, q - 1)
                        post.powers(act, 1 - u, q - 1)
                    if e == 5 and more:
                        norm.squares(act, 1 - u, q + 1)
                    if e == 6 and more:
                        norm.logs(act, 1 - u, q + 1)
                        norm.powers(act, 1 - u, q + 1)
                    if e == 12 and more:
                        exponentiate(q + 1)
                if more:
                    keep_gates(1 - u, q + 1)

            norm.squares(act, 0, 0)
            norm.logs(act, 0, 0)
            norm.powers(act, 0, 0)
            exponentiate(0)
            keep_gates(0, 0)
            first_layer.swap_weight(act)
            first_layer.place_other(act, 0, 0, 0)
            first_layer.place_other(act, 0, 0, 1)
            loop(act, quad)
            post.squares(act, 1, chip.quads - 1)
            post.logs(act, 1, chip.quads - 1)
            post.powers(act, 1, chip.quads - 1)

        @block.vector
        def _(dve):
            nc.vector.tensor_copy(ident_b[:, :], op["ident"]).then_inc(set_up, 1)
            nc.vector.tensor_copy(pick[:, :, :, :].rearrange("p e b d -> p (e b) d"),
                                  op["f0_pick"][0:rows, :].unsqueeze(2).to_broadcast([rows, 2 * E0, D])
                                  ).then_inc(set_up, 1)

            def gates(q, between):
                link = [0]

                def step(instruction):
                    instruction.then_inc(steps[link[0]], 1)

                def wait():
                    dve.wait_ge(steps[link[0]], q + 1)
                    link[0] += 1
                    if link[0] % 4 == 0:
                        between()

                dve.wait_ge(scored, q + 1)
                flat = scores[:, :, :]
                step(nc.vector.tensor_tensor(flat.rearrange("p g e -> p (g e)"), chip.psum[:, 7, 0:6 * E0],
                                             op["f0_gate_b"], ALU.add))
                wait()
                top_two(chip, dve, step, wait, flat, op["f0_rank"].rearrange("p (g e) -> p g e", e=E0), E0, work, 6)
                gates_of_two(chip, dve, step, wait, E0, work, gap_ready, ratio_ready, gates_ready, q, 6)
                gate = work["gate"][:, :, :].rearrange("p (j b) e -> p j (b e)", b=2)
                if not at_start(q):
                    dve.wait_ge(parts_done, q)
                step(nc.vector.tensor_copy(parts[:, :, 0, :], gate))
                wait()
                step(nc.vector.tensor_tensor(remains[:, 0, :, :], gate, parts[:, :, 0, :], ALU.subtract))
                wait()
                step(nc.vector.tensor_copy(parts[:, :, 1, :], remains[:, 0, :, :]))
                wait()
                nc.vector.tensor_tensor(parts[:, :, 2, :], remains[:, 0, :, :], parts[:, :, 1, :],
                                        ALU.subtract).then_inc(parts_ready, 1)

            def finish(u, q):
                yield post.scale(dve, u, q, yn[:, u, :])
                dve.wait_ge(post.ready, q + 1)
                yield nc.vector.tensor_scalar(yg[:, u, :], yn[:, u, :], op["f0_gamma"], op["f0_beta"],
                                              ALU.mult, ALU.add).then_inc(yg_ready, 1)
                dve.wait_ge(yg_ready, q + 1)
                yield nc.vector.tensor_tensor(chip.h_quad(q), chip.h_quad(q), yg[:, u, :], ALU.add)

            def quad(u, q, more):
                at = [0]

                def share_of_next_expert():
                    e = at[0]
                    at[0] += 1
                    dve.wait_ge(expert_done[e], q + 1)
                    dve.wait_ge(spread_ready[e], q + 1)
                    if e >= 2 or not at_start(q):
                        dve.wait_ge(added, E0 * q + e - 1)
                    nc.vector.tensor_tensor(share[:, e % 2, :], chip.psum[:, 4, 0:QN], spread[:, e % 2, :],
                                            ALU.mult).then_inc(share_ready[e], 1)
                    if e == 11 and more:
                        first_layer.place_high(dve, 1 - u, q + 1)

                dve.wait_ge(base_done, q + 1)
                nc.vector.tensor_tensor(y[:, u, :], chip.psum[:, 4, 0:QN], xn[:, u, :], ALU.add).then_inc(base_ready, 1)
                closing = iter(()) if at_start(q) else finish(1 - u, q - 1)
                while at[0] < 8:
                    share_of_next_expert()
                    if at[0] >= 4:
                        next(closing, None)
                    if at[0] == 7 and more:
                        norm.scale(dve, 1 - u, q + 1, xn[:, 1 - u, :])
                if more:
                    gates(q + 1, share_of_next_expert)
                while at[0] < E0:
                    share_of_next_expert()

            norm.scale(dve, 0, 0, xn[:, 0, :])
            gates(0, lambda: None)
            first_layer.place_high(dve, 0, 0)
            first_layer.split_weight(dve)
            loop(dve, quad)
            for _ in finish(1, chip.quads - 1):
                pass

        @block.gpsimd
        def _(pool):
            def split(u, q):
                pool.wait_ge(norm.ready, q + 1)
                yield from first_layer.split(pool, xn[:, u, :], q)

            def quad(u, q, more):
                splitting = split(1 - u, q + 1) if more else iter(())
                pool.wait_ge(base_ready, q + 1)
                for e in range(E0):
                    if e:
                        pool.wait_ge(added, E0 * q + e)
                    pool.wait_ge(share_ready[e], q + 1)
                    nc.gpsimd.tensor_tensor(y[:, u, :], y[:, u, :], share[:, e % 2, :], ALU.add).then_inc(added, 1)
                    if e >= E0 // 2:
                        next(splitting, None)

            for _ in split(0, 0):
                pass
            loop(pool, quad)


def linear_attention(chip):
    nc, op, ident = chip.nc, chip.operand, chip.operand["ident"]
    with ExitStack() as ctx:
        def sb(n, shape, dt=F32):
            return ctx.enter_context(nc.sbuf_tensor(f"a1_{n}", shape, dt))

        def sem(n):
            return chip.semaphore(f"a1_{n}")

        norm = Norm(chip, ctx, "a1_norm", lambda u, i: chip.psum[:, 4 + i, :])
        post = Norm(chip, ctx, "a1_post", lambda u, i: chip.psum[:, 6 + i, :])
        xn = sb("xn", [P, QN])
        value = sb("value", [P, QN])
        query = sb("query", [P, 3, P])
        peak, total, inverse = sb("peak", [P, 2]), sb("total", [P, 2]), sb("inverse", [P, 2])
        key = sb("key", [P, QN])
        key_t = sb("key_t", [P, 2, P])
        key_z = sb("key_z", [P, 2, P])
        outer = sb("outer", [P, 2, P])
        o = sb("o", [P, QN])
        spread_o = sb("spread", [P, 2, 2, 8, T])
        y, yn, yg = sb("y", [P, QN]), sb("yn", [P, QN]), sb("yg", [P, QN])

        cleared = sem("cleared")
        projected, value_ready, query_ready = sem("projected"), sem("value_ready"), sem("query_ready")
        peak_ready, key_ready, inverse_ready = sem("peak_ready"), sem("key_ready"), sem("inverse_ready")
        key_done, key_t_ready, key_z_ready = sem("key_done"), sem("key_t_ready"), sem("key_z_ready")
        outer_done, outer_ready = sem("outer_done"), sem("outer_ready")
        o_done, o_ready, spread_ready = sem("o_done"), sem("o_ready"), sem("spread_ready")
        mixed, y_ready, yg_ready, h_ready = sem("mixed"), sem("y_ready"), sem("yg_ready"), sem("h_ready")

        def bank(i):
            return chip.psum[:, i, 0:QN]

        def at_start(q):
            return isinstance(q, int) and q == 0

        def loop(eng, quad):
            turns = chip.quads // 2

            def both(it, last):
                for u in range(2):
                    quad(u, 2 * it + u, not (last and u == 1), not last)

            both(0, turns == 1)
            if turns > 2:
                with eng.Fori(1, turns - 1) as it:
                    both(it, False)
            if turns > 1:
                both(turns - 1, True)

        block = ctx.enter_context(nc.Block())

        @block.tensor
        def _(pe):
            def centre(q):
                if not at_start(q):
                    pe.wait_ge(norm.ready, q)
                norm.centre(0, chip.h_quad(q))

            def project(q):
                pe.wait_ge(norm.ready, q + 1)
                if not at_start(q):
                    pe.wait_ge(o_ready, q)
                    pe.wait_ge(outer_ready, q)
                    pe.wait_ge(key_z_ready, q)
                nc.tensor.matmul(bank(1), op["a1_wk"], xn[:, :], start=True, stop=True)
                nc.tensor.matmul(bank(2), op["a1_wv"], xn[:, :], start=True, stop=True)
                for j in range(3):
                    last = nc.tensor.matmul(bank(3)[:, j * P:(j + 1) * P], xn[:, j * P:(j + 1) * P],
                                            op["a1_wq"], start=True, stop=True)
                last.then_inc(projected, 1)

            def turn_keys(q):
                pe.wait_ge(key_ready, q + 1)
                pe.wait_ge(value_ready, q + 1)
                for s, out in ((0, bank(1)[:, 0:P]), (2, bank(1)[:, P:2 * P]), (1, bank(2)[:, 0:P])):
                    last = nc.tensor.transpose(out, key[:, s * P:(s + 1) * P], ident)
                last.then_inc(key_done, 1)

            def outer_products(q):
                pe.wait_ge(key_t_ready, q + 1)
                pe.wait_ge(key_z_ready, q + 1)
                pe.wait_ge(query_ready, q + 1)
                for pair in range(2):
                    out = bank(3)[:, pair * P:(pair + 1) * P]
                    nc.tensor.matmul(out, key_t[:, pair, :], query[:, 2 * pair, :], start=True, stop=False)
                    last = nc.tensor.matmul(out, key_z[:, pair, :], query[:, 1, :], start=False, stop=True)
                last.then_inc(outer_done, 1)

            def apply(q):
                pe.wait_ge(outer_ready, q + 1)
                for pair in range(2):
                    last = nc.tensor.matmul(bank(1)[:, pair * T:(pair + 1) * T], outer[:, pair, :],
                                            value[:, pair * T:(pair + 1) * T], start=True, stop=True)
                last.then_inc(o_done, 1)

            def mix(u, q, rows):
                if 0 in rows:
                    pe.wait_ge(spread_ready, q + 1)
                    if not at_start(q):
                        pe.wait_ge(y_ready, q)
                tokens = spread_o[:, u, :, :, :].rearrange("p g h (j r) -> p r (g h j)", r=8)
                for jr in rows:
                    last = nc.tensor.matmul(bank(0), op["a1_wo"][:, jr * P:(jr + 1) * P], tokens[:, jr, :],
                                            start=(jr == 0), stop=(jr == 7))
                if 7 in rows:
                    last.then_inc(mixed, 1)

            def post_centre(q):
                pe.wait_ge(y_ready, q + 1)
                if not at_start(q):
                    pe.wait_ge(post.ready, q)
                post.centre(0, y[:, :])

            def quad(u, q, more, more2):
                if more:
                    project(q + 1)
                if more2:
                    centre(q + 2)
                mix(u, q, (0, 1, 2))
                if more:
                    turn_keys(q + 1)
                if not at_start(q):
                    post_centre(q - 1)
                if more:
                    outer_products(q + 1)
                mix(u, q, (3,))
                if more:
                    apply(q + 1)
                if more2:
                    norm.average(pe, 0, q + 2)
                mix(u, q, (4,))
                if not at_start(q):
                    post.average(pe, 0, q - 1)
                mix(u, q, (5, 6, 7))

            pe.wait_ge(cleared, 1)
            centre(0)
            norm.average(pe, 0, 0)
            project(0)
            centre(1)
            turn_keys(0)
            norm.average(pe, 0, 1)
            outer_products(0)
            apply(0)
            loop(pe, quad)
            post_centre(chip.quads - 1)
            post.average(pe, 0, chip.quads - 1)

        @block.scalar
        def _(act):
            nc.scalar.preload_act_table_set("natural_log_exp_and_others")

            def deviation(q):
                norm.logs(act, 0, q)
                norm.powers(act, 0, q)

            def keep_queries(q):
                act.wait_ge(projected, q + 1)
                nc.scalar.activation(query[:, :, :], bank(3).rearrange("p (s e) -> p s e", s=3),
                                     ACT.Copy, scale=D ** -0.5).then_inc(query_ready, 1)

            def key_exp(q):
                act.wait_ge(peak_ready, q + 1)
                for pair in range(2):
                    cols = slice(pair * T, (pair + 1) * T)
                    last = nc.scalar.activation(key[:, cols], bank(1)[:, cols], ACT.Exp,
                                                bias=peak[:, pair:pair + 1], accum_out=total[:, pair:pair + 1])
                last.then_inc(key_ready, 1)

            def keep_turned(q):
                act.wait_ge(key_done, q + 1)
                nc.scalar.activation(key_t[:, :, :], bank(1)[:, 0:2 * P].rearrange("p (g d) -> p g d", g=2),
                                     ACT.Copy).then_inc(key_t_ready, 1)

            def keep_o(q):
                act.wait_ge(o_done, q + 1)
                nc.scalar.activation(o[:, :], bank(1), ACT.Copy).then_inc(o_ready, 1)

            def keep_y(q):
                act.wait_ge(mixed, q + 1)
                nc.scalar.activation(y[:, :], bank(0), ACT.Identity, bias=op["a1_bo"]).then_inc(y_ready, 1)

            def quad(u, q, more, more2):
                if not at_start(q):
                    keep_y(q - 1)
                if more:
                    keep_queries(q + 1)
                    key_exp(q + 1)
                if more2:
                    norm.squares(act, 0, q + 2)
                if more:
                    keep_turned(q + 1)
                if not at_start(q):
                    post.squares(act, 0, q - 1)
                if more:
                    keep_o(q + 1)
                if more2:
                    deviation(q + 2)
                if not at_start(q):
                    post.logs(act, 0, q - 1)
                    post.powers(act, 0, q - 1)

            norm.squares(act, 0, 0)
            deviation(0)
            keep_queries(0)
            key_exp(0)
            norm.squares(act, 0, 1)
            keep_turned(0)
            deviation(1)
            keep_o(0)
            loop(act, quad)
            keep_y(chip.quads - 1)
            post.squares(act, 0, chip.quads - 1)
            post.logs(act, 0, chip.quads - 1)
            post.powers(act, 0, chip.quads - 1)

        @block.vector
        def _(dve):
            nc.vector.memset(key_z[:, :, :], 0.0).then_inc(cleared, 1)
            dve.wait_ge(cleared, 1)

            def keep_values(q):
                dve.wait_ge(projected, q + 1)
                nc.vector.tensor_reduce(peak[:, :], bank(1).rearrange("p (g t) -> p g t", t=T),
                                        X, ALU.max, negate=True).then_inc(peak_ready, 1)
                nc.vector.tensor_copy(value[:, :], bank(2)).then_inc(value_ready, 1)

            def keep_turned(q):
                dve.wait_ge(key_ready, q + 1)
                nc.vector.reciprocal(inverse[:, :], total[:, :]).then_inc(inverse_ready, 1)
                dve.wait_ge(key_done, q + 1)
                for pair in range(2):
                    half = slice(64 * pair, 64 * pair + 64)
                    last = nc.vector.tensor_copy(key_z[half, pair, :], bank(2)[half, 0:P])
                last.then_inc(key_z_ready, 1)

            def mask_outer(q):
                dve.wait_ge(outer_done, q + 1)
                dve.wait_ge(inverse_ready, q + 1)
                for pair in range(2):
                    last = nc.vector.scalar_tensor_tensor(
                        outer[:, pair, :], bank(3)[:, pair * P:(pair + 1) * P],
                        inverse[:, pair:pair + 1], op["a1_heads"], ALU.mult, ALU.mult)
                last.then_inc(outer_ready, 1)

            def spread(u, q):
                dve.wait_ge(o_ready, q + 1)
                for h in range(8):
                    last = nc.vector.tensor_scalar(spread_o[:, u, :, h, :], o[:, :].rearrange("p (g t) -> p g t", t=T),
                                                   op["a1_head"][:, h:h + 1], None, ALU.mult)
                last.then_inc(spread_ready, 1)

            def finish(q):
                if not at_start(q):
                    dve.wait_ge(h_ready, q)
                post.scale(dve, 0, q, yn[:, :])
                dve.wait_ge(post.ready, q + 1)
                nc.vector.tensor_scalar(yg[:, :], yn[:, :], op["a1_gamma"], op["a1_beta"],
                                        ALU.mult, ALU.add).then_inc(yg_ready, 1)
                dve.wait_ge(yg_ready, q + 1)
                nc.vector.tensor_tensor(chip.h_quad(q), chip.h_quad(q), yg[:, :], ALU.add).then_inc(h_ready, 1)

            def quad(u, q, more, more2):
                if more:
                    keep_values(q + 1)
                    keep_turned(q + 1)
                    mask_outer(q + 1)
                    spread(1 - u, q + 1)
                if more2:
                    norm.scale(dve, 0, q + 2, xn[:, :])
                if not at_start(q):
                    finish(q - 1)

            norm.scale(dve, 0, 0, xn[:, :])
            keep_values(0)
            keep_turned(0)
            mask_outer(0)
            norm.scale(dve, 0, 1, xn[:, :])
            spread(0, 0)
            loop(dve, quad)
            finish(chip.quads - 1)


def routed(chip):
    nc, op = chip.nc, chip.operand
    with ExitStack() as ctx:
        def sb(n, shape, dt=F32):
            return ctx.enter_context(nc.sbuf_tensor(f"f1_{n}", shape, dt))

        def sem(n):
            return chip.semaphore(f"f1_{n}")

        norm = Norm(chip, ctx, "f1_norm", lambda u, i: chip.psum[:, 6 + i, :])
        xn = sb("xn", [P, 2, QN])
        shared = sb("shared", [P, 2, F1])
        weight = sb("weight", [P, 2, 2, 2, F1])
        bias = sb("bias", [P, 2, 2, 2])
        hid = [sb(f"hid{n}", [P, 2, 2, 2, T]) for n in range(3)]
        shared_ready = sem("shared_ready")
        weight_ready = sem("weight_ready")
        entered = sem("entered")
        hid_act = [sem(f"hid_act{n}") for n in range(3)]
        hid_dve = [sem(f"hid_dve{n}") for n in range(3)]
        layered = [sem(f"layered{n}") for n in range(2)]
        left, h_ready = sem("left"), sem("h_ready")

        def below(q, n):
            return isinstance(q, int) and q < n

        def loop(eng, quad):
            turns = chip.quads // 2

            def both(it, last):
                for u in range(2):
                    quad(u, 2 * it + u, not last)

            both(0, turns == 1)
            if turns > 2:
                with eng.Fori(1, turns - 1) as it:
                    both(it, False)
            if turns > 1:
                both(turns - 1, True)

        def layer_bank(layer, pair):
            return chip.psum[:, 2 + 2 * layer + pair, 0:QN]

        block = ctx.enter_context(nc.Block())

        @block.tensor
        def _(pe):
            def centre(u, q):
                if not below(q, 1):
                    pe.wait_ge(norm.ready, q)
                norm.centre(u, chip.h_quad(q))

            def enter(u, q):
                pe.wait_ge(norm.ready, q + 1)
                if not below(q, 2):
                    pe.wait_ge(h_ready, q - 1)
                for b in range(2):
                    half = slice(64 * b, 64 * b + 64)
                    last = nc.tensor.matmul(chip.psum[:, b, 0:QN], op["f1_wi"][half, :], xn[half, u, :],
                                            start=True, stop=True)
                last.then_inc(entered, 1)

            def through(u, q, layer):
                pe.wait_ge(hid_act[layer], q + 1)
                pe.wait_ge(hid_dve[layer], q + 1)
                if layer == 0:
                    pe.wait_ge(weight_ready, q + 1)
                for pair in range(2):
                    last = nc.tensor.matmul(layer_bank(layer, pair), weight[:, u, layer, pair, :],
                                            hid[layer][:, u, pair, :, :].rearrange("p b t -> p (b t)"),
                                            start=True, stop=True)
                last.then_inc(layered[layer], 1)

            def leave(u, q):
                pe.wait_ge(hid_act[2], q + 1)
                pe.wait_ge(hid_dve[2], q + 1)
                for b in range(2):
                    for pair in range(2):
                        last = nc.tensor.matmul(chip.psum[64 * b:64 * b + 64, 0, pair * T:(pair + 1) * T],
                                                op["f1_wo"], hid[2][:, u, pair, b, :], start=True, stop=True)
                last.then_inc(left, 1)

            def quad(u, q, more2):
                enter(u, q)
                if not below(q, 1):
                    through(1 - u, q - 1, 1)
                if more2:
                    centre(u, q + 2)
                through(u, q, 0)
                if not below(q, 1):
                    leave(1 - u, q - 1)
                if more2:
                    norm.average(pe, u, q + 2)

            for q in range(2):
                centre(q, q)
                norm.average(pe, q, q)
            loop(pe, quad)
            through(1, chip.quads - 1, 1)
            leave(1, chip.quads - 1)

        @block.scalar
        def _(act):
            nc.scalar.preload_act_table_set("natural_log_exp_and_others")

            def hidden(u, q, layer):
                act.wait_ge(layered[layer], q + 1)
                nc.scalar.activation(hid[layer + 1][:, u, 0, :, :].rearrange("p b t -> p (b t)"), layer_bank(layer, 0),
                                     ACT.Relu, bias=bias[:, u, layer, 0:1]).then_inc(hid_act[layer + 1], 1)

            def quad(u, q, more2):
                act.wait_ge(entered, q + 1)
                nc.scalar.activation(hid[0][:, u, :, 0, :], chip.psum[:, 0, 0:QN].rearrange("p (g t) -> p g t", g=2),
                                     ACT.Relu, bias=op["f1_bi"]).then_inc(hid_act[0], 1)
                if not below(q, 1):
                    hidden(1 - u, q - 1, 1)
                if more2:
                    norm.squares(act, u, q + 2)
                hidden(u, q, 0)
                if more2:
                    norm.logs(act, u, q + 2)
                    norm.powers(act, u, q + 2)

            for q in range(2):
                norm.squares(act, q, q)
                norm.logs(act, q, q)
                norm.powers(act, q, q)
            loop(act, quad)
            hidden(1, chip.quads - 1, 1)

        @block.vector
        def _(dve):
            def hidden(u, q, layer):
                dve.wait_ge(layered[layer], q + 1)
                nc.vector.tensor_scalar(hid[layer + 1][:, u, 1, :, :].rearrange("p b t -> p (b t)"), layer_bank(layer, 1),
                                        bias[:, u, layer, 1:2], 0.0, ALU.add, ALU.max).then_inc(hid_dve[layer + 1], 1)

            def finish(q):
                dve.wait_ge(left, q + 1)
                nc.vector.scalar_tensor_tensor(chip.h_quad(q), chip.psum[:, 0, 0:QN], op["f1_bo"],
                                               chip.h_quad(q), ALU.add, ALU.add).then_inc(h_ready, 1)

            def quad(u, q, more2):
                dve.wait_ge(entered, q + 1)
                nc.vector.tensor_scalar(hid[0][:, u, :, 1, :], chip.psum[:, 1, 0:QN].rearrange("p (g t) -> p g t", g=2),
                                        op["f1_bi"], 0.0, ALU.add, ALU.max).then_inc(hid_dve[0], 1)
                if not below(q, 1):
                    hidden(1 - u, q - 1, 1)
                hidden(u, q, 0)
                if not below(q, 1):
                    finish(q - 1)
                if more2:
                    norm.scale(dve, u, q + 2, xn[:, u, :])

            for q in range(2):
                norm.scale(dve, q, q, xn[:, q, :])
            loop(dve, quad)
            hidden(1, chip.quads - 1, 1)
            finish(chip.quads - 1)

        @block.gpsimd
        def _(pool):
            for layer in range(2):
                nc.gpsimd.tensor_tensor(shared[:, layer, :], op["f1_ws"][:, layer * F1:(layer + 1) * F1],
                                        op["ident"], ALU.add).then_inc(shared_ready, 1)
            pool.wait_ge(shared_ready, 2)

            def quad(u, q, more2):
                if not below(q, 2):
                    pool.wait_ge(hid_act[2], q - 1)
                    pool.wait_ge(hid_dve[2], q - 1)
                for pair in range(2):
                    route = pool.value_load(chip.routes[0:1, bass.ds(2 * q + pair, 1)], min_val=0, max_val=E1 - 1)
                    for layer in range(2):
                        nc.gpsimd.tensor_tensor(weight[:, u, layer, pair, :],
                                                op["f1_wr"][:, bass.ds(route * F1 + layer * E1 * F1, F1)],
                                                shared[:, layer, :], ALU.add)
                        last = nc.gpsimd.tensor_tensor(bias[:, u, layer, pair:pair + 1],
                                                       op["f1_br"][:, bass.ds(route + layer * E1, 1)],
                                                       op["f1_bs"][:, layer:layer + 1], ALU.add)
                last.then_inc(weight_ready, 1)

            loop(pool, quad)


def experts2(chip):
    nc, op = chip.nc, chip.operand
    with ExitStack() as ctx:
        def sb(n, shape, dt=F32):
            return ctx.enter_context(nc.sbuf_tensor(f"f2_{n}", shape, dt))

        def sem(n):
            return chip.semaphore(f"f2_{n}")

        pairs = E2 // 2
        step_count = 2 * pairs
        gate_lag, sum_lag = 3, 4
        rows = 3 * 2 * E2
        norm = Norm(chip, ctx, "f2_norm", lambda u, i: chip.psum[:, 6 + i, :])
        xn = sb("xn", [P, 2, 2, QN])
        router = sb("router", [2 * R2, 2, QN])
        scores = sb("scores", [P, 2, 6 * E2])
        rank = sb("rank", [P, 2, 6 * E2])
        shift, power, share = (sb(n, [P, 12, E2]) for n in ("shift", "power", "share"))
        top, total, inverse = (sb(n, [P, 12]) for n in ("top", "total", "inverse"))
        work = {n: sb(n, [P, 12, E2]) for n in ("equal", "ranked", "rest", "hot1", "hot2", "gate1", "gate")}
        work |= {n: sb(n, [P, 12]) for n in ("best1", "best2", "first", "gap", "ratio", "whole", "w1", "w2")}
        remains = sb("remains", [P, 6, 2 * E2])
        parts = sb("parts", [P, 6, 3, 2 * E2], BF16)
        parts_t = sb("parts_t", [rows, 2, QN], BF16)
        parts_t32 = sb("parts_t32", [rows, 2, QN])
        ident_b = sb("ident_b", [P, P], BF16)
        pick = sb("pick", [rows, pairs, 2, 2 * D], BF16)
        hid1 = sb("hid1", [P, 2, QN])
        hid2 = sb("hid2", [P, step_count, 2, QN])
        gated = sb("gated", [P, 2, 2, QN])

        def by_step(n):
            return [[sem(f"{n}{s}_{b}") for b in range(2)] for s in range(step_count)]

        set_up, routed_done, router_ready, scored = sem("set_up"), sem("routed_done"), sem("router_ready"), sem("scored")
        shift_ready, power_ready = sem("shift_ready"), sem("power_ready")
        steps = [sem(f"step{n}") for n in range(26)]
        gap_ready, ratio_ready, gates_ready = sem("gap_ready"), sem("ratio_ready"), sem("gates_ready")
        parts_ready, parts_done, parts_t_ready = sem("parts_ready"), sem("parts_done"), sem("parts_t_ready")
        hid1_done, hid1_ready, hid2_done, hid2_ready, spread_done, gated_ready = map(
            by_step, ("hid1_done", "hid1_ready", "hid2_done", "hid2_ready", "spread_done", "gated_ready"))
        summed, h_ready = sem("summed"), sem("h_ready")

        def at_start(it):
            return isinstance(it, int) and it == 0

        def loop(eng, body):
            turns = chip.quads // 4

            def turn(it, last):
                for parity in range(2):
                    body(2 * it + parity, parity, not (last and parity == 1))

            turn(0, turns == 1)
            if turns > 2:
                with eng.Fori(1, turns - 1) as it:
                    turn(it, False)
            if turns > 1:
                turn(turns - 1, True)

        def earlier(s, n, it):
            if s >= n:
                return s - n, it
            return None if at_start(it) else (s - n + step_count, it - 1)

        def wait_step(eng, signals, at, b):
            if at is not None:
                eng.wait_ge(signals[at[0]][b], at[1] + 1)

        block = ctx.enter_context(nc.Block())

        @block.tensor
        def _(pe):
            def route(v, q, parity):
                pe.wait_ge(norm.ready, q + 1)
                nc.tensor.matmul(chip.psum[0:2 * R2, 7, 0:QN], op["f2_rw1"], xn[:, parity, v, :],
                                 start=True, stop=True).then_inc(routed_done, 1)

            def score(v, q):
                pe.wait_ge(router_ready, q + 1)
                for j in range(3):
                    at = 2 * E2 * (3 * v + j)
                    last = nc.tensor.matmul(chip.psum[:, 6, at:at + 2 * E2], router[:, v, j * P:(j + 1) * P],
                                            op["f2_rw2"][0:2 * R2, :], start=True, stop=True)
                last.then_inc(scored, 1)

            def prepare(i, it, parity):
                quads = [2 * it, 2 * it + 1]
                if i == 0:
                    pe.wait_ge(steps[0], it)
                    norm.centre(0, chip.h_quad(quads[0]))
                if i == 1:
                    norm.average(pe, 0, quads[0])
                if i == 3:
                    route(0, quads[0], parity)
                    norm.centre(1, chip.h_quad(quads[1]))
                if i == 4:
                    pe.wait_ge(router_ready, quads[0] + 1)
                    norm.average(pe, 1, quads[1])
                if i == 6:
                    route(1, quads[1], parity)
                    score(0, quads[0])
                if i == 8:
                    score(1, quads[1])

            def turn_gates(it):
                pe.wait_ge(parts_ready, it + 1)
                wait_step(pe, gated_ready, earlier(2, gate_lag, it), 1)
                for j in range(6):
                    at = 64 * (j // 3)
                    last = nc.tensor.matmul(chip.psum[at:at + rows, 4, j % 3 * P:(j % 3 + 1) * P],
                                            parts[:, j, :, :].rearrange("p a e -> p (a e)"), ident_b[:, :],
                                            start=True, stop=True)
                last.then_inc(parts_done, 1)

            def spread_gates(at, b):
                if at is None:
                    return
                s, it = at
                if b:
                    wait_step(pe, gated_ready, at, 0)
                else:
                    wait_step(pe, gated_ready, earlier(s, 1, it), 1)
                    pe.wait_ge(parts_t_ready, 4 * it + 4)
                nc.tensor.matmul(chip.psum[:, 4, 0:QN], pick[:, s % pairs, b, :], parts_t[:, s // pairs, :],
                                 start=True, stop=True).then_inc(spread_done[s][b], 1)

            def third(at):
                if at is None:
                    return
                s, it = at
                k, v = s % pairs, s // pairs
                if k == 0:
                    if v or not at_start(it):
                        pe.wait_ge(h_ready, 2 * it + v)
                    nc.tensor.matmul(chip.psum[:, 5, 0:QN], op["f2_b3"][0:rows, :], parts_t32[:, v, :],
                                     start=True, stop=False, skip_group_check=True)
                for b in range(2):
                    wait_step(pe, gated_ready, at, b)
                    last = nc.tensor.matmul(chip.psum[64 * b:64 * b + 64, 5, 0:QN], op["f2_w3"][:, k * D:(k + 1) * D],
                                            gated[:, s % 2, b, :], start=False, stop=(k == pairs - 1),
                                            skip_group_check=True)
                if k == pairs - 1:
                    last.then_inc(summed, 1)

            def body(it, parity, more):
                for s in range(step_count):
                    k, v = s % pairs, s // pairs
                    for b in range(2):
                        half = slice(64 * b, 64 * b + 64)
                        wait_step(pe, hid1_ready, earlier(s, 1, it), b)
                        nc.tensor.matmul(chip.psum[:, b, 0:QN], op["f2_w1"][half, k * P:(k + 1) * P],
                                         xn[half, parity, v, :], start=True, stop=True).then_inc(hid1_done[s][b], 1)
                    spread_gates(earlier(s, gate_lag, it), 0)
                    third(earlier(s, sum_lag, it))
                    if more:
                        prepare(2 * s, it + 1, 1 - parity)
                    for b in range(2):
                        pe.wait_ge(hid1_ready[s][b], it + 1)
                        wait_step(pe, hid2_ready, earlier(s, 1, it), b)
                        nc.tensor.matmul(chip.psum[:, 2 + b, 0:QN], op["f2_w2"][:, k * P:(k + 1) * P],
                                         hid1[:, b, :], start=True, stop=True).then_inc(hid2_done[s][b], 1)
                    spread_gates(earlier(s, gate_lag, it), 1)
                    if more:
                        prepare(2 * s + 1, it + 1, 1 - parity)
                    if s == gate_lag - 1:
                        turn_gates(it)

            pe.wait_ge(set_up, 4)
            for v in range(2):
                if v:
                    pe.wait_ge(router_ready, v)
                norm.centre(v, chip.h_quad(v))
                norm.average(pe, v, v)
                route(v, v, 0)
            score(0, 0)
            score(1, 1)
            loop(pe, body)
            for s in range(sum_lag):
                spread_gates(earlier(s, gate_lag, chip.quads // 2) if s < gate_lag else None, 0)
                third(earlier(s, sum_lag, chip.quads // 2))
                spread_gates(earlier(s, gate_lag, chip.quads // 2) if s < gate_lag else None, 1)

        @block.scalar
        def _(act):
            nc.scalar.preload_act_table_set("natural_log_exp_and_others")

            def router_units(v, q):
                act.wait_ge(routed_done, q + 1)
                nc.scalar.activation(router[:, v, :], chip.psum[0:2 * R2, 7, 0:QN], ACT.Relu,
                                     bias=op["f2_rb1"][0:2 * R2, :]).then_inc(router_ready, 1)

            def softmax_exp(it):
                act.wait_ge(shift_ready, it + 1)
                nc.scalar.activation(power[:, :, :], shift[:, :, :], ACT.Exp).then_inc(power_ready, 1)

            def prepare(i, it):
                quads = [2 * it, 2 * it + 1]
                if i == 0:
                    norm.squares(act, 0, quads[0])
                if i == 1:
                    norm.logs(act, 0, quads[0])
                    norm.powers(act, 0, quads[0])
                if i == 3:
                    router_units(0, quads[0])
                    norm.squares(act, 1, quads[1])
                if i == 4:
                    norm.logs(act, 1, quads[1])
                    norm.powers(act, 1, quads[1])
                if i == 6:
                    router_units(1, quads[1])
                if i == 9:
                    softmax_exp(it)

            def body(it, parity, more):
                for s in range(step_count):
                    k = s % pairs
                    for b in range(2):
                        act.wait_ge(hid1_done[s][b], it + 1)
                        nc.scalar.activation(hid1[:, b, :], chip.psum[:, b, 0:QN], ACT.Relu,
                                             bias=op["f2_b1"][:, k:k + 1]).then_inc(hid1_ready[s][b], 1)
                    if s == 0:
                        act.wait_ge(gap_ready, it + 1)
                        nc.scalar.activation(work["ratio"][:, :], work["gap"][:, :], ACT.Exp).then_inc(ratio_ready, 1)
                    if more:
                        prepare(2 * s, it + 1)
                    for b in range(2):
                        act.wait_ge(hid2_done[s][b], it + 1)
                        wait_step(act, gated_ready, earlier(s, step_count, it), b)
                        nc.scalar.activation(hid2[:, s, b, :], chip.psum[:, 2 + b, 0:QN], ACT.Relu,
                                             bias=op["f2_b2"][:, k:k + 1]).then_inc(hid2_ready[s][b], 1)
                    if more:
                        prepare(2 * s + 1, it + 1)
                    if s == gate_lag - 1:
                        act.wait_ge(parts_done, it + 1)
                        for copy in (parts_t, parts_t32):
                            for v in range(2):
                                nc.scalar.activation(copy[:, v, :], chip.psum[64 * v:64 * v + rows, 4, 0:QN],
                                                     ACT.Copy).then_inc(parts_t_ready, 1)

            for v in range(2):
                norm.squares(act, v, v)
                norm.logs(act, v, v)
                norm.powers(act, v, v)
                router_units(v, v)
            softmax_exp(0)
            loop(act, body)

        @block.vector
        def _(dve):
            nc.vector.tensor_copy(ident_b[:, :], op["ident"]).then_inc(set_up, 1)
            nc.vector.tensor_copy(pick[:, :, :, :].rearrange("p k b (e d) -> p (k b e) d", d=D),
                                  op["f2_pick"][0:rows, :].unsqueeze(2).to_broadcast([rows, 2 * E2, D])
                                  ).then_inc(set_up, 1)
            for v in range(2):
                nc.vector.tensor_copy(rank[:, v, :], op["f2_rank"]).then_inc(set_up, 1)
            dve.wait_ge(set_up, 4)

            def links(it, start, between):
                at = [start]

                def step(instruction):
                    instruction.then_inc(steps[at[0]], 1)

                def wait():
                    dve.wait_ge(steps[at[0]], it + 1)
                    at[0] += 1
                    if (at[0] - start) % 4 == 0:
                        between()

                return step, wait

            def choose(it, between):
                step, wait = links(it, 0, between)

                def wide(a):
                    return a[:, :].unsqueeze(2).to_broadcast([P, 12, E2])

                dve.wait_ge(scored, 2 * it + 2)
                step(nc.vector.tensor_tensor(scores[:, :, :].rearrange("p v e -> p (v e)"), chip.psum[:, 6, 0:12 * E2],
                                             op["f2_rb2"], ALU.add))
                wait()
                flat = scores[:, :, :].rearrange("p v (g e) -> p (v g) e", e=E2)
                ranks = rank[:, :, :].rearrange("p v (g e) -> p (v g) e", e=E2)
                step(nc.vector.tensor_reduce(top[:, :], flat, X, ALU.max))
                wait()
                nc.vector.tensor_tensor(shift[:, :, :], flat, wide(top), ALU.subtract).then_inc(shift_ready, 1)
                between()
                dve.wait_ge(power_ready, it + 1)
                step(nc.vector.tensor_reduce(total[:, :], power[:, :, :], X, ALU.add))
                wait()
                step(nc.vector.reciprocal(inverse[:, :], total[:, :]))
                wait()
                step(nc.vector.tensor_tensor(share[:, :, :], power[:, :, :], wide(inverse), ALU.mult))
                wait()
                top_two(chip, dve, step, wait, share[:, :, :], ranks, E2, work)

            def gates(it, between):
                step, wait = links(it, 16, between)
                gates_of_two(chip, dve, step, wait, E2, work, gap_ready, ratio_ready, gates_ready, it)
                gate = work["gate"][:, :, :].rearrange("p (j b) e -> p j (b e)", b=2)
                if not at_start(it):
                    dve.wait_ge(parts_done, it)
                step(nc.vector.tensor_copy(parts[:, :, 0, :], gate))
                wait()
                step(nc.vector.tensor_tensor(remains[:, :, :], gate, parts[:, :, 0, :], ALU.subtract))
                wait()
                step(nc.vector.tensor_copy(parts[:, :, 1, :], remains[:, :, :]))
                wait()
                nc.vector.tensor_tensor(parts[:, :, 2, :], remains[:, :, :], parts[:, :, 1, :],
                                        ALU.subtract).then_inc(parts_ready, 1)

            def product(at, b):
                if at is None:
                    return
                s, it = at
                wait_step(dve, spread_done, at, b)
                wait_step(dve, hid2_ready, at, b)
                nc.vector.tensor_tensor(gated[:, s % 2, b, :], hid2[:, s, b, :], chip.psum[:, 4, 0:QN],
                                        ALU.mult).then_inc(gated_ready[s][b], 1)

            def add(at):
                if at is None or at[0] % pairs != pairs - 1:
                    return
                q = 2 * at[1] + at[0] // pairs
                dve.wait_ge(summed, q + 1)
                nc.vector.tensor_tensor(chip.h_quad(q), chip.psum[:, 5, 0:QN], chip.h_quad(q),
                                        ALU.add).then_inc(h_ready, 1)

            def body(it, parity, more):
                products = [(s, b) for s in range(step_count) for b in range(2)]

                def multiply():
                    if not products:
                        return
                    s, b = products.pop(0)
                    product(earlier(s, gate_lag, it), b)
                    if b == 0:
                        add(earlier(s, sum_lag, it))
                    if more and (s, b) == (1, 0):
                        norm.scale(dve, 0, 2 * it + 2, xn[:, 1 - parity, 0, :])
                    if more and (s, b) == (2, 1):
                        norm.scale(dve, 1, 2 * it + 3, xn[:, 1 - parity, 1, :])

                gates(it, multiply)
                while len(products) > 4:
                    multiply()
                if more:
                    choose(it + 1, multiply)
                while products:
                    multiply()

            for v in range(2):
                norm.scale(dve, v, v, xn[:, 0, v, :])
            choose(0, lambda: None)
            loop(dve, body)
            for s in range(sum_lag):
                if s < gate_lag:
                    product(earlier(s, gate_lag, chip.quads // 2), 0)
                add(earlier(s, sum_lag, chip.quads // 2))
                if s < gate_lag:
                    product(earlier(s, gate_lag, chip.quads // 2), 1)


def heads_attention(chip):
    nc, op, ident = chip.nc, chip.operand, chip.operand["ident"]
    hd = D // HEADS3
    wide = HEADS3 * (P + hd) + 64
    with ExitStack() as ctx:
        def sb(n, shape, dt=F32):
            return ctx.enter_context(nc.sbuf_tensor(f"a3_{n}", shape, dt))

        def sem(n):
            return chip.semaphore(f"a3_{n}")

        square, centred, log, rstd = sb("square", [P, QN]), sb("centred", [P, QN]), sb("log", [P, QN]), sb("rstd", [P, QN])
        xn = sb("xn", [P, 2, QN])
        query = sb("query", [P, QN])
        query_b = sb("query_b", [P, 2, HEADS3, 6, 2, 64])
        key = sb("key", [P, 2, QN])
        value = sb("value", [P, 2, 2, wide])
        value_z = sb("value_z", [P, 2, 2, wide])
        peak = sb("peak", [P, 2, 3, 2])
        total = sb("total", [P, 2, 3, 2])
        inverse = sb("inverse", [P, 2, 3, 2])
        prob = sb("prob", [P, 2, 3, 2, T])
        even = sb("even", [P, 2, 3, 2, T])
        prob_t = sb("prob_t", [P, 2, 3, QN])
        mix_b = sb("mix_b", [P, QN], BF16)
        mix = sb("mix", [P, QN])

        cleared, pool_passed = sem("cleared"), sem("pool_passed")
        centre_done, centre_kept, average_done, log_ready, rstd_ready, xn_ready = (sem(n) for n in (
            "centre_done", "centre_kept", "average_done", "log_ready", "rstd_ready", "xn_ready"))
        query_done, query_ready, query_b_ready = sem("query_done"), sem("query_ready"), sem("query_b_ready")
        key_done, key_ready, value_done, value_ready = sem("key_done"), sem("key_ready"), sem("value_done"), sem("value_ready")
        heads = range(HEADS3)
        scored, peak_ready, exp_ready, inverse_ready, even_act, even_dve, prob_done, prob_act, prob_dve, mixed = (
            [sem(f"{n}{h}") for h in heads] for n in (
                "scored", "peak_ready", "exp_ready", "inverse_ready", "even_act", "even_dve", "prob_done",
                "prob_act", "prob_dve", "mixed"))
        mix_b_ready, mix_ready, left, h_ready = sem("mix_b_ready"), sem("mix_ready"), sem("left"), sem("h_ready")

        spare = chip.psum[:, 7, 0:QN]

        def scores_of(h):
            at = 3 * (h % 2)
            return chip.psum[:, at:at + 3, 0:QN].rearrange("p c (g t) -> p c g t", t=T)

        def turned_of(h, s):
            return chip.psum[:, 3 * (h % 2) + s, 0:QN]

        def at_start(q):
            return isinstance(q, int) and q == 0

        def earlier(u, q, h, n):
            if h >= n:
                return u, q, h - n
            return None if at_start(q) else (1 - u, q - 1, h - n + HEADS3)

        def loop(eng, quad):
            turns = chip.quads // 2

            def both(it, last):
                for u in range(2):
                    quad(u, 2 * it + u, not (last and u == 1), not last)

            both(0, turns == 1)
            if turns > 2:
                with eng.Fori(1, turns - 1) as it:
                    both(it, False)
            if turns > 1:
                both(turns - 1, True)

        after_last = (0, chip.quads)

        block = ctx.enter_context(nc.Block())

        @block.tensor
        def _(pe):
            def centre(q):
                nc.tensor.matmul(spare, op["centre"], chip.h_quad(q), start=True, stop=True).then_inc(centre_done, 1)

            def average(q):
                pe.wait_ge(centre_kept, 2 * q + 2)
                nc.tensor.matmul(spare, op["mean"], square[:, :], start=True, stop=True).then_inc(average_done, 1)

            def queries(u, q):
                pe.wait_ge(xn_ready, q + 1)
                nc.tensor.matmul(spare, op["a3_wq"], xn[:, u, :], start=True, stop=True).then_inc(query_done, 1)

            def keys(u, q):
                pe.wait_ge(query_ready, q + 1)
                nc.tensor.matmul(spare, op["a3_wk"], xn[:, u, :], start=True, stop=True).then_inc(key_done, 1)

            def values(u, q):
                pe.wait_ge(key_ready, q + 1)
                for s in range(3):
                    last = nc.tensor.matmul(spare[:, s * P:(s + 1) * P], xn[:, u, s * P:(s + 1) * P],
                                            op["a3_wv"], start=True, stop=True)
                last.then_inc(value_done, 1)

            def leave(q):
                pe.wait_ge(mix_ready, q + 1)
                nc.tensor.matmul(spare, op["a3_wo"], mix[:, :], start=True, stop=True).then_inc(left, 1)

            def score(u, q, h):
                if h == 0:
                    pe.wait_ge(query_b_ready, q + 1)
                    pe.wait_ge(key_ready, q + 1)
                before = earlier(u, q, h, 2)
                if before:
                    pe.wait_ge(prob_act[before[2]], 2 * before[1] + 2)
                    pe.wait_ge(prob_dve[before[2]], before[1] + 1)
                for c in range(3):
                    for pair in range(2):
                        last = nc.tensor.matmul(scores_of(h)[:, c, pair, :],
                                                query_b[:, u, h, 3 * pair + c, :, :].rearrange("p b t -> p (b t)"),
                                                key[:, u, pair * T:(pair + 1) * T], start=True, stop=True)
                last.then_inc(scored[h], 1)

            def turn(step):
                if step is None:
                    return
                u, q, h = step
                pe.wait_ge(even_dve[h], q + 1)
                pe.wait_ge(even_act[h], q + 1)
                for s in range(3):
                    for c in range(3):
                        probs = even[:, h % 2, c, :, :].rearrange("p g t -> p (g t)")[:, s * P:(s + 1) * P]
                        last = nc.tensor.transpose(turned_of(h, s)[:, c * P:(c + 1) * P], probs, ident)
                last.then_inc(prob_done[h], 1)

            def mixing(step):
                if step is None:
                    return
                u, q, h = step
                pe.wait_ge(prob_act[h], 2 * q + 2)
                pe.wait_ge(prob_dve[h], q + 1)
                if h == 0:
                    pe.wait_ge(value_ready, q + 1)
                    if not at_start(q):
                        pe.wait_ge(mix_b_ready, q)
                for pair in range(2):
                    for middle in (False, True):
                        for b in range(2):
                            v = (value_z if middle else value)[:, u, pair, h * P + b * D:h * P + (b + 1) * D]
                            probs = prob_t[:, h % 2, 1 if middle else 2 * pair, :].rearrange(
                                "p (c b t) -> p b c t", c=3, b=2)[:, b, :, :]
                            last = nc.tensor.matmul(
                                chip.psum[64 * b:64 * b + 64, 6, pair * T:(pair + 1) * T]
                                .rearrange("p (c t) -> p c t", c=3), v, probs,
                                start=(h == 0 and pair == 0 and not middle),
                                stop=(h == HEADS3 - 1 and middle), skip_group_check=True)
                last.then_inc(mixed[h], 1)

            def quad(u, q, more, more2):
                for h in heads:
                    score(u, q, h)
                    if h == 0 and more:
                        if not (isinstance(q, int) and q < 2):
                            pe.wait_ge(h_ready, q - 1)
                        queries(1 - u, q + 1)
                    if h == 2 and more2:
                        pe.wait_ge(value_ready, q + 2)
                        centre(q + 2)
                    turn(earlier(u, q, h, 1))
                    if h == 1 and more:
                        values(1 - u, q + 1)
                    if h == 3 and not at_start(q):
                        if more2:
                            pe.wait_ge(log_ready, q + 3)
                        leave(q - 1)
                    mixing(earlier(u, q, h, 2))
                    if h == 0 and more:
                        keys(1 - u, q + 1)
                    if h == 2 and more2:
                        average(q + 2)

            pe.wait_ge(cleared, 2)
            for q in range(2):
                if q:
                    pe.wait_ge(log_ready, q)
                centre(q)
                average(q)
            pe.wait_ge(log_ready, 2)
            queries(0, 0)
            keys(0, 0)
            values(0, 0)
            pe.wait_ge(value_ready, 1)
            loop(pe, quad)
            turn(earlier(*after_last, 0, 1))
            mixing(earlier(*after_last, 0, 2))
            mixing(earlier(*after_last, 1, 2))
            leave(chip.quads - 1)

        @block.scalar
        def _(act):
            nc.scalar.preload_act_table_set("natural_log_exp_and_others")

            def keep_centre(q):
                act.wait_ge(centre_done, q + 1)
                nc.scalar.activation(square[:, :], spare, ACT.Square).then_inc(centre_kept, 1)
                if not at_start(q):
                    act.wait_ge(xn_ready, q)
                nc.scalar.activation(centred[:, :], spare, ACT.Copy).then_inc(centre_kept, 1)

            def deviation(q):
                act.wait_ge(average_done, q + 1)
                nc.scalar.activation(log[:, :], spare, ACT.Ln, bias=chip.eps[:, 0:1]).then_inc(log_ready, 1)
                act.wait_ge(log_ready, q + 1)
                nc.scalar.activation(rstd[:, :], log[:, :], ACT.Exp, scale=-0.5).then_inc(rstd_ready, 1)

            def keep_keys(u, q):
                act.wait_ge(key_done, q + 1)
                nc.scalar.activation(key[:, u, :], spare, ACT.Identity, bias=op["a3_bk"]).then_inc(key_ready, 1)

            def keep_turned(step):
                if step is None:
                    return
                u, q, h = step
                act.wait_ge(prob_done[h], q + 1)
                before = earlier(u, q, h, 2)
                if before:
                    act.wait_ge(mixed[before[2]], before[1] + 1)
                for s in (0, 2):
                    nc.scalar.activation(prob_t[:, h % 2, s, :], turned_of(h, s), ACT.Copy).then_inc(prob_act[h], 1)

            def round_mix(q):
                act.wait_ge(mixed[HEADS3 - 1], q + 1)
                nc.scalar.activation(mix_b[:, :], chip.psum[:, 6, 0:QN], ACT.Copy).then_inc(mix_b_ready, 1)

            def quad(u, q, more, more2):
                for h in heads:
                    keep_turned(earlier(u, q, h, 1))
                    if h == 2 and more2:
                        keep_centre(q + 2)
                    act.wait_ge(peak_ready[h], q + 1)
                    for c in range(3):
                        for pair in range(2):
                            last = nc.scalar.activation(prob[:, h % 2, c, pair, :], scores_of(h)[:, c, pair, :], ACT.Exp,
                                                        bias=peak[:, h % 2, c, pair:pair + 1],
                                                        accum_out=total[:, h % 2, c, pair:pair + 1])
                    last.then_inc(exp_ready[h], 1)
                    act.wait_ge(inverse_ready[h], q + 1)
                    for pair in range(2):
                        last = nc.scalar.activation(even[:, h % 2, 2, pair, :], prob[:, h % 2, 2, pair, :], ACT.Copy,
                                                    scale=inverse[:, h % 2, 2, pair:pair + 1])
                    last.then_inc(even_act[h], 1)
                    if h == 0 and more:
                        keep_keys(1 - u, q + 1)
                    if h == 1 and not at_start(q):
                        round_mix(q - 1)
                    if h == 2 and more2:
                        deviation(q + 2)

            for q in range(2):
                keep_centre(q)
                deviation(q)
            keep_keys(0, 0)
            loop(act, quad)
            keep_turned(earlier(*after_last, 0, 1))
            round_mix(chip.quads - 1)

        @block.vector
        def _(dve):
            def normed(u, q):
                dve.wait_ge(rstd_ready, q + 1)
                nc.vector.tensor_tensor(xn[:, u, :], centred[:, :], rstd[:, :], ALU.mult).then_inc(xn_ready, 1)

            def keep_queries(q):
                dve.wait_ge(query_done, q + 1)
                if not at_start(q):
                    dve.wait_ge(query_b_ready, q)
                nc.vector.tensor_scalar(query[:, :], spare, op["a3_bq"], hd ** -0.5,
                                        ALU.add, ALU.mult).then_inc(query_ready, 1)

            def keep_values(u, q):
                dve.wait_ge(value_done, q + 1)
                if not (isinstance(q, int) and q < 2):
                    dve.wait_ge(mixed[HEADS3 - 1], q - 1)
                slices = spare.rearrange("p (s b h e) -> p s b h e", s=3, b=2, h=HEADS3)
                bv = op["a3_bv"].rearrange("p (b h e) -> p b h e", b=2, h=HEADS3)
                for b in range(2):
                    def heads_of(tile):
                        return tile[:, b * D:b * D + HEADS3 * (P + hd)].rearrange(
                            "p (h c) -> p h c", h=HEADS3)[:, :, 0:hd]

                    for n, s in ((0, 0), (1, 2)):
                        nc.vector.tensor_tensor(heads_of(value[:, u, n, :]), slices[:, s, b, :, :], bv[:, b, :, :], ALU.add)
                    for pair in range(2):
                        half = slice(64 * pair, 64 * pair + 64)
                        last = nc.vector.tensor_tensor(heads_of(value_z[half, u, pair, :]), slices[half, 1, b, :, :],
                                                       bv[half, b, :, :], ALU.add)
                last.then_inc(value_ready, 1)

            def keep_turned(step):
                if step is None:
                    return
                u, q, h = step
                dve.wait_ge(prob_done[h], q + 1)
                before = earlier(u, q, h, 2)
                if before:
                    dve.wait_ge(mixed[before[2]], before[1] + 1)
                nc.vector.tensor_copy(prob_t[:, h % 2, 1, :], turned_of(h, 1)).then_inc(prob_dve[h], 1)

            def widen_mix(q):
                dve.wait_ge(mix_b_ready, q + 1)
                nc.vector.tensor_copy(mix[:, :], mix_b[:, :]).then_inc(mix_ready, 1)

            def finish(q):
                dve.wait_ge(left, q + 1)
                nc.vector.scalar_tensor_tensor(chip.h_quad(q), spare, op["a3_bo"],
                                               chip.h_quad(q), ALU.add, ALU.add).then_inc(h_ready, 1)

            def quad(u, q, more, more2):
                for h in heads:
                    dve.wait_ge(scored[h], q + 1)
                    nc.vector.tensor_reduce(peak[:, h % 2, :, :], scores_of(h), X, ALU.max,
                                            negate=True).then_inc(peak_ready[h], 1)
                    keep_turned(earlier(u, q, h, 1))
                    if h == 0 and more:
                        keep_queries(q + 1)
                    if h == 1 and more:
                        keep_values(1 - u, q + 1)
                    if h == 2 and not at_start(q):
                        widen_mix(q - 1)
                    if h == 3:
                        if not at_start(q):
                            finish(q - 1)
                        if more2:
                            normed(u, q + 2)
                    dve.wait_ge(exp_ready[h], q + 1)
                    nc.vector.reciprocal(inverse[:, h % 2, :, :], total[:, h % 2, :, :]).then_inc(inverse_ready[h], 1)
                    dve.wait_ge(inverse_ready[h], q + 1)
                    for c in range(2):
                        for pair in range(2):
                            last = nc.vector.tensor_scalar(even[:, h % 2, c, pair, :], prob[:, h % 2, c, pair, :],
                                                           inverse[:, h % 2, c, pair:pair + 1], None, ALU.mult)
                    last.then_inc(even_dve[h], 1)

            for q in range(2):
                normed(q, q)
            keep_queries(0)
            dve.wait_ge(cleared, 2)
            keep_values(0, 0)
            loop(dve, quad)
            keep_turned(earlier(*after_last, 0, 1))
            widen_mix(chip.quads - 1)
            finish(chip.quads - 1)

        @block.gpsimd
        def _(pool):
            nc.gpsimd.memset(value[:, :, :, :], 0.0).then_inc(cleared, 1)
            nc.gpsimd.memset(value_z[:, :, :, :], 0.0).then_inc(cleared, 1)

            def spread_queries(u, q):
                pool.wait_ge(query_ready, q + 1)
                if not (isinstance(q, int) and q < 2):
                    pool.wait_ge(scored[HEADS3 - 1], q - 1)
                pool.sem_inc(pool_passed, 1)
                for h in heads:
                    for b in range(2):
                        last = nc.gpsimd.tensor_scalar(query_b[:, u, h, :, b, :],
                                                       query[:, :].rearrange("p (c t) -> p c t", t=64),
                                                       op["a3_heads"][:, 2 * h + b:2 * h + b + 1], None, ALU.mult)
                last.then_inc(query_b_ready, 1)

            def quad(u, q, more, more2):
                if more:
                    spread_queries(1 - u, q + 1)

            spread_queries(0, 0)
            loop(pool, quad)


def experts3(chip):
    nc, op, ident = chip.nc, chip.operand, chip.operand["ident"]
    groups = E3 * F3 // P
    with ExitStack() as ctx:
        def sb(n, shape, dt=F32):
            return ctx.enter_context(nc.sbuf_tensor(f"f3_{n}", shape, dt))

        def sem(n):
            return chip.semaphore(f"f3_{n}")

        norm = Norm(chip, ctx, "f3_norm", lambda u, i: chip.psum[:, 6 + i, :])
        xn = sb("xn", [P, 2, QN])
        first_layer = Split(chip, ctx, "f3_split", op["f3_w1"])
        shut = sb("shut", [P, groups * P], BF16)
        scores = sb("scores", [P, 6, E3])
        equal, ranked = sb("equal", [P, 6, E3]), sb("ranked", [P, 6, E3])
        best, first = sb("best", [P, 6]), sb("first", [P, 6])
        hot = sb("hot", [P, 6, 2 * E3])
        hot_t = sb("hot_t", [P, 2, QN])
        hot_b = sb("hot_b", [P, 2, QN], BF16)
        hid = sb("hid", [P, 2, 2, QN])
        final = sb("final", [P, 2, QN])
        tokens = sb("tokens", [P, 2, 3, 2, D])

        set_up = sem("set_up")
        scored, hot_ready, hot_done = sem("scored"), sem("hot_ready"), sem("hot_done")
        hot_b_ready, hot_t_ready = sem("hot_b_ready"), sem("hot_t_ready")
        steps = [sem(f"step{n}") for n in range(5)]
        hid_done, hid_act, hid_dve, used = (
            [sem(f"{n}{g}") for g in range(groups)] for n in ("hid_done", "hid_act", "hid_dve", "used"))
        final_ready, final_done, tokens_ready = sem("final_ready"), sem("final_done"), sem("tokens_ready")
        stored = [sem(f"stored{u}") for u in range(2)]

        def at_start(q):
            return isinstance(q, int) and q == 0

        def loop(eng, quad):
            turns = chip.quads // 2

            def both(it, last):
                for u in range(2):
                    quad(u, 2 * it + u, it, not (last and u == 1))

            both(0, turns == 1)
            if turns > 2:
                with eng.Fori(1, turns - 1) as it:
                    both(it, False)
            if turns > 1:
                both(turns - 1, True)

        block = ctx.enter_context(nc.Block())

        @block.tensor
        def _(pe):
            def route(u, q):
                pe.wait_ge(norm.ready, q + 1)
                for j in range(3):
                    for b in range(2):
                        last = nc.tensor.matmul(chip.psum[:, 7, (2 * j + b) * E3:(2 * j + b + 1) * E3],
                                                xn[:, u, j * P:(j + 1) * P],
                                                op["f3_rw"][:, b * D:b * D + E3], start=True, stop=True)
                last.then_inc(scored, 1)

            def turn_choice(q):
                pe.wait_ge(hot_ready, q + 1)
                for j in range(3):
                    last = nc.tensor.transpose(chip.psum[:, 6, j * P:(j + 1) * P],
                                               hot[:, 2 * j:2 * j + 2, :].rearrange("p g e -> p (g e)"), ident)
                last.then_inc(hot_done, 1)

            def hidden(u, q, g):
                if g >= 2:
                    pe.wait_ge(hid_act[g - 2], q + 1)
                    pe.wait_ge(hid_dve[g - 2], q + 1)
                elif not at_start(q):
                    pe.wait_ge(hid_act[groups - 2 + g], q)
                    pe.wait_ge(hid_dve[groups - 2 + g], q)
                if g == 0:
                    first_layer.wait_x(pe, q)
                for b in range(2):
                    first_layer.product(chip.psum[:, 2 * (g % 2) + b, 0:QN], u, b, slice(g * P, (g + 1) * P), False)
                if g == 0:
                    pe.wait_ge(hot_b_ready, q + 1)
                for b in range(2):
                    half = slice(64 * b, 64 * b + 64)
                    last = nc.tensor.matmul(chip.psum[:, 2 * (g % 2) + b, 0:QN], shut[half, g * P:(g + 1) * P],
                                            hot_b[half, u, :], start=False, stop=True)
                last.then_inc(hid_done[g], 1)

            def base(u, q):
                pe.wait_ge(hot_t_ready, q + 1)
                if not at_start(q):
                    pe.wait_ge(final_ready, q)
                nc.tensor.matmul(chip.psum[:, 4, 0:QN], op["f3_b2"], hot_t[:, u, :],
                                 start=True, stop=False, skip_group_check=True)

            def output(q, g):
                pe.wait_ge(hid_act[g], q + 1)
                pe.wait_ge(hid_dve[g], q + 1)
                for b in range(2):
                    last = nc.tensor.matmul(chip.psum[64 * b:64 * b + 64, 4, 0:QN],
                                            op["f3_w2"][:, g * D:(g + 1) * D], hid[:, g % 2, b, :],
                                            start=False, stop=(g == groups - 1), skip_group_check=True)
                last.then_inc(used[g], 1)

            def turn_result(u, q):
                pe.wait_ge(final_ready, q + 1)
                if not at_start(q):
                    pe.wait_ge(tokens_ready, q)
                for j in range(3):
                    last = nc.tensor.transpose(chip.psum[:, 5, j * P:(j + 1) * P],
                                               final[:, u, j * P:(j + 1) * P], ident)
                last.then_inc(final_done, 1)

            def quad(u, q, it, more):
                for g in range(groups):
                    hidden(u, q, g)
                    if g == 0 and more:
                        pe.wait_ge(hot_t_ready, q + 1)
                        norm.centre(1 - u, chip.h_quad(q + 1))
                    if g == 1:
                        base(u, q)
                    if g:
                        output(q, g - 1)
                    elif not at_start(q):
                        output(q - 1, groups - 1)
                    if g == 0 and more:
                        norm.average(pe, 1 - u, q + 1)
                    if g == 1 and more:
                        route(1 - u, q + 1)
                    if g == 2 and not at_start(q):
                        turn_result(1 - u, q - 1)
                    if g == 3 and more:
                        turn_choice(q + 1)

            pe.wait_ge(set_up, 2)
            norm.centre(0, chip.h_quad(0))
            norm.average(pe, 0, 0)
            route(0, 0)
            turn_choice(0)
            first_layer.wait_weight(pe)
            loop(pe, quad)
            output(chip.quads - 1, groups - 1)
            turn_result(1, chip.quads - 1)

        @block.scalar
        def _(act):
            nc.scalar.preload_act_table_set("natural_log_exp_and_others")

            def keep_choice(u, q):
                act.wait_ge(hot_done, q + 1)
                nc.scalar.activation(hot_b[:, u, :], chip.psum[:, 6, 0:QN], ACT.Copy).then_inc(hot_b_ready, 1)
                nc.scalar.activation(hot_t[:, u, :], chip.psum[:, 6, 0:QN], ACT.Copy).then_inc(hot_t_ready, 1)

            def keep_tokens(u, q, it):
                act.wait_ge(final_done, q + 1)
                if not (isinstance(it, int) and it == 0):
                    act.wait_ge(stored[u], 64 * it)
                nc.scalar.activation(tokens[:, u, :, :, :], chip.psum[:, 5, 0:QN]
                                     .rearrange("p (j b d) -> p j b d", j=3, b=2), ACT.Copy).then_inc(tokens_ready, 1)

            def quad(u, q, it, more):
                for g in range(groups):
                    act.wait_ge(hid_done[g], q + 1)
                    if g >= 2:
                        act.wait_ge(used[g - 2], q + 1)
                    elif not at_start(q):
                        act.wait_ge(used[groups - 2 + g], q)
                    nc.scalar.activation(hid[:, g % 2, 0, :], chip.psum[:, 2 * (g % 2), 0:QN], ACT.Relu,
                                         bias=op["f3_b1"][:, g:g + 1]).then_inc(hid_act[g], 1)
                    if g == 0 and more:
                        norm.squares(act, 1 - u, q + 1)
                        norm.logs(act, 1 - u, q + 1)
                        norm.powers(act, 1 - u, q + 1)
                    if g == 2 and not at_start(q):
                        keep_tokens(1 - u, q - 1, it - 1 + u)
                    if g == 2 and more:
                        first_layer.place_other(act, 1 - u, q + 1, 0)
                    if g == 3 and more:
                        first_layer.place_other(act, 1 - u, q + 1, 1)
                if more:
                    keep_choice(1 - u, q + 1)

            norm.squares(act, 0, 0)
            norm.logs(act, 0, 0)
            norm.powers(act, 0, 0)
            first_layer.swap_weight(act)
            keep_choice(0, 0)
            first_layer.place_other(act, 0, 0, 0)
            first_layer.place_other(act, 0, 0, 1)
            loop(act, quad)
            keep_tokens(1, chip.quads - 1, chip.quads // 2 - 1)

        @block.vector
        def _(dve):
            nc.vector.tensor_copy(shut[:, :], op["f3_shut"]).then_inc(set_up, 1)
            nc.vector.memset(hot[:, :, :], 0.0).then_inc(set_up, 1)
            dve.wait_ge(set_up, 2)

            def wide(a):
                return a[:, :].unsqueeze(2).to_broadcast([P, 6, E3])

            def choose(q):
                ranks = op["f3_rank"].rearrange("p (g e) -> p g e", e=E3)
                dve.wait_ge(scored, q + 1)
                nc.vector.tensor_tensor(scores[:, :, :].rearrange("p g e -> p (g e)"), chip.psum[:, 7, 0:6 * E3],
                                        op["f3_rb"], ALU.add).then_inc(steps[0], 1)
                dve.wait_ge(steps[0], q + 1)
                nc.vector.tensor_reduce(best[:, :], scores[:, :, :], X, ALU.max).then_inc(steps[1], 1)
                dve.wait_ge(steps[1], q + 1)
                nc.vector.tensor_tensor(equal[:, :, :], scores[:, :, :], wide(best), ALU.is_equal).then_inc(steps[2], 1)
                dve.wait_ge(steps[2], q + 1)
                nc.vector.tensor_tensor(ranked[:, :, :], equal[:, :, :], ranks, ALU.mult).then_inc(steps[3], 1)
                dve.wait_ge(steps[3], q + 1)
                nc.vector.tensor_reduce(first[:, :], ranked[:, :, :], X, ALU.max).then_inc(steps[4], 1)
                dve.wait_ge(steps[4], q + 1)
                if not at_start(q):
                    dve.wait_ge(hot_done, q)
                nc.vector.tensor_tensor(hot[:, :, 0:E3], ranks, wide(first), ALU.is_equal).then_inc(hot_ready, 1)

            def finish(u, q):
                dve.wait_ge(used[groups - 1], q + 1)
                nc.vector.scalar_tensor_tensor(final[:, u, :], chip.psum[:, 4, 0:QN], 0.0, chip.h_quad(q),
                                               ALU.max, ALU.add).then_inc(final_ready, 1)

            def quad(u, q, it, more):
                for g in range(groups):
                    dve.wait_ge(hid_done[g], q + 1)
                    if g >= 2:
                        dve.wait_ge(used[g - 2], q + 1)
                    elif not at_start(q):
                        dve.wait_ge(used[groups - 2 + g], q)
                    nc.vector.tensor_scalar(hid[:, g % 2, 1, :], chip.psum[:, 2 * (g % 2) + 1, 0:QN],
                                            op["f3_b1"][:, g:g + 1], 0.0, ALU.add, ALU.max).then_inc(hid_dve[g], 1)
                    if g == 0 and not at_start(q):
                        finish(1 - u, q - 1)
                    if g == 0 and more:
                        norm.scale(dve, 1 - u, q + 1, xn[:, 1 - u, :])
                    if g == 2 and more:
                        first_layer.place_high(dve, 1 - u, q + 1)
                        choose(q + 1)

            first_layer.split_weight(dve)
            norm.scale(dve, 0, 0, xn[:, 0, :])
            first_layer.place_high(dve, 0, 0)
            choose(0)
            loop(dve, quad)
            finish(1, chip.quads - 1)

        @block.gpsimd
        def _(pool):
            def split(u, q):
                pool.wait_ge(norm.ready, q + 1)
                for _ in first_layer.split(pool, xn[:, u, :], q):
                    pass

            split(0, 0)
            loop(pool, lambda u, q, it, more: split(1 - u, q + 1) if more else None)

        @block.sync
        def _(sp):
            def quad(u, q, it, more):
                sp.wait_ge(tokens_ready, q + 1)
                for chunk, rows, pair, t in ((0, slice(0, 128), 0, 0), (1, slice(0, 64), 0, 128),
                                             (1, slice(64, 128), 1, 0), (2, slice(0, 128), 1, 64)):
                    n = rows.stop - rows.start
                    out = chip.out[bass.ds(4 * q + 2 * pair, 2), t:t + n, :].rearrange("b t d -> t b d")
                    sp.dma_start(out, tokens[rows, u, chunk, :, :]).then_inc(stored[u], 16)

            loop(sp, quad)
            for u in range(2):
                sp.wait_ge(stored[u], 64 * (chip.quads // 2))


def build(nc, images, tokens, neighbours, embed, pack_a, pack_b, pack_c, routes, out, quads=BATCH // 4):
    with ExitStack() as ctx:
        def sb(n, shape, dt=F32):
            return ctx.enter_context(nc.sbuf_tensor(f"{n}_sbuf", shape, dt))

        hidden = sb("hidden", [P, 2 * quads * T])
        eps = sb("eps", [P, 1])
        weights_b = sb("weights_b", [P, columns(PACK_B)[1]])
        psum = ctx.enter_context(nc.psum_tensor("psum", [P, 8, 512], F32))
        chip = Chip(nc, quads, hidden, psum, eps)
        chip.place(PACK_B, weights_b)
        loaded_b = ctx.enter_context(nc.semaphore("loaded_b"))
        loaded_c = ctx.enter_context(nc.semaphore("loaded_c"))
        chip.routes = sb("routes", [1, E1 * 4], I32)
        chip.out = out
        loaded = ctx.enter_context(nc.semaphore("loaded"))

        with ExitStack() as first:
            chip.tokens = first.enter_context(nc.sbuf_tensor("tokens_sbuf", [TT, BATCH], I32))
            chip.embed = first.enter_context(nc.sbuf_tensor("embed_sbuf", [P, 8 * D], F32))
            weights_a = first.enter_context(nc.sbuf_tensor("weights_a", [P, columns(PACK_A)[1]], F32))
            chip.place(PACK_A, weights_a)
            with nc.Block() as block:
                @block.vector
                def _(dve):
                    nc.vector.memset(eps[:, :], EPS)

                @block.sync
                def _(sp):
                    sp.dma_start(chip.tokens[:, :], tokens).then_inc(loaded, 16)
                    sp.dma_start(chip.embed[:, :], embed).then_inc(loaded, 16)
                    sp.dma_start(weights_a[:, :], pack_a).then_inc(loaded, 16)
                    sp.dma_start(chip.routes[:, :], routes).then_inc(loaded, 16)
                    sp.dma_start(weights_b[:, :], pack_b).then_inc(loaded_b, 16)
                    sp.wait_ge(loaded, 64)
            embedding(chip, images, neighbours)
            chip.end_phase()

        weights_c = sb("weights_c", [P, columns(PACK_C)[1]])
        chip.place(PACK_C, weights_c)
        with nc.Block() as block:
            @block.sync
            def _(sp):
                sp.dma_start(weights_c[:, :], pack_c).then_inc(loaded_c, 16)
                sp.wait_ge(loaded_b, 16)

        attention(chip, "a0", 1.0, D ** -0.5)
        chip.end_phase()
        experts0(chip)
        chip.end_phase()
        linear_attention(chip)
        chip.end_phase()
        with nc.Block() as block:
            @block.sync
            def _(sp):
                sp.wait_ge(loaded_c, 16)

        routed(chip)
        chip.end_phase()
        attention(chip, "a2", D ** -0.5, 1.0)
        chip.end_phase()
        experts2(chip)
        chip.end_phase()
        heads_attention(chip)
        chip.end_phase()
        experts3(chip)
        chip.end_phase()



def twice(a):
    out = np.zeros((P,) + a.shape[1:], np.float32)
    out[:a.shape[0]] = a
    out[64:64 + a.shape[0]] = a
    return out


def diagonal(a, rows=64, cols=None):
    cols = a.shape[1] if cols is None else cols
    out = np.zeros((P, 2 * cols), np.float32)
    for b in range(2):
        out[b * rows:b * rows + a.shape[0], b * cols:b * cols + a.shape[1]] = a
    return out


def spread(a, n=6):
    return np.tile(np.asarray(a).reshape(1, -1), (P, n))


def filters():
    def haar(n, sign):
        m = np.zeros((n // 2, n))
        m[np.arange(n // 2), 2 * np.arange(n // 2)] = 0.7071067811865476
        m[np.arange(n // 2), 2 * np.arange(n // 2) + 1] = sign * 0.7071067811865476
        return m

    def resize(n):
        step = n / 8
        at = (np.arange(8)[:, None] + 0.5) * step - 0.5
        w = np.maximum(0, 1 - np.abs(at - np.arange(n)[None, :]) / step)
        return w / w.sum(axis=1, keepdims=True)

    low = haar(IMG, 1)
    return np.stack([resize(56) @ haar(HALF, 1) @ low, resize(56) @ haar(HALF, -1) @ low,
                     resize(112) @ low, resize(112) @ haar(IMG, -1)])


def pack(which, parts):
    where, width = columns(which)
    out = np.zeros((P, width), np.float32)
    for name, (at, n) in where.items():
        a = np.asarray(parts[name])
        a = a.reshape(a.shape[0], -1)
        assert a.shape[1] == n, (name, a.shape, n)
        out[:a.shape[0], at:at + n] = a
    return out


def pack_operands(**w):
    w = {k: np.asarray(v) for k, v in w.items()}
    f = filters().reshape(32, IMG)
    eye = np.eye(P)
    parts = {
        "rows": f.reshape(32, HALF, 2).transpose(1, 2, 0).reshape(HALF, 64),
        "cols": f.reshape(32, 2, HALF).transpose(2, 1, 0).reshape(HALF, 64),
        "tok_b": twice(w["L0_tok_b"][:, None]),
        "ident_a": eye,
        "ident": eye,
        "centre": diagonal(np.eye(D) - 1 / D),
        "mean": diagonal(np.full((D, D), 1 / D)),
    }
    for n, layer in (("a0", "L0"), ("a2", "L2")):
        parts[f"{n}_wk"] = diagonal(w[f"{layer}_attn_Wk"])
        parts[f"{n}_wq"] = diagonal(w[f"{layer}_attn_Wq"])
        parts[f"{n}_wv"] = diagonal(w[f"{layer}_attn_Wv"].T)
    parts |= {
        "f0_gate_w": diagonal(w["L0_ffn_gate_w"]), "f0_gate_b": spread(w["L0_ffn_gate_b"]),
        "f0_rank": spread(np.arange(E0, 0, -1)),
        "f0_w1": twice(w["L0_ffn_w1"].transpose(1, 0, 2).reshape(D, -1)),
        "f0_b1": w["L0_ffn_b1"].T,
        "f0_w2": w["L0_ffn_w2"].transpose(1, 0, 2).reshape(F0, -1),
        "f0_b2": np.tile(diagonal(w["L0_ffn_b2"], rows=E0)[0:2 * E0], (3, 1)),
        "f0_pick": np.tile(np.eye(2 * E0).reshape(2 * E0, 2, E0).transpose(0, 2, 1).reshape(2 * E0, -1), (3, 1)),
        "f0_gamma": twice(w["L0_ffn_gamma"][:, None]), "f0_beta": twice(w["L0_ffn_beta"][:, None]),
        "a1_wq": diagonal(w["L1_attn_Wqkv"][:, 0:64]), "a1_wk": diagonal(w["L1_attn_Wqkv"][:, 64:128]),
        "a1_wv": diagonal(w["L1_attn_Wqkv"][:, 128:192]), 
        "a1_wo": np.stack([diagonal(np.tile(w["L1_attn_Wout"][8 * jr:8 * jr + 8], (8, 1))) for jr in range(8)], axis=1),
        "a1_heads": np.kron(np.eye(16), np.ones((8, 8))),
        "a1_head": np.kron(np.ones((2, 1)), np.kron(np.eye(8), np.ones((8, 1)))),
        "a1_bo": twice(w["L1_attn_bout"][:, None]),
        "a1_gamma": twice(w["L1_attn_gamma"][:, None]), "a1_beta": twice(w["L1_attn_beta"][:, None]),
        "f1_wi": twice(w["L1_ffn_Wi"].T), "f1_bi": w["L1_ffn_bi"][:, None],
        "f1_wr": w["L1_ffn_Wr"].transpose(3, 0, 1, 2).reshape(F1, -1),
        "f1_br": w["L1_ffn_br"].transpose(2, 0, 1).reshape(F1, -1),
        "f1_ws": w["L1_ffn_Ws"][:, 0].transpose(2, 0, 1).reshape(F1, -1),
        "f1_bs": w["L1_ffn_bs"][:, 0].T,
        "f1_wo": w["L1_ffn_Wo"].T, "f1_bo": twice(w["L1_ffn_bo"][:, None]),
        "f2_rw1": diagonal(w["L2_ffn_router_w1"]),
        "f2_rb1": np.concatenate([w["L2_ffn_router_b1"]] * 2)[:, None],
        "f2_rw2": diagonal(w["L2_ffn_router_w2"], rows=R2), "f2_rb2": spread(w["L2_ffn_router_b2"], 12),
        "f2_rank": spread(np.arange(E2, 0, -1)),
        "f2_w1": twice(w["L2_ffn_expert_w1"].transpose(1, 0, 2).reshape(D, -1)),
        "f2_b1": w["L2_ffn_expert_b1"].reshape(3, P).T, "f2_b2": w["L2_ffn_expert_b2"].reshape(3, P).T,
        "f2_b3": np.tile(diagonal(w["L2_ffn_expert_b3"], rows=E2)[0:2 * E2], (3, 1)),
        "f2_pick": np.tile(np.eye(2 * E2).reshape(2 * E2, 2, 3, 2).transpose(0, 2, 1, 3).reshape(2 * E2, -1), (3, 1)),
        "a3_wq": diagonal(w["L3_attn_Wq"].T), "a3_bq": twice(w["L3_attn_bq"][:, None]),
        "a3_wk": diagonal(w["L3_attn_Wk"].T), "a3_bk": twice(w["L3_attn_bk"][:, None]),
        "a3_wv": diagonal(w["L3_attn_Wv"].T), "a3_bv": spread(w["L3_attn_bv"], 2),
        "a3_wo": diagonal(w["L3_attn_Wo"].T), "a3_bo": twice(w["L3_attn_bo"][:, None]),
        "a3_heads": np.eye(2 * HEADS3).reshape(2, HEADS3, 2, HEADS3).transpose(0, 1, 3, 2)
        .reshape(2 * HEADS3, 2 * HEADS3).repeat(D // HEADS3, axis=0),
        "f3_rw": diagonal(w["L3_ffn_router_w"].T, cols=64),
        "f3_rb": spread(w["L3_ffn_router_b"]), "f3_rank": spread(np.arange(E3, 0, -1)),
        "f3_w1": twice(w["L3_ffn_W1"].transpose(1, 0, 2).reshape(D, -1)),
        "f3_b1": w["L3_ffn_b1"].reshape(4, P).T,
        "f3_shut": twice(-BIG * (1 - np.kron(np.eye(E3), np.ones((1, F3))))),
        "f3_w2": w["L3_ffn_W2"].reshape(4, P, D).transpose(1, 0, 2).reshape(P, -1),
        "f3_b2": diagonal(w["L3_ffn_b2"]),
    }
    w2 = np.zeros((3, P, P), np.float32)
    for e in range(E2):
        half = slice(64 * (e % 2), 64 * (e % 2) + 64)
        w2[e // 2, half, half] = w["L2_ffn_expert_w2"][e]
    parts["f2_w2"] = w2.transpose(1, 0, 2)
    parts["f2_w3"] = w["L2_ffn_expert_w3"].reshape(3, P, D).transpose(1, 0, 2)
    maps = {(0, 0): 0, (1, 0): 1, (0, 1): 2, (1, 1): 3, (3, 2): 4, (2, 3): 5, (3, 3): 6}
    embed = np.zeros((4, 4, 8, 8, D), np.float32)
    for (rt, ct), m in maps.items():
        for cj in range(8):
            embed[rt, ct, cj, cj] = w["L0_tok_W"][m]
    emb = w["L0_txt_emb"]
    near = np.clip(np.arange(VOCAB)[:, None] + np.arange(TAPS) - TAPS // 2, 0, VOCAB - 1)
    return {
        "images": w["x"], "tokens": np.ascontiguousarray(w["x_txt"].T),
        "neighbours": emb[near].reshape(VOCAB, TAPS * D), "embed": embed.reshape(P, -1),
        "pack_a": pack(PACK_A, parts), "pack_b": pack(PACK_B, parts), "pack_c": pack(PACK_C, parts),
        "routes": w["L1_ffn_route_id"].reshape(1, -1),
    }


def kernel(**inputs):
    import concourse.bacc as bacc
    from concourse.bass_utils import run_bass_kernel_spmd as run

    nc = bacc.Bacc("TRN2", target_bir_lowering=False, num_devices=1)
    operands = pack_operands(**inputs)
    names = ("images", "tokens", "neighbours", "embed", "pack_a", "pack_b", "pack_c", "routes")
    arrays = {n: np.ascontiguousarray(operands[n]) for n in names}
    args = [nc.dram_tensor(n, a.shape, mybir.dt.from_np(a.dtype), kind="ExternalInput").ap()
            for n, a in arrays.items()]
    out = nc.dram_tensor("out", (BATCH, T, D), F32, kind="ExternalOutput").ap()
    build(nc, *args, out)
    return run(nc, [arrays], core_ids=[0]).results[0]["out"]
```
